# Optimizing a Trainium2 kernel written in Bass

```python
import numpy as np
import jax
import jax.numpy as jnp

def _softmax(x, axis=-1):
    return jax.nn.softmax(x, axis=axis)

def _gelu(x):
    return jax.nn.gelu(x, approximate=True)

def _silu(x):
    return jax.nn.silu(x)

def _sigmoid(x):
    return jax.nn.sigmoid(x)

def _layernorm(x, axis=-1, eps=1e-05):
    m = jnp.mean(x, axis=axis, keepdims=True)
    v = jnp.var(x, axis=axis, keepdims=True)
    return (x - m) / jnp.sqrt(v + eps)

def _scatter_add(tgt, idx, src, axis=0):
    return tgt.at[idx].add(src)

def _segment_sum(src, seg, n):
    return jax.ops.segment_sum(src, seg, n)
kernel_name = 'mk_gnn_ffn_d1_gnn_r8_f909ad'

def setup_inputs(seed: int=0):
    np.random.seed(seed)
    _w = jnp.asarray

    def _rec_inputs():
        import jax
        import jax.numpy as jnp
        _gk = jax.random.key(seed)
        x = -0.0003713 + 1 * jax.random.normal(jax.random.fold_in(_gk, 1), (6250, 256), jnp.float32)
        src = jax.random.randint(jax.random.fold_in(_gk, 2), (100000,), 0, 6250, jnp.int32)
        dst = jnp.minimum((6250 * jax.random.uniform(jax.random.fold_in(_gk, 3), (100000,)) ** 2.0).astype(jnp.int32), 49999)
        _o = jnp.argsort(dst, stable=True)
        src = src[_o]
        dst = dst[_o]
        return (x, src, dst)
    x, src, dst = _rec_inputs()

    def _L0_gnn_setup():
        import jax, jax.numpy as jnp
        import numpy as np
        N = 6250
        E = 100000
        D = 256
        H = 8
        HD = D // H
        F = 4 * D
        SCALE = D ** (-0.5)
        EPS = 1e-05

        def _layer_norm(x, g, b):
            m = jnp.mean(x, axis=-1, keepdims=True)
            v = jnp.mean((x - m) ** 2, axis=-1, keepdims=True)
            return (x - m) * jax.lax.rsqrt(v + EPS) * g + b

        def _self_attention(x, edge_indices, w_qkv, b_qkv):
            qkv = (x @ w_qkv + b_qkv).reshape(N, H, 3 * HD)
            q, k, v = (qkv[..., :HD], qkv[..., HD:2 * HD], qkv[..., 2 * HD:])
            rows, cols = (edge_indices[0], edge_indices[1])
            alpha = jnp.einsum('ehd,ehd->eh', q[rows], k[cols]) * SCALE
            m = jax.ops.segment_max(alpha, rows, num_segments=N)
            ea = jnp.exp(alpha - m[rows])
            denom = jax.ops.segment_sum(ea, rows, num_segments=N)
            w = ea / denom[rows]
            out = jax.ops.segment_sum(w[:, :, None] * v[cols], rows, num_segments=N)
            return out.reshape(N, D)
        key = jax.random.key(seed)
        ks = jax.random.split(key, 10)
        x = jax.random.normal(ks[0], (N, D), dtype=jnp.float32)
        edge_indices = jax.random.randint(ks[1], (2, E), 0, N, dtype=jnp.int32)
        s = 0.02
        return {'x': x, 'edge_indices': edge_indices, 'w_qkv': jax.random.normal(ks[2], (D, 3 * D), dtype=jnp.float32) * s, 'b_qkv': jnp.zeros((3 * D,), dtype=jnp.float32), 'ln1_g': jnp.ones((D,), dtype=jnp.float32), 'ln1_b': jnp.zeros((D,), dtype=jnp.float32), 'ln2_g': jnp.ones((D,), dtype=jnp.float32), 'ln2_b': jnp.zeros((D,), dtype=jnp.float32), 'w1': jax.random.normal(ks[3], (D, F), dtype=jnp.float32) * s, 'b1': jnp.zeros((F,), dtype=jnp.float32), 'w2': jax.random.normal(ks[4], (F, D), dtype=jnp.float32) * s, 'b2': jnp.zeros((D,), dtype=jnp.float32)}
    _L0_gnn_all = _L0_gnn_setup()
    _L0_gnn_in = {k: v for k, v in _L0_gnn_all.items() if k in ('w_qkv', 'b_qkv', 'ln1_g', 'ln1_b', 'ln2_g', 'ln2_b', 'w1', 'b1', 'w2', 'b2')}
    del _L0_gnn_all

    def _L0_ffn_setup():
        import jax, jax.numpy as jnp
        import numpy as np
        B, T, D, H, E = (16, 512, 256, 512, 8)
        key = jax.random.key(seed)
        ks = jax.random.split(key, 5)
        x = jax.random.normal(ks[0], (B, T, D), dtype=jnp.float32)
        gate_w = jax.random.normal(ks[1], (D, E), dtype=jnp.float32) * 0.02
        gate_b = jnp.zeros((E,), dtype=jnp.float32)
        W1 = jax.random.normal(ks[2], (E, D, H), dtype=jnp.float32) * 0.02
        b1 = jnp.zeros((E, H), dtype=jnp.float32)
        W2 = jax.random.normal(ks[3], (E, H, D), dtype=jnp.float32) * 0.02
        b2 = jnp.zeros((E, D), dtype=jnp.float32)
        return {'x': x, 'gate_w': gate_w, 'gate_b': gate_b, 'W1': W1, 'b1': b1, 'W2': W2, 'b2': b2}
    _L0_ffn_all = _L0_ffn_setup()
    _L0_ffn_in = {k: v for k, v in _L0_ffn_all.items() if k in ('gate_w', 'gate_b', 'W1', 'b1', 'W2', 'b2')}
    del _L0_ffn_all
    return {'x': x, 'src': src, 'dst': dst, 'L0_gnn_w_qkv': _L0_gnn_in['w_qkv'], 'L0_gnn_b_qkv': _L0_gnn_in['b_qkv'], 'L0_gnn_ln1_g': _L0_gnn_in['ln1_g'], 'L0_gnn_ln1_b': _L0_gnn_in['ln1_b'], 'L0_gnn_ln2_g': _L0_gnn_in['ln2_g'], 'L0_gnn_ln2_b': _L0_gnn_in['ln2_b'], 'L0_gnn_w1': _L0_gnn_in['w1'], 'L0_gnn_b1': _L0_gnn_in['b1'], 'L0_gnn_w2': _L0_gnn_in['w2'], 'L0_gnn_b2': _L0_gnn_in['b2'], 'L0_ffn_gate_w': _L0_ffn_in['gate_w'], 'L0_ffn_gate_b': _L0_ffn_in['gate_b'], 'L0_ffn_W1': _L0_ffn_in['W1'], 'L0_ffn_b1': _L0_ffn_in['b1'], 'L0_ffn_W2': _L0_ffn_in['W2'], 'L0_ffn_b2': _L0_ffn_in['b2']}

def reference(x, src, dst, L0_gnn_w_qkv, L0_gnn_b_qkv, L0_gnn_ln1_g, L0_gnn_ln1_b, L0_gnn_ln2_g, L0_gnn_ln2_b, L0_gnn_w1, L0_gnn_b1, L0_gnn_w2, L0_gnn_b2, L0_ffn_gate_w, L0_ffn_gate_b, L0_ffn_W1, L0_ffn_b1, L0_ffn_W2, L0_ffn_b2):
    import jax
    import jax.numpy as jnp

    def _L0_gnn_ref(x, edge_indices, w_qkv, b_qkv, ln1_g, ln1_b, ln2_g, ln2_b, w1, b1, w2, b2):
        import jax, jax.numpy as jnp
        import numpy as np
        N = 6250
        E = 100000
        D = 256
        H = 8
        HD = D // H
        F = 4 * D
        SCALE = D ** (-0.5)
        EPS = 1e-05

        def _layer_norm(x, g, b):
            m = jnp.mean(x, axis=-1, keepdims=True)
            v = jnp.mean((x - m) ** 2, axis=-1, keepdims=True)
            return (x - m) * jax.lax.rsqrt(v + EPS) * g + b

        def _self_attention(x, edge_indices, w_qkv, b_qkv):
            qkv = (x @ w_qkv + b_qkv).reshape(N, H, 3 * HD)
            q, k, v = (qkv[..., :HD], qkv[..., HD:2 * HD], qkv[..., 2 * HD:])
            rows, cols = (edge_indices[0], edge_indices[1])
            alpha = jnp.einsum('ehd,ehd->eh', q[rows], k[cols]) * SCALE
            m = jax.ops.segment_max(alpha, rows, num_segments=N)
            ea = jnp.exp(alpha - m[rows])
            denom = jax.ops.segment_sum(ea, rows, num_segments=N)
            w = ea / denom[rows]
            out = jax.ops.segment_sum(w[:, :, None] * v[cols], rows, num_segments=N)
            return out.reshape(N, D)
        x = _layer_norm(x + _self_attention(x, edge_indices, w_qkv, b_qkv), ln1_g, ln1_b)
        ffn = jax.nn.relu(x @ w1 + b1) @ w2 + b2
        x = _layer_norm(x + ffn, ln2_g, ln2_b)
        return x

    def _L0_ffn_ref(x, gate_w, gate_b, W1, b1, W2, b2):
        import jax, jax.numpy as jnp
        import numpy as np
        B, T, D, H, E = (16, 512, 256, 512, 8)
        Bb, Tt, Dd = x.shape
        Ee = gate_w.shape[1]
        xf = x.reshape(-1, Dd)
        N = xf.shape[0]
        logits = xf @ gate_w + gate_b
        probs = jax.nn.softmax(logits, axis=-1)
        top2_vals, top2_idx = jax.lax.top_k(probs, 2)
        cw = jnp.zeros((N, Ee), dtype=xf.dtype).at[jnp.arange(N)[:, None], top2_idx].add(top2_vals)

        def step(acc, params):
            w1, bb1, w2, bb2, we = params
            h = jax.nn.gelu(xf @ w1 + bb1, approximate=False)
            y = h @ w2 + bb2
            return (acc + we[:, None] * y, None)
        out, _ = jax.lax.scan(step, jnp.zeros_like(xf), (W1, b1, W2, b2, cw.T))
        return out.reshape(Bb, Tt, Dd)
    edge_index = jnp.stack([src, dst])
    x = x + _L0_gnn_ref(_layernorm(x, axis=-1), edge_index, L0_gnn_w_qkv, L0_gnn_b_qkv, L0_gnn_ln1_g, L0_gnn_ln1_b, L0_gnn_ln2_g, L0_gnn_ln2_b, L0_gnn_w1, L0_gnn_b1, L0_gnn_w2, L0_gnn_b2)
    x = x + _L0_ffn_ref(_layernorm(x, axis=-1)[None], L0_ffn_gate_w, L0_ffn_gate_b, L0_ffn_W1, L0_ffn_b1, L0_ffn_W2, L0_ffn_b2)[0]
    return x

_drawn_inputs = setup_inputs


def setup_inputs(seed=0):
    import zlib

    import numpy as np

    out = dict(_drawn_inputs(seed))
    spreads = {'L0_gnn_b_qkv': (0.0, 0.1),
     'L0_gnn_ln1_g': (1.0, 0.2),
     'L0_gnn_ln1_b': (0.0, 0.1),
     'L0_gnn_ln2_g': (1.0, 0.2),
     'L0_gnn_ln2_b': (0.0, 0.1),
     'L0_gnn_b1': (0.0, 0.378),
     'L0_gnn_b2': (0.0, 0.1),
     'L0_ffn_gate_b': (0.0, 0.8),
     'L0_ffn_b1': (0.0, 0.8),
     'L0_ffn_b2': (0.0, 0.617)}
    factors = {'L0_ffn_gate_w': 3.968, 'L0_ffn_W1': 5.638, 'L0_ffn_W2': 5.303}
    for name, (base, spread) in spreads.items():
        noise = np.random.default_rng([zlib.crc32(name.encode()), seed]).standard_normal(out[name].shape)
        drawn = base * np.exp(spread * noise) if base else spread * noise
        out[name] = jnp.asarray(drawn.astype(out[name].dtype))
    for name, factor in factors.items():
        out[name] = (out[name] * factor).astype(out[name].dtype)
    return out
```

```python
import concourse.bass as bass
from concourse import mybir
from contextlib import ExitStack

F32, I32, BF16 = mybir.dt.float32, mybir.dt.int32, mybir.dt.bfloat16
ALU, ACT, AX = mybir.AluOpType, mybir.ActivationFunctionType, mybir.AxisListType

P = 128
N, E, D, H = 6250, 100000, 256, 8
HD = D // H
DC = D // P
F = 4 * D
NX, FX = 8, 512
EPS = 1e-5
SCALE = D ** -0.5

NT = -(-N // P)
GT = 4
NG = N // (GT * P)
REST = N - NG * GT * P
EP = 125
ET = E // EP
EB = 8
CH = 16
ST = -(-(-(-E // P) + NT) // CH) * CH
SC = ST // CH
CL = SC * P
PAD_KEY = -1
NO_LO = 256.0
LOW = -1e30


class Tally:

    def __init__(self, sem):
        self.sem, self.n, self.k, self.per = sem, 0, None, 0

    def value(self, back=0):
        v = self.n - back
        return v if self.k is None else self.k * self.per + v

    def enter(self, k, per):
        self.k, self.per, self.base = k, per, self.n

    def leave(self, turns):
        assert self.n - self.base == self.per, (self.n - self.base, self.per)
        self.n = self.base + self.per * turns
        self.k = None


def linker(eng, tally):

    def link(ins):
        ins.then_inc(tally.sem, 1)
        tally.n += 1
        eng.wait_ge(tally.sem, tally.value())

    return link


def make_tools(nc):
    ctx = ExitStack()

    def sb(name, shape, dt=F32):
        return ctx.enter_context(nc.sbuf_tensor(name, shape, dt))

    def pb(name, shape=(P, 512), dt=F32):
        return ctx.enter_context(nc.psum_tensor(name, list(shape), dt))

    def sem(name):
        return ctx.enter_context(nc.semaphore(name))

    return ctx, sb, pb, sem


def stage_constants(nc, K):
    ctx, sb, pb, sem = make_tools(nc)
    with ctx:
        made, ints, cast = sem("made"), sem("ints"), sem("cast")
        with nc.Block() as block:

            @block.gpsimd
            def _(pool):
                pool.memset(K["ident"][:], 0.0).then_inc(made, 1)
                pool.memset(K["lower"][:], 1.0).then_inc(made, 1)
                pool.memset(K["ones"][:], 1.0).then_inc(made, 1)
                pool.iota(K["col_i"][:], [[1, P]], base=0, channel_multiplier=0).then_inc(ints, 1)
                pool.iota(K["part_i"][:], [[0, 1]], base=0, channel_multiplier=1).then_inc(ints, 1)
                pool.wait_ge(made, 3)
                pool.affine_select(out=K["ident"][:], in_=K["ident"][:], compare_op=ALU.not_equal, fill=1.0,
                                   base=0, pattern=[[-1, P]], channel_multiplier=1).then_inc(made, 1)
                pool.affine_select(out=K["upper"][:], in_=K["ones"][:], compare_op=ALU.is_gt, fill=0.0,
                                   base=0, pattern=[[-1, P]], channel_multiplier=1).then_inc(made, 1)
                pool.affine_select(out=K["lower"][:], in_=K["ones"][:], compare_op=ALU.is_gt, fill=0.0,
                                   base=0, pattern=[[1, P]], channel_multiplier=-1).then_inc(made, 1)

            @block.vector
            def _(dve):
                dve.wait_ge(ints, 2)
                dve.tensor_copy(K["col"][:], K["col_i"][:])
                dve.tensor_copy(K["part"][:], K["part_i"][:])
                dve.wait_ge(made, 6)
                dve.tensor_copy(K["ident_b"][:], K["ident"][:])
                dve.tensor_copy(K["ones_b"][:], K["ones"][:]).then_inc(cast, 1)
                dve.wait_ge(cast, 1)


def stage_qkv(nc, K, x, w_qkv, b_qkv, h0_d, k_d, v_d, q_sb):
    ctx, sb, pb, sem = make_tools(nc)
    with ctx:
        w_raw, w = sb("w_raw", [P, DC, 3 * D]), sb("w", [P, DC, 3 * D])
        b_raw, b = sb("b_raw", [P, 3 * D]), sb("b", [P, 3 * D])
        xb, h = sb("xb", [P, 2, GT, D]), sb("h", [P, 2, GT, D])
        hT = sb("hT", [P, 2, DC, GT * P])
        kv = sb("kv", [P, 2, GT, 2 * D])
        stats, mv = sb("stats", [P, 2, GT, 6]), sb("mv", [P, 2, GT, 2])
        std, rstd = sb("std", [P, 2, GT]), sb("rstd", [P, 2, GT])
        eps = sb("eps", [P, 1])
        pT = [[pb(f"pT{a}{c}") for c in range(DC)] for a in range(2)]
        pQK = [pb(f"pQK{a}") for a in range(2)]
        pV = [pb(f"pV{a}") for a in range(2)]
        w_in, w_ready, x_in = sem("w_in"), sem("w_ready"), [sem(f"x_in{a}") for a in range(2)]
        stored = [sem(f"stored{a}") for a in range(2)]
        var_ready, std_ready, h_ready = sem("var_ready"), sem("std_ready"), sem("h_ready")
        hT_psum, hT_ready = sem("hT_psum"), sem("hT_ready")
        qkv_psum, qkv_out, dve_link = sem("qkv_psum"), sem("qkv_out"), sem("dve_link")
        turns = sem("turns")

        def groups(eng, tallies, body):
            for a in range(2):
                body(0, a, GT, True)
            with eng.Fori(1, NG // 2) as k:
                for t, per in tallies:
                    t.enter(k - 1, per)
                for a in range(2):
                    body(k, a, GT, False)
            for t, per in tallies:
                t.leave(NG // 2 - 1)
            body(NG // 2, 0, 1, False)

        def rows(dram, k, a, nt):
            if nt == 1:
                return dram[NG * GT * P:NG * GT * P + REST, :]
            v = dram[0:NG * GT * P, :].rearrange("(g t p) d -> g p t d", t=GT, p=P)
            return v[k * 2 + a]

        with nc.Block() as block:

            @block.sync
            def _(sp):
                sp.dma_start(w_raw[:], w_qkv.rearrange("(c p) n -> p c n", p=P)).then_inc(w_in, 16)
                sp.dma_start(b_raw[:], b_qkv.unsqueeze(0).to_broadcast([P, 3 * D])).then_inc(w_in, 16)

                def body(k, a, nt, first):
                    if not first:
                        sp.wait_ge(h_ready, k * 2 + a - 1)
                    if nt == 1:
                        sp.dma_start(xb[0:REST, a, 0, :], rows(x, k, a, 1)).then_inc(x_in[a], 16)
                    else:
                        sp.dma_start(xb[:, a], rows(x, k, a, nt)).then_inc(x_in[a], 16)

                groups(sp, [], body)

            @block.gpsimd
            def _(pool):
                def body(k, a, nt, first):
                    pool.wait_ge(h_ready, k * 2 + a + 1)
                    pool.wait_ge(qkv_out, k * 2 * GT + a * GT + nt)
                    pool.sem_inc(turns)
                    if nt == 1:
                        pool.dma_start(rows(h0_d, k, a, 1), h[0:REST, a, 0, :]).then_inc(stored[a], 16)
                        pool.dma_start(rows(k_d, k, a, 1), kv[0:REST, a, 0, 0:D]).then_inc(stored[a], 16)
                        pool.dma_start(rows(v_d, k, a, 1), kv[0:REST, a, 0, D:2 * D]).then_inc(stored[a], 16)
                    else:
                        pool.dma_start(rows(h0_d, k, a, nt), h[:, a]).then_inc(stored[a], 16)
                        pool.dma_start(rows(k_d, k, a, nt), kv[:, a, :, 0:D]).then_inc(stored[a], 16)
                        pool.dma_start(rows(v_d, k, a, nt), kv[:, a, :, D:2 * D]).then_inc(stored[a], 16)

                groups(pool, [], body)
                pool.wait_ge(stored[0], 48 * (NG // 2 + 1))
                pool.wait_ge(stored[1], 48 * (NG // 2))

            @block.vector
            def _(dve):
                link = linker(dve, t := Tally(dve_link))
                dve.memset(eps[:], EPS).then_inc(w_ready, 1)
                dve.wait_ge(w_in, 32)
                for c in range(DC):
                    dve.tensor_copy(w[:, c].rearrange("p (s h e) -> p s h e", s=3, h=H),
                                    w_raw[:, c].rearrange("p (h s e) -> p s h e", s=3, h=H)).then_inc(w_ready, 1)
                link(dve.tensor_copy(b[:].rearrange("p (s h e) -> p s h e", s=3, h=H),
                                     b_raw[:].rearrange("p (h s e) -> p s h e", s=3, h=H)))

                def body(k, a, nt, first):
                    dve.wait_ge(x_in[a], k * 16 + 16)
                    for i in range(nt):
                        ins = dve.bn_stats(stats[:, a, i], xb[:, a, i])
                    link(ins)
                    dve.sem_inc(turns)
                    for i in range(nt):
                        ins = dve.bn_aggr(mv[:, a, i], stats[:, a, i])
                    ins.then_inc(var_ready, 1)
                    dve.wait_ge(std_ready, k * 2 + a + 1)
                    link(dve.reciprocal(rstd[:, a, 0:nt], std[:, a, 0:nt]))
                    if not first:
                        dve.wait_ge(hT_psum, k * 2 + a - 1)
                        dve.wait_ge(stored[a], k * 48)
                    for i in range(nt):
                        ins = dve.tensor_scalar(h[:, a, i], xb[:, a, i], mv[:, a, i, 0:1], rstd[:, a, i:i + 1],
                                                ALU.subtract, ALU.mult)
                    ins.then_inc(h_ready, 1)
                    for i in range(nt):
                        tile = (k * 2 + a) * GT + i
                        dve.wait_ge(qkv_psum, tile + 1)
                        dve.tensor_tensor(q_sb[:, tile], pQK[i % 2][:, 0:D], b[:, 0:D], ALU.add)
                        dve.tensor_tensor(kv[:, a, i, 0:D], pQK[i % 2][:, D:2 * D], b[:, D:2 * D], ALU.add)
                        dve.tensor_tensor(kv[:, a, i, D:2 * D], pV[i % 2][:, 0:D], b[:, 2 * D:3 * D],
                                          ALU.add).then_inc(qkv_out, 1)

                groups(dve, [(t, 4)], body)

            @block.scalar
            def _(act):
                act.wait_ge(w_ready, 1)

                def body(k, a, nt, first):
                    act.wait_ge(var_ready, k * 2 + a + 1)
                    act.activation(std[:, a, 0:nt], mv[:, a, 0:nt, 1], ACT.Sqrt, bias=eps[:]).then_inc(std_ready, 1)
                    act.wait_ge(hT_psum, k * 2 + a + 1)
                    if not first:
                        act.wait_ge(qkv_psum, ((k - 1) * 2 + a + 1) * GT)
                    for c in range(DC):
                        ins = act.copy(hT[:, a, c, 0:nt * P], pT[a][c][:, 0:nt * P])
                    ins.then_inc(hT_ready, 1)

                groups(act, [], body)

            @block.tensor
            def _(pe):
                pe.wait_ge(w_ready, 1 + DC)

                def body(k, a, nt, first):
                    pe.wait_ge(h_ready, k * 2 + a + 1)
                    if not first:
                        pe.wait_ge(hT_ready, k * 2 + a - 1)
                    for c in range(DC):
                        for i in range(nt):
                            ins = pe.transpose(pT[a][c][:, i * P:(i + 1) * P], h[:, a, i, c * P:(c + 1) * P],
                                               K["ident"][:])
                    ins.then_inc(hT_psum, 1)
                    pe.wait_ge(hT_ready, k * 2 + a + 1)
                    for i in range(nt):
                        tile = (k * 2 + a) * GT + i
                        if not (first and a == 0 and i < 2):
                            pe.wait_ge(qkv_out, tile - 1)
                        for c in range(DC):
                            pe.matmul(pQK[i % 2][:], hT[:, a, c, i * P:(i + 1) * P], w[:, c, 0:2 * D],
                                      start=c == 0, stop=c == DC - 1)
                        for c in range(DC):
                            ins = pe.matmul(pV[i % 2][:, 0:D], hT[:, a, c, i * P:(i + 1) * P], w[:, c, 2 * D:3 * D],
                                            start=c == 0, stop=c == DC - 1)
                        ins.then_inc(qkv_psum, 1)

                groups(pe, [], body)


def constants(nc, sb):
    K = {n: sb(f"k_{n}", [P, P]) for n in ("ident", "lower", "upper", "ones", "col")}
    K["part"] = sb("k_part", [P, 1])
    K["col_i"], K["part_i"] = sb("k_col_i", [P, P], I32), sb("k_part_i", [P, 1], I32)
    K["ident_b"], K["ones_b"] = sb("k_ident_b", [P, P], BF16), sb("k_ones_b", [P, P], BF16)
    return K


RING = 4
NB = ET // EB


def sort_steps(eng, tallies, step):
    turns = NB // RING
    for r in range(RING):
        step(0, r, "first")
    with eng.Fori(1, turns - 1) as k:
        for t, per in tallies:
            t.enter(k - 1, per)
        for r in range(RING):
            step(k, r, "middle")
    for t, per in tallies:
        t.leave(turns - 2)
    for r in range(RING):
        step(turns - 1, r, "last")


def stage_sort(nc, K, src, dst, sorted_d, win_d):
    ctx, sb, pb, sem = make_tools(nc)
    with ctx:
        src_i, dst_i = sb("src_i", [EP, ET], I32), sb("dst_i", [EP, ET], I32)
        rec = sb("rec", [EP, ET, 2], I32)
        part_i = sb("part_of_key_i", [EP, 2, ET], I32)
        key_f, lo_f, hi_f = sb("key_f", [EP, ET]), sb("lo_f", [EP, ET]), sb("hi_f", [EP, ET])
        hl_b = sb("hl_b", [EP, ET, 2], BF16)
        ohlo = sb("ohlo", [EP, 2, EB, P], BF16)
        ohhi = sb("ohhi", [EP, RING, EB, NT], BF16)
        Hr = sb("Hr", [P, 2, EB + 1, NT])
        ohtS = sb("ohtS", [P, 2, EB, EP])
        hl_st, rec_st = sb("hl_st", [EP, RING, EB, 2], BF16), sb("rec_st", [EP, RING, EB, 2], I32)
        idx_st = sb("idx_st", [EP, RING, EB], I32)
        rk = sb("rk", [EP, 2, EB])
        same, found = sb("same", [EP, EB, EP], BF16), sb("found", [EP, EB * NT])
        looked, pos = sb("looked", [EP, EB]), sb("pos", [EP, EB])
        pos_i, hi_pos, lo_pos = sb("pos_i", [EP, EB], I32), sb("hi_pos", [EP, EB], I32), sb("lo_pos", [EP, EB], I32)
        cnt, zero_row = sb("cnt", [P, NT]), sb("zero_row", [P, NT])
        tot, nt_i, nt_f = sb("tot", [P, NT], I32), sb("nt_i", [P, NT], I32), sb("nt_f", [P, NT])
        t_end, t_start, excl = sb("t_end", [P, NT]), sb("t_start", [P, NT]), sb("excl", [P, NT])
        WP = 64
        WJ = ST // WP
        tv_i, tv_f = sb("tv_i", [WP, WJ], I32), sb("tv_f", [WP, WJ])
        past, win_f, win_i = sb("past", [WP, WJ, NT]), sb("win_f", [WP, WJ]), sb("win_i", [WP, WJ], I32)
        pads = sb("pads", [P, ST, 2], I32)
        cntp = [pb(f"cntp{a}") for a in range(2)]
        oht = [pb(f"oht{a}") for a in range(2)]
        krow = [pb(f"krow{a}") for a in range(2)]
        lk = [pb(f"lk{a}") for a in range(2)]
        HB = EB // 2

        e_in, rec_made, split = sem("e_in"), sem("rec_made"), sem("split")
        filled, pads_made = sem("filled"), sem("pads_made")
        oh_ready, counted, prefix, tv_made = sem("oh_ready"), sem("counted"), sem("prefix"), sem("tv_made")
        win_ready, win_out, dve_link, oh_used = sem("win_ready"), sem("win_out"), sem("dve_link"), sem("oh_used")
        cnt_ready = sem("cnt_ready")

        def one_hots(dve, t0, a, r):
            dve.tensor_tensor(ohlo[:, a], K["col"][0:EP, :].unsqueeze(1).to_broadcast([EP, EB, P]),
                              lo_f[:, bass.ds(t0, EB)].unsqueeze(2).to_broadcast([EP, EB, P]), ALU.is_equal)
            return dve.tensor_tensor(ohhi[:, r], K["col"][0:EP, 0:NT].unsqueeze(1).to_broadcast([EP, EB, NT]),
                                     hi_f[:, bass.ds(t0, EB)].unsqueeze(2).to_broadcast([EP, EB, NT]),
                                     ALU.is_equal)

        with nc.Block() as block:

            @block.sync
            def _(sp):
                sp.dma_start(src_i[:], src.rearrange("(p t) -> p t", p=EP)).then_inc(e_in, 16)
                sp.dma_start(dst_i[:], dst.rearrange("(p t) -> p t", p=EP)).then_inc(e_in, 16)
                sp.wait_ge(pads_made, 2)
                sp.dma_start(sorted_d.rearrange("(p t) c -> p t c", p=P), pads[:]).then_inc(filled, 16)
                sp.wait_ge(win_ready, 1)
                sp.dma_start(win_d.rearrange("(p j) -> p j", p=WP), win_i[:]).then_inc(win_out, 16)
                sp.wait_ge(filled, 16)
                sp.wait_ge(win_out, 16)

            @block.gpsimd
            def _(pool):
                pool.memset(pads[:, :, 0], PAD_KEY).then_inc(pads_made, 1)
                pool.memset(pads[:, :, 1], 0).then_inc(pads_made, 1)
                pool.iota(tv_i[:], [[1, WJ]], base=0, channel_multiplier=WJ).then_inc(tv_made, 1)
                pool.wait_ge(e_in, 32)
                pool.tensor_copy(rec[:, :, 0], src_i[:]).then_inc(rec_made, 1)
                pool.tensor_copy(rec[:, :, 1], dst_i[:]).then_inc(rec_made, 1)

            @block.vector
            def _(dve):
                link = linker(dve, Tally(dve_link))
                dve.wait_ge(e_in, 32)
                dve.tensor_scalar(part_i[:, 0], src_i[:], P - 1, None, ALU.bitwise_and)
                link(dve.tensor_scalar(part_i[:, 1], src_i[:], 7, None, ALU.logical_shift_right))
                dve.tensor_copy(key_f[:], src_i[:])
                dve.tensor_copy(lo_f[:], part_i[:, 0])
                link(dve.tensor_copy(hi_f[:], part_i[:, 1]))
                dve.tensor_scalar(hl_b[:, :, 0], hi_f[:], float(P), None, ALU.mult)
                link(dve.tensor_copy(hl_b[:, :, 1], lo_f[:]))
                for r in range(2):
                    one_hots(dve, r * EB, r, r).then_inc(oh_ready, 1)
                with dve.Fori(1, NB // 2) as k:
                    for a in range(2):
                        dve.wait_ge(oh_used, k * 2 + a - 1)
                        one_hots(dve, (k * 2 + a) * EB, a, a).then_inc(oh_ready, 1)
                dve.wait_ge(oh_used, NB)
                dve.tensor_copy(cnt[:], cntp[0][:, 0:NT]).then_inc(cnt_ready, 1)
                link(dve.memset(zero_row[:], 0.0))
                dve.wait_ge(prefix, 1)
                dve.tensor_copy(excl[:], lk[0][:, 0:NT])
                link(dve.tensor_scalar(tot[:], lk[1][:, 0:NT], float(P - 1), None, ALU.add))
                link(dve.tensor_scalar(nt_i[:], tot[:], 7, None, ALU.logical_shift_right))
                link(dve.tensor_copy(nt_f[:], nt_i[:]))
                link(dve.tensor_tensor_scan(t_end[:], zero_row[:], nt_f[:], 0.0, ALU.add, ALU.add))
                link(dve.tensor_tensor(t_start[:], t_end[:], nt_f[:], ALU.subtract))
                dve.scalar_tensor_tensor(Hr[:, 0, 0], t_start[:], float(P), excl[:], ALU.mult, ALU.add)
                dve.wait_ge(tv_made, 1)
                link(dve.tensor_copy(tv_f[:], tv_i[:]))
                link(dve.tensor_tensor(past[:], t_end[0:WP].unsqueeze(1).to_broadcast([WP, WJ, NT]),
                                       tv_f[:].unsqueeze(2).to_broadcast([WP, WJ, NT]), ALU.is_le))
                link(dve.tensor_reduce(win_f[:], past[:], AX.X, ALU.add))
                dve.tensor_scalar(win_i[:], win_f[:], float(NT - 1), None, ALU.min).then_inc(win_ready, 1)

            @block.tensor
            def _(pe):
                def batch(k, a, first, last):
                    pe.wait_ge(oh_ready, k * 2 + a + 1)
                    for j in range(EB):
                        ins = pe.matmul(cntp[0][:, 0:NT], ohlo[:, a, j], ohhi[:, a, j],
                                        start=first and a == 0 and j == 0, stop=last and a == 1 and j == EB - 1)
                    ins.then_inc(oh_used, 1)

                for a in range(2):
                    batch(0, a, True, False)
                with pe.Fori(1, NB // 2 - 1) as k:
                    for a in range(2):
                        batch(k, a, False, False)
                for a in range(2):
                    batch(NB // 2 - 1, a, False, True)
                pe.wait_ge(cnt_ready, 1)
                pe.matmul(lk[0][:, 0:NT], K["lower"][:], cnt[:], start=True, stop=True)
                pe.matmul(lk[1][:, 0:NT], K["ones"][:], cnt[:], start=True, stop=True).then_inc(prefix, 1)

        oh_r, hist, krow_ps, krow_used = sem("oh_r"), sem("hist"), sem("krow_ps"), sem("krow_used")
        H_ready, oht_ready, lk_ps, lk_used = sem("H_ready"), sem("oht_ready"), sem("lk_ps"), sem("lk_used")
        hl_ready, rec_ready, idx_ready = sem("hl_ready"), sem("rec_ready"), sem("idx_ready")
        scattered = [sem(f"scattered{r}") for r in range(RING)]
        link2, turns = sem("link2"), sem("sort_turns")
        with nc.Block() as block:

            @block.vector
            def _(dve):
                tally = Tally(link2)
                link = linker(dve, tally)

                def ranks(k, r, kind):
                    a, s = r % 2, k * RING + r
                    dve.wait_ge(krow_ps, s + 1)
                    for j in range(EB):
                        ins = dve.scalar_tensor_tensor(
                            same[:, j], krow[j // HB][0:EP, (j % HB) * EP:(j % HB + 1) * EP],
                            key_f[:, bass.ds(s * EB + j, 1)], K["upper"][0:EP, 0:EP], ALU.is_equal, ALU.mult,
                            accum_out=rk[:, a, j:j + 1])
                    ins.then_inc(krow_used, 1)
                    dve.wait_ge(hist, s + 1)
                    if kind != "first" or r >= 1:
                        dve.wait_ge(lk_ps, s)
                    for j in range(EB):
                        to = Hr[:, a, j + 1] if j < EB - 1 else Hr[:, 1 - a, 0]
                        ins = dve.tensor_tensor(to, Hr[:, a, j], cntp[a][:, j * NT:(j + 1) * NT], ALU.add)
                        if j < EB - 1:
                            link(ins)
                    ins.then_inc(H_ready, 1)
                    dve.wait_ge(H_ready, s + 1)

                def places(k, r, kind):
                    a, s = r % 2, k * RING + r
                    dve.wait_ge(lk_ps, s + 1)
                    link(dve.tensor_tensor(found[:], lk[a][0:EP, 0:EB * NT],
                                           ohhi[:, r].rearrange("p j n -> p (j n)"), ALU.mult))
                    link(dve.tensor_reduce(looked[:], found[:].rearrange("p (j n) -> p j n", j=EB), AX.X, ALU.add))
                    link(dve.tensor_tensor(pos_i[:], looked[:], rk[:, a], ALU.add))
                    dve.tensor_scalar(lo_pos[:], pos_i[:], P - 1, None, ALU.bitwise_and)
                    link(dve.tensor_scalar(hi_pos[:], pos_i[:], 7, None, ALU.logical_shift_right))
                    if kind != "first":
                        dve.wait_ge(scattered[r], k * EB * 16)
                    dve.scalar_tensor_tensor(idx_st[:, r], lo_pos[:], float(ST), hi_pos[:], ALU.mult,
                                             ALU.add).then_inc(idx_ready, 1)
                    dve.wait_ge(idx_ready, s + 1)

                per = (EB - 1 + 4) * RING

                def turn(k, kind, back_kind):
                    for r in range(RING):
                        s = k * RING + r
                        if not (kind == "last" and r == RING - 1):
                            if kind != "first" or r >= 1:
                                dve.wait_ge(hist, s)
                            one_hots(dve, (s + 1) * EB, (r + 1) % 2, (r + 1) % RING).then_inc(oh_r, 1)
                        ranks(k, r, kind)
                        if r > 0:
                            places(k, r - 1, kind)
                        elif back_kind:
                            places(k - 1, RING - 1, back_kind)

                one_hots(dve, 0, 0, 0).then_inc(oh_r, 1)
                turn(0, "first", None)
                turn(1, "middle", "first")
                with dve.Fori(2, NB // RING - 1) as k:
                    tally.enter(k - 2, per)
                    turn(k, "middle", "middle")
                tally.leave(NB // RING - 3)
                turn(NB // RING - 1, "last", "middle")
                places(NB // RING - 1, RING - 1, "last")

            @block.tensor
            def _(pe):
                def count(k, r, kind):
                    a, s = r % 2, k * RING + r
                    pe.wait_ge(oh_r, s + 1)
                    if kind != "first" or r >= 2:
                        pe.wait_ge(H_ready, s - 1)
                    if kind != "first" or r >= 1:
                        pe.wait_ge(oht_ready, s)
                    for j in range(EB):
                        pe.matmul(cntp[a][:, j * NT:(j + 1) * NT], ohlo[:, a, j], ohhi[:, r, j], start=True, stop=True)
                        ins = pe.matmul(oht[j // HB][:, (j % HB) * EP:(j % HB + 1) * EP], ohlo[:, a, j],
                                        K["ident_b"][0:EP, 0:EP], start=True, stop=True)
                    ins.then_inc(hist, 1)
                    pe.wait_ge(hl_ready, s + 1)
                    if kind != "first" or r >= 1:
                        pe.wait_ge(krow_used, s)
                    for j in range(EB):
                        for c in range(2):
                            ins = pe.matmul(krow[j // HB][0:EP, (j % HB) * EP:(j % HB + 1) * EP],
                                            hl_st[:, r, j, c:c + 1].to_broadcast([EP, EP]),
                                            K["ident_b"][0:EP, 0:EP], start=c == 0, stop=c == 1)
                    ins.then_inc(krow_ps, 1)

                def look_up(k, r, kind):
                    a, s = r % 2, k * RING + r
                    pe.wait_ge(H_ready, s + 1)
                    pe.wait_ge(oht_ready, s + 1)
                    if kind != "first" or r >= 2:
                        pe.wait_ge(idx_ready, s - 1)
                    for j in range(EB):
                        ins = pe.matmul(lk[a][0:EP, j * NT:(j + 1) * NT], ohtS[:, a, j], Hr[:, a, j],
                                        start=True, stop=True)
                    ins.then_inc(lk_ps, 1)

                def step(k, r, kind):
                    if r < RING - 1:
                        count(k, r + 1, kind)
                    elif kind != "last":
                        count(k + 1, 0, "middle")
                    look_up(k, r, kind)

                count(0, 0, "first")
                sort_steps(pe, [], step)

            @block.scalar
            def _(act):
                def stage_keys(k, r, kind):
                    s = k * RING + r
                    if kind != "first":
                        act.wait_ge(krow_ps, s - RING + 1)
                    act.copy(hl_st[:, r], hl_b[:, bass.ds(s * EB, EB), :]).then_inc(hl_ready, 1)

                def step(k, r, kind):
                    s, a = k * RING + r, r % 2
                    if r < RING - 1:
                        stage_keys(k, r + 1, kind)
                    elif kind != "last":
                        stage_keys(k + 1, 0, "middle")
                    act.wait_ge(hist, s + 1)
                    if kind != "first" or r >= 2:
                        act.wait_ge(lk_ps, s - 1)
                    for b in range(2):
                        ins = act.copy(ohtS[:, a, b * HB:(b + 1) * HB].rearrange("p j e -> p (j e)"),
                                       oht[b][:, 0:HB * EP])
                    ins.then_inc(oht_ready, 1)
                    if kind != "first":
                        act.wait_ge(scattered[r], k * EB * 16)
                    act.copy(rec_st[:, r], rec[:, bass.ds(s * EB, EB), :]).then_inc(rec_ready, 1)

                stage_keys(0, 0, "first")
                sort_steps(act, [], step)

            @block.gpsimd
            def _(pool):
                def step(k, r, kind):
                    s = k * RING + r
                    pool.wait_ge(rec_ready, s + 1)
                    pool.wait_ge(idx_ready, s + 1)
                    pool.sem_inc(turns)
                    for j in range(EB):
                        pool.indirect_dma_start(sorted_d, bass.IndirectOffsetOnAxis(idx_st[:, r, j:j + 1], 0),
                                                rec_st[:, r, j, :], None).then_inc(scattered[r], 16)

                sort_steps(pool, [], step)
                for r in range(RING):
                    pool.wait_ge(scattered[r], 16 * ET // RING)


GB = 4
GR = 4
GN = ST // (GB * GR)


def gather_steps(eng, tallies, step):
    for r in range(GR):
        step(Batch(0, r))
    with eng.Fori(1, GN - 1) as k:
        for t, per in tallies:
            t.enter(k - 1, per)
        for r in range(GR):
            step(Batch(k, r))
    for t, per in tallies:
        t.leave(GN - 2)
    for r in range(GR):
        step(Batch(GN - 1, r))


def windows(nc, engine, table, x):
    _, w = nc.values_load_multi_w_load_instructions(
        table[0:1, bass.ds(x.b * GB, GB)], engines=(engine,), min_val=0, max_val=NT - 1,
        skip_runtime_bounds_check_because="a window's number is below NT as it is made")
    return w


class Batch:

    def __init__(self, k, r):
        self.k, self.r, self.a = k + r // GR, r % GR, r % 2
        self.b = self.k * GR + self.r

    def after(self, d):
        x = Batch(self.k, self.r + d)
        return None if isinstance(x.b, int) and x.b >= GN * GR else x

    def early(self, n):
        return isinstance(self.b, int) and self.b < n


def across(table):
    return table.rearrange("p (g c) -> p c g", c=CH)


def stage_tables(nc, sorted_d, win_d, T):
    ctx, sb, pb, sem = make_tools(nc)
    with ctx:
        rec, low_i = sb("rec_s", [P, ST, 2], I32), sb("low_i", [P, ST], I32)
        pad, win_all = sb("pad", [P, ST]), sb("win_all", [P, ST], I32)
        t_in, dve_link = sem("t_in"), sem("t_link")
        with nc.Block() as block:

            @block.sync
            def _(sp):
                sp.dma_start(rec[:], sorted_d.rearrange("(p t) c -> p t c", p=P)).then_inc(t_in, 16)
                sp.dma_start(T["win"][:], win_d.unsqueeze(0)).then_inc(t_in, 16)
                sp.dma_start(win_all[:], win_d.unsqueeze(0).to_broadcast([P, ST])).then_inc(t_in, 16)

            @block.vector
            def _(dve):
                link = linker(dve, Tally(dve_link))
                dve.wait_ge(t_in, 48)
                dve.memset(T["keep"][:, 0:1], 0.0)
                dve.tensor_tensor(T["keep"][:, 1:ST], win_all[:, 1:ST], win_all[:, 0:ST - 1], ALU.is_equal)
                dve.tensor_copy(T["key"][:], rec[:, :, 0])
                dve.tensor_copy(T["dst"][:], rec[:, :, 1])
                dve.tensor_copy(across(T["win_x"][:]), T["win"][:].rearrange("p (c g) -> p c g", c=CH))
                link(dve.tensor_scalar(low_i[:], rec[:, :, 0], P - 1, None, ALU.bitwise_and))
                link(dve.tensor_copy(T["lo"][:], low_i[:]))
                link(dve.tensor_scalar(pad[:], T["key"][:], 0.0, NO_LO - (P - 1), ALU.is_lt, ALU.mult))
                link(dve.tensor_tensor(T["lo"][:], T["lo"][:], pad[:], ALU.add))
                for name in ("key", "dst", "lo"):
                    ins = dve.tensor_copy(across(T[name + "_x"][:]), T[name][:].rearrange("p (c g) -> p c g", c=CH))
                link(ins)


def gathers(nc, pool, table, got, idx_st, idx_ready, free, arrived, turns):

    def step(x):
        pool.wait_ge(idx_ready, x.b + 1)
        if not x.early(GR):
            pool.wait_ge(free, x.b - GR + 1)
        pool.sem_inc(turns)
        for j in range(GB):
            pool.indirect_dma_start(got[:, x.r, j, :], None, table,
                                    bass.IndirectOffsetOnAxis(idx_st[:, x.r, j:j + 1], 0)).then_inc(arrived[x.r], 16)

    gather_steps(pool, [], step)
    for r in range(GR):
        pool.wait_ge(arrived[r], 16 * GB * GN)


def stage_scores(nc, K, T, q_sb, k_d, A):
    ctx, sb, pb, sem = make_tools(nc)
    with ctx:
        kg = sb("kg", [P, GR, GB, D])
        idx_st, lo_st = sb("idx_g", [P, GR, GB], I32), sb("lo_st", [P, GR, GB], BF16)
        spread = sb("spread", [P, 2, GB, P])
        prod = sb("prod", [P, 2, GB, D])
        p_lo = [pb(f"p_lo{a}") for a in range(2)]
        p_q = [pb(f"p_q{a}", [P, GB * D]) for a in range(2)]
        idx_ready, arrived, k_used = sem("idx_g_ready"), [sem(f"k_in{r}") for r in range(GR)], sem("k_used")
        lo_ready, lo_psum, spread_ready, q_psum = sem("lo_ready"), sem("lo_psum"), sem("spread_ready"), sem("q_psum")
        summed, turns = sem("summed"), sem("g_turns")

        with nc.Block() as block:

            @block.gpsimd
            def _(pool):
                gathers(nc, pool, k_d, kg, idx_st, idx_ready, k_used, arrived, turns)

            @block.scalar
            def _(act):
                def step(x):
                    if not x.early(GR):
                        act.wait_ge(arrived[x.r], x.k * GB * 16)
                        act.wait_ge(lo_psum, x.b - GR + 1)
                    act.copy(lo_st[:, x.r], T["lo_x"][:, bass.ds(x.b * GB, GB)]).then_inc(lo_ready, 1)
                    act.copy(idx_st[:, x.r], T["dst_x"][:, bass.ds(x.b * GB, GB)]).then_inc(idx_ready, 1)

                gather_steps(act, [], step)

            @block.tensor
            def _(pe):
                def rows(x):
                    pe.wait_ge(lo_ready, x.b + 1)
                    if not x.early(2):
                        pe.wait_ge(spread_ready, x.b - 1)
                    for j in range(GB):
                        ins = pe.matmul(p_lo[x.a][:, j * P:(j + 1) * P], lo_st[:, x.r, j:j + 1].to_broadcast([P, P]),
                                        K["ident_b"][:], start=True, stop=True)
                    ins.then_inc(lo_psum, 1)

                def spreads(x):
                    pe.wait_ge(spread_ready, x.b + 1)
                    if not x.early(2):
                        pe.wait_ge(k_used, x.b - 1)
                    ws = windows(nc, mybir.EngineType.PE, T["win_x"], x)
                    for j, w in enumerate(ws):
                        ins = pe.matmul(p_q[x.a][:, j * D:(j + 1) * D], spread[:, x.a, j],
                                        q_sb[:, bass.ds(w, 1), :].rearrange("p o d -> p (o d)"),
                                        start=True, stop=True)
                    ins.then_inc(q_psum, 1)

                def step(x):
                    if x.after(2):
                        rows(x.after(2))
                    if x.after(1):
                        spreads(x.after(1))

                rows(Batch(0, 0))
                rows(Batch(0, 1))
                spreads(Batch(0, 0))
                gather_steps(pe, [], step)

            @block.vector
            def _(dve):
                def one_hot(x):
                    dve.wait_ge(lo_psum, x.b + 1)
                    if not x.early(2):
                        dve.wait_ge(q_psum, x.b - 1)
                    dve.tensor_scalar(spread[:, x.a].rearrange("p j e -> p (j e)"), p_lo[x.a][:], K["part"][:, 0:1],
                                      None, ALU.is_equal).then_inc(spread_ready, 1)

                def step(x):
                    if x.after(1):
                        one_hot(x.after(1))
                    dve.wait_ge(q_psum, x.b + 1)
                    dve.wait_ge(arrived[x.r], (x.k + 1) * GB * 16)
                    dve.tensor_tensor(prod[:, x.a].rearrange("p j d -> p (j d)"), p_q[x.a][:],
                                      kg[:, x.r].rearrange("p j d -> p (j d)"), ALU.mult).then_inc(k_used, 1)
                    dve.wait_ge(k_used, x.b + 1)
                    dve.tensor_reduce(A[:, bass.ds(x.b * GB, GB), :],
                                      prod[:, x.a].rearrange("p j (h e) -> p j h e", h=H), AX.X,
                                      ALU.add).then_inc(summed, 1)

                one_hot(Batch(0, 0))
                gather_steps(dve, [], step)
                dve.wait_ge(summed, GR * GN)


def stage_softmax(nc, K, T, A, big):
    ctx, sb, pb, sem = make_tools(nc)
    with ctx:
        aT, kT = big[:, 0:CL], sb("kT", [P, CL])
        cut = big[:, CL:2 * CL + 1]
        fwd, top = sb("fwd", [P, CL]), sb("top", [P, CL])
        rows = sb("rows", [1, 4, H, CH])
        cont, whole = sb("cont", [1, H, CH + 1]), sb("whole", [1, H, CH])
        gate, end = sb("gate", [1, 2, H, CH]), sb("end", [1, 2, H, CH])
        carry, carry_ch = sb("carry", [1, 2, H, CH]), sb("carry_ch", [1, 2, CH * H])
        carry_c = sb("carry_c", [P, 2])
        key8 = top[:].rearrange("p (g x) -> p g x", g=SC)
        pt = [pb(f"pt{i}") for i in range(4)]
        pr, pc = pb("pr"), pb("pc")
        t_psum, t_out, link_s = sem("t_psum"), sem("t_out"), sem("link_s")
        k_psum, k_out, rows_psum, rows_ready, edges_ready = (sem("k_psum"), sem("k_out"), sem("rows_psum"),
                                                             sem("rows_ready"), sem("edges_ready"))
        carry_psum, diff_ready, exp_ready = sem("carry_psum"), sem("diff_ready"), sem("exp_ready")
        b_psum, b_out, key8_ready = sem("b_psum"), sem("b_out"), sem("key8_ready")
        A4 = A[:].rearrange("p (c g) h -> p c g h", c=CH)
        Ax = A[:].rearrange("p (g c) h -> p g (c h)", c=CH)
        Q = 4
        QN = SC // Q
        W = Q * P

        with nc.Block() as block:

            @block.tensor
            def _(pe):
                pe.wait_ge(key8_ready, 1)
                for i in range(QN):
                    if i >= 2:
                        pe.wait_ge(t_out, i - 1)
                    for g in range(Q):
                        ins = pe.transpose(pt[i % 2][:, g * P:(g + 1) * P], Ax[:, i * Q + g, :], K["ident"][:])
                    ins.then_inc(t_psum, 1)
                    if i >= 2:
                        pe.wait_ge(k_out, i - 1)
                    for g in range(Q):
                        ins = pe.transpose(pt[2 + i % 2][:, g * P:(g + 1) * P],
                                           key8[:, i * Q + g, :], K["ident"][:])
                    ins.then_inc(k_psum, 1)
                pe.wait_ge(edges_ready, 1)
                for i, col in enumerate((fwd[:, CL - 1:CL], top[:, 0:1], kT[:, 0:1], kT[:, CL - 1:CL])):
                    ins = pe.matmul(pr[0:1, i * P:(i + 1) * P], col, K["ident"][:], start=True, stop=True)
                ins.then_inc(rows_psum, 1)
                pe.wait_ge(rows_ready, 1)
                for i in range(2):
                    ins = pe.matmul(pc[:, i:i + 1], carry_ch[0:1, i, :], K["ones"][0:1, 0:1], start=True, stop=True)
                ins.then_inc(carry_psum, 1)
                for i in range(QN):
                    pe.wait_ge(exp_ready, i + 1)
                    if i >= 4:
                        pe.wait_ge(b_out, i - 3)
                    for g in range(Q):
                        ins = pe.transpose(pt[i % 4][:, g * P:(g + 1) * P], aT[:, (i * Q + g) * P:(i * Q + g + 1) * P],
                                           K["ident"][:])
                    ins.then_inc(b_psum, 1)

            @block.scalar
            def _(act):
                for i in range(QN):
                    act.wait_ge(t_psum, i + 1)
                    act.copy(aT[:, i * W:(i + 1) * W], pt[i % 2][:]).then_inc(t_out, 1)
                for i in range(QN):
                    act.wait_ge(diff_ready, i + 1)
                    act.activation(aT[:, i * W:(i + 1) * W], fwd[:, i * W:(i + 1) * W], ACT.Exp,
                                   scale=SCALE).then_inc(exp_ready, 1)

            @block.vector
            def _(dve):
                link = linker(dve, Tally(link_s))
                dve.tensor_copy(top[:].rearrange("p (t h) -> p t h", h=H),
                                T["key_x"][:].unsqueeze(2).to_broadcast([P, ST, H])).then_inc(key8_ready, 1)
                for i in range(QN):
                    dve.wait_ge(k_psum, i + 1)
                    dve.tensor_copy(kT[:, i * W:(i + 1) * W], pt[2 + i % 2][:]).then_inc(k_out, 1)
                dve.wait_ge(k_out, QN)
                dve.memset(cut[:, 0:1], 0.0)
                dve.memset(cut[:, CL:CL + 1], 0.0)
                link(dve.tensor_tensor(cut[:, 1:CL], kT[:, 1:CL], kT[:, 0:CL - 1], ALU.not_equal))
                link(dve.tensor_scalar(cut[:, 1:CL], cut[:, 1:CL], LOW, None, ALU.mult))
                dve.wait_ge(t_out, QN)
                dve.tensor_tensor_scan(fwd[:], cut[:, 0:CL], aT[:], LOW, ALU.add, ALU.max)
                dve.tensor_tensor_scan(top[:, ::-1], cut[:, 1:CL + 1][:, ::-1], aT[:, ::-1], LOW, ALU.add,
                                       ALU.max).then_inc(edges_ready, 1)
                dve.wait_ge(rows_psum, 1)
                link(dve.tensor_copy(rows[:], pr[0:1, 0:4 * P].rearrange("o (r c h) -> o r h c", r=4, h=H)))
                link(dve.memset(cont[:], 0.0))
                dve.tensor_tensor(cont[:, :, 1:CH], rows[:, 2, :, 1:CH], rows[:, 3, :, 0:CH - 1], ALU.is_equal)
                link(dve.tensor_tensor(whole[:], rows[:, 2], rows[:, 3], ALU.is_equal))
                dve.tensor_tensor(gate[:, 0], whole[:], cont[:, :, 0:CH], ALU.mult)
                link(dve.tensor_tensor(gate[:, 1], whole[:], cont[:, :, 1:CH + 1], ALU.mult))
                link(dve.tensor_scalar(gate[:], gate[:], 1.0, -LOW, ALU.subtract, ALU.mult))
                flat = [x.rearrange("o h c -> o (h c)") for x in
                        (gate[:, 0], rows[:, 0], end[:, 0], gate[:, 1], rows[:, 1], end[:, 1])]
                dve.tensor_tensor_scan(flat[2], flat[0], flat[1], LOW, ALU.add, ALU.max)
                link(dve.tensor_tensor_scan(flat[5][:, ::-1], flat[3][:, ::-1], flat[4][:, ::-1], LOW, ALU.add,
                                            ALU.max))
                link(dve.tensor_scalar(cont[:], cont[:], 1.0, -LOW, ALU.subtract, ALU.mult))
                dve.memset(carry[:, 0, :, 0:1], LOW)
                dve.memset(carry[:, 1, :, CH - 1:CH], LOW)
                dve.tensor_tensor(carry[:, 0, :, 1:CH], end[:, 0, :, 0:CH - 1], cont[:, :, 1:CH], ALU.add)
                link(dve.tensor_tensor(carry[:, 1, :, 0:CH - 1], end[:, 1, :, 1:CH], cont[:, :, 1:CH], ALU.add))
                dve.tensor_copy(carry_ch[:].rearrange("o r (c h) -> o r h c", h=H), carry[:]).then_inc(rows_ready, 1)
                dve.wait_ge(carry_psum, 1)
                link(dve.tensor_copy(carry_c[:], pc[:, 0:2]))
                link(dve.tensor_tensor_scan(fwd[:], cut[:, 0:CL], aT[:], carry_c[:, 0:1], ALU.add, ALU.max))
                link(dve.tensor_tensor_scan(top[:, ::-1], cut[:, 1:CL + 1][:, ::-1], fwd[:, ::-1], carry_c[:, 1:2],
                                            ALU.add, ALU.max))
                for i in range(QN):
                    s = slice(i * W, (i + 1) * W)
                    dve.tensor_tensor(fwd[:, s], aT[:, s], top[:, s], ALU.subtract).then_inc(diff_ready, 1)
                for i in range(QN):
                    dve.wait_ge(b_psum, i + 1)
                    dve.tensor_copy(A4[:, :, i * Q:(i + 1) * Q, :].rearrange("p c g h -> p g c h"),
                                    pt[i % 4][:].rearrange("p (g c h) -> p g c h", g=Q, h=H)).then_inc(b_out, 1)
                dve.wait_ge(b_out, QN)


def stage_sums(nc, K, T, A, v_d, acc):
    DX = D + H
    ctx, sb, pb, sem = make_tools(nc)
    with ctx:
        vg = sb("vg", [P, GR, GB, D])
        idx_st = sb("idx_v", [P, GR, GB], I32)
        pick = sb("pick", [P, 2, GB, P])
        wv = sb("wv", [P, 2, GB, DX])
        run = sb("run", [P, 2, GB, DX])
        p_s = [[pb(f"p_s{a}{j}") for j in range(GB)] for a in range(2)]
        idx_ready, arrived, v_used = sem("idx_v_ready"), [sem(f"v_in{r}") for r in range(GR)], sem("v_used")
        kept = sem("kept")
        w_ready, s_psum, added, cleared, turns = (sem("wcol_ready"), sem("s_psum"), sem("added"), sem("cleared"),
                                                  sem("v_turns"))
        with nc.Block() as block:

            @block.gpsimd
            def _(pool):
                gathers(nc, pool, v_d, vg, idx_st, idx_ready, v_used, arrived, turns)

            @block.scalar
            def _(act):
                def targets(x):
                    if not x.early(GR):
                        act.wait_ge(arrived[x.r], x.k * GB * 16)
                    act.copy(idx_st[:, x.r], T["dst"][:, bass.ds(x.b * GB, GB)]).then_inc(idx_ready, 1)

                def weights(x):
                    if not x.early(2):
                        act.wait_ge(s_psum, x.b - 1)
                    act.copy(wv[:, x.a, :, D:DX], A[:, bass.ds(x.b * GB, GB), :]).then_inc(w_ready, 1)

                def step(x):
                    if x.after(GR - 1):
                        targets(x.after(GR - 1))
                    if x.after(1):
                        weights(x.after(1))
                    if not x.early(1):
                        place(x.after(-1))

                def place(x):
                    ws = windows(nc, mybir.EngineType.Activation, T["win"], x)
                    for j, w in enumerate(ws):
                        act.wait_ge(added, x.b * GB + j + 1)
                        if j == 0 and not x.early(1):
                            act.wait_ge(kept, x.b * GB)
                        elif j:
                            act.wait_ge(kept, x.b * GB + j)
                        act.copy(acc[:, bass.ds(w, 1), :].rearrange("p o d -> p (o d)"), run[:, x.a, j]).then_inc(kept, 1)

                for i in range(GR - 1):
                    targets(Batch(0, i))
                weights(Batch(0, 0))
                act.wait_ge(cleared, 2)
                gather_steps(act, [], step)
                place(Batch(GN - 1, GR - 1))
                act.wait_ge(kept, ST)

            @block.tensor
            def _(pe):
                def step(x):
                    pe.wait_ge(w_ready, x.b + 1)
                    pe.wait_ge(v_used, x.b + 1)
                    if not x.early(2):
                        pe.wait_ge(added, (x.b - 1) * GB)
                    for j in range(GB):
                        ins = pe.matmul(p_s[x.a][j][:, 0:DX], pick[:, x.a, j], wv[:, x.a, j], start=True, stop=True)
                    ins.then_inc(s_psum, 1)

                gather_steps(pe, [], step)

            @block.vector
            def _(dve):
                def weigh(x):
                    if not x.early(2):
                        dve.wait_ge(s_psum, x.b - 1)
                    dve.tensor_tensor(pick[:, x.a], K["col"][:].unsqueeze(1).to_broadcast([P, GB, P]),
                                      T["lo"][:, bass.ds(x.b * GB, GB)].unsqueeze(2).to_broadcast([P, GB, P]),
                                      ALU.is_equal)
                    dve.wait_ge(arrived[x.r], (x.k + 1) * GB * 16)
                    dve.tensor_tensor(wv[:, x.a, :, 0:D].rearrange("p j (h e) -> p j h e", h=H),
                                      vg[:, x.r].rearrange("p j (h e) -> p j h e", h=H),
                                      A[:, bass.ds(x.b * GB, GB), :].unsqueeze(3).to_broadcast([P, GB, H, HD]),
                                      ALU.mult).then_inc(v_used, 1)

                def add(x):
                    dve.wait_ge(s_psum, x.b + 1)
                    if not x.early(2):
                        dve.wait_ge(kept, (x.b - 1) * GB)
                    for j in range(GB):
                        last = run[:, x.a, j - 1] if j else run[:, 1 - x.a, GB - 1]
                        dve.scalar_tensor_tensor(run[:, x.a, j], last, T["keep"][:, bass.ds(x.b * GB + j, 1)],
                                                 p_s[x.a][j][:, 0:DX], ALU.mult, ALU.add).then_inc(added, 1)
                        dve.wait_ge(added, x.b * GB + j + 1)

                def step(x):
                    if x.after(1):
                        weigh(x.after(1))
                    add(x)

                dve.memset(run[:], 0.0).then_inc(cleared, 1)
                dve.memset(acc[:], 0.0).then_inc(cleared, 1)
                dve.wait_ge(cleared, 2)
                weigh(Batch(0, 0))
                gather_steps(dve, [], step)


def stage_dense(nc, K, A_in, acc, h0_d, out):
    FB, XB = F // P, FX // P
    G = GT * P
    ctx, sb, pb, sem = make_tools(nc)
    with ctx:
        w1, w2 = sb("w1", [P, DC, F]), sb("w2", [P, FB, D])
        xw1, xw2 = sb("xw1", [P, NX, DC, FX]), sb("xw2", [P, NX, XB, D])
        gw, gb = sb("gw", [P, DC, NX]), sb("gb", [P, NX])
        xb2 = sb("xb2", [NX, D])
        b1c, xb1c = sb("b1c", [P, FB]), sb("xb1c", [P, NX, XB])
        vec = sb("vec", [P, 5, D])
        xin, hin = sb("xin", [P, 2, GT, D]), sb("hin", [P, GT, D])
        y1 = sb("y1", [P, GT, D])
        n_b = y1
        y1T, nT = sb("y1T", [P, DC, G]), sb("nT", [P, 2, DC, G])
        x1 = xin
        res = xin
        h1T, gT = sb("h1T", [P, FB, G]), sb("gT", [P, 2, XB, G])
        rden = sb("rden", [P, GT, H])
        stats, mv, std, rstd = sb("d_stats", [P, GT, 6]), sb("d_mv", [P, GT, 2]), sb("d_std", [P, GT]), sb("d_rstd", [P, GT])
        eps = sb("d_eps", [P, 1])
        lg, ex, pr = sb("lg", [P, GT, NX]), sb("ex", [P, GT, NX]), sb("pr_x", [P, GT, NX])
        top, tot = sb("top_x", [P, GT]), sb("tot_x", [P, GT])
        more, equal, rank = sb("more", [P, GT, NX, NX]), sb("equal", [P, GT, NX, NX]), sb("rank", [P, GT, NX])
        before = sb("before", [P, NX, NX])
        cw, cwT = sb("cw", [P, 2, GT, NX]), sb("cwT", [NX, G])
        p_up = [pb(f"p_up{i}") for i in range(2)]
        p_dn, p_md = pb("p_dn", [P, GT * D]), pb("p_md", [P, GT * D])
        p_t = [pb(f"p_t{i}") for i in range(DC)]

        w_in, consts = sem("dw_in"), sem("dconsts")
        g_in = [sem(f"g_in{a}") for a in range(2)]
        var_r, std_r, y1_r, n_r = sem("var_r"), sem("std_r"), sem("y1_r"), sem("n_r")
        t_ps, t_out = sem("dt_ps"), sem("dt_out")
        up_ps, up_out = sem("up_ps"), sem("up_out")
        dn_ps, dn_used = sem("dn_ps"), sem("dn_used")
        md_ps, md_used = sem("md_ps"), sem("md_used")
        lg_ps, lg_r, ex_r, cw_r, ct_ps, ct_r = (sem("lg_ps"), sem("lg_r"), sem("ex_r"), sem("cw_r"), sem("ct_ps"),
                                                sem("ct_r"))
        res_r, stored, dl, x1_r, turns = (sem("res_r"), [sem(f"d_stored{a}") for a in range(2)], sem("dl"),
                                          sem("x1_r"), sem("d_turns"))
        h_used = sem("h_used")

        class At:

            def __init__(self, k, a):
                self.k, self.a = k, a
                self.g = k * 2 + a
                self.early = isinstance(k, int) and k == 0
                self.nt = 1 if isinstance(k, int) and k * 2 + a == NG else GT
                self.n = self.nt * P
                self.first = self.early and a == 0

        def run(eng, tallies, front0, turn, moe_last):
            front0(At(0, 0))
            pairs = NG // 2

            def pair(k):
                turn(At(k, 0), At(k, 1))
                turn(At(k, 1), At(k + 1, 0))

            pair(0)
            with eng.Fori(1, pairs - 1) as k:
                for t, per in tallies:
                    t.enter(k - 1, per)
                pair(k)
            for t, per in tallies:
                t.leave(pairs - 2)
            pair(pairs - 1)
            moe_last(At(pairs, 0))

        def rows(dram, q):
            if q.nt == 1:
                return dram[NG * G:NG * G + REST, :]
            return dram[0:NG * G, :].rearrange("(g t p) d -> g p t d", t=GT, p=P)[q.g]

        def part(q, buf):
            return buf[0:REST, q.a, 0, :] if q.nt == 1 else buf[:, q.a]

        with nc.Block() as block:

            @block.sync
            def _(sp):
                def col(v, n):
                    return v.rearrange("(b p) -> p b", p=P)

                def load(q):
                    if not q.early:
                        sp.wait_ge(stored[q.a], q.k * 16)
                        sp.sem_inc(turns)
                    if not q.first:
                        sp.wait_ge(h_used, q.g)
                        sp.sem_inc(turns)
                    h_to = hin[0:REST, 0, :] if q.nt == 1 else hin[:]
                    sp.dma_start(h_to, rows(h0_d, q)).then_inc(g_in[q.a], 16)
                    sp.dma_start(part(q, xin), rows(A_in["x"], q)).then_inc(g_in[q.a], 16)

                def store(q):
                    sp.wait_ge(res_r, q.g + 1)
                    sp.sem_inc(turns)
                    sp.dma_start(rows(out, q), part(q, res)).then_inc(stored[q.a], 16)

                def row(v):
                    return v.unsqueeze(0).to_broadcast([P, v.shape[0]])

                def front0(q):
                    load(q)
                    for i, name in enumerate(("ln1_g", "ln1_b", "ln2_g", "ln2_b", "b2")):
                        sp.dma_start(vec[:, i], row(A_in["L0_gnn_" + name])).then_inc(w_in, 16)
                    sp.dma_start(w1[:], A_in["L0_gnn_w1"].rearrange("(c p) f -> p c f", p=P)).then_inc(w_in, 16)
                    sp.dma_start(w2[:], A_in["L0_gnn_w2"].rearrange("(c p) f -> p c f", p=P)).then_inc(w_in, 16)
                    sp.dma_start(gw[:], A_in["L0_ffn_gate_w"].rearrange("(c p) f -> p c f", p=P)).then_inc(w_in, 16)
                    sp.dma_start(gb[:], row(A_in["L0_ffn_gate_b"])).then_inc(w_in, 16)
                    sp.dma_start(xb2[:], A_in["L0_ffn_b2"]).then_inc(w_in, 16)
                    with nc.allow_non_contiguous_dma(reason="biases by partition, once"):
                        sp.dma_start(b1c[:], A_in["L0_gnn_b1"].rearrange("(b p) -> p b", p=P)).then_inc(w_in, 16)
                        sp.dma_start(xb1c[:], A_in["L0_ffn_b1"].rearrange("e (b p) -> p e b", p=P)).then_inc(w_in, 16)
                    for e in range(NX):
                        sp.dma_start(xw1[:, e], A_in["L0_ffn_W1"][e].rearrange("(c p) f -> p c f", p=P)).then_inc(w_in, 16)
                        sp.dma_start(xw2[:, e], A_in["L0_ffn_W2"][e].rearrange("(c p) f -> p c f", p=P)).then_inc(w_in, 16)

                def turn(q, nx):
                    load(nx)
                    store(q)

                run(sp, [], front0, turn, store)
                for a in range(2):
                    sp.wait_ge(stored[a], 16 * (NG // 2 + 1 - a))

            W_ALL = 16 * (12 + 2 * NX)

            @block.vector
            def _(dve):
                t_l = Tally(dl)
                link = linker(dve, t_l)
                t_var = Tally(var_r)

                def wide(i, nt):
                    return vec[:, i].unsqueeze(1).to_broadcast([P, nt, D])

                def norm_in(src, nt):
                    for i in range(nt):
                        ins = dve.bn_stats(stats[:, i], src[:, i])
                    link(ins)
                    dve.sem_inc(turns)
                    for i in range(nt):
                        ins = dve.bn_aggr(mv[:, i], stats[:, i])
                    t_var.n += 1
                    ins.then_inc(var_r, 1)

                def norm_out(dst, src, nt):
                    dve.wait_ge(std_r, t_var.value())
                    link(dve.reciprocal(rstd[:, 0:nt], std[:, 0:nt]))
                    for i in range(nt):
                        ins = dve.tensor_scalar(dst[:, i], src[:, i], mv[:, i, 0:1], rstd[:, i:i + 1], ALU.subtract,
                                                ALU.mult)
                    return ins

                def attention(q):
                    nt = q.nt
                    dve.wait_ge(g_in[q.a], q.k * 32 + 32)
                    av = acc[:, bass.ds(q.g * GT, nt), :]
                    link(dve.tensor_scalar(rden[:, 0:nt], av[:, :, D:D + H], 1e-30, None, ALU.max))
                    link(dve.reciprocal(rden[:, 0:nt], rden[:, 0:nt]))
                    if not q.first:
                        dve.wait_ge(t_ps, q.g * 2)
                    y1v = y1[:, 0:nt]
                    link(dve.tensor_tensor(y1v.rearrange("p t (h e) -> p t h e", h=H),
                                           av[:, :, 0:D].rearrange("p t (h e) -> p t h e", h=H),
                                           rden[:, 0:nt].unsqueeze(3).to_broadcast([P, nt, H, HD]), ALU.mult))
                    add = dve.tensor_tensor(y1v, y1v, hin[:, 0:nt], ALU.add)
                    add.then_inc(h_used, 1)
                    dve.wait_ge(h_used, q.g + 1)
                    norm_in(y1, nt)
                    link(norm_out(y1, y1, nt))
                    link(dve.tensor_tensor(y1v, y1v, wide(0, nt), ALU.mult))
                    dve.tensor_tensor(y1v, y1v, wide(1, nt), ALU.add).then_inc(y1_r, 1)
                    dve.wait_ge(y1_r, q.g + 1)

                def after_ffn(q):
                    nt = q.nt
                    nv = n_b[:, 0:nt]
                    dve.wait_ge(dn_ps, q.g + 1)
                    if not q.first:
                        dve.wait_ge(t_ps, q.g * 2)
                    dve.tensor_tensor(nv.rearrange("p t d -> p (t d)"), p_dn[:, 0:nt * D],
                                      y1[:, 0:nt].rearrange("p t d -> p (t d)"), ALU.add).then_inc(dn_used, 1)
                    dve.wait_ge(dn_used, q.g + 1)
                    link(dve.tensor_tensor(nv, nv, wide(4, nt), ALU.add))
                    norm_in(n_b, nt)

                def residual(q):
                    nt = q.nt
                    nv, xv = n_b[:, 0:nt], x1[:, q.a, 0:nt]
                    link(norm_out(n_b, n_b, nt))
                    link(dve.tensor_tensor(nv, nv, wide(2, nt), ALU.mult))
                    link(dve.tensor_tensor(nv, nv, wide(3, nt), ALU.add))
                    link(dve.tensor_tensor(xv, xv, nv, ALU.add))
                    norm_in(x1[:, q.a], nt)

                def normal(q):
                    norm_out(n_b, x1[:, q.a], q.nt).then_inc(n_r, 1)

                def gate(q):
                    nt = q.nt
                    dve.wait_ge(lg_ps, q.g + 1)
                    lv = lg[:, 0:nt]
                    link(dve.tensor_tensor(lv, p_t[0][:, 0:nt * NX].rearrange("p (t e) -> p t e", e=NX),
                                           gb[:].unsqueeze(1).to_broadcast([P, nt, NX]), ALU.add))
                    link(dve.tensor_reduce(top[:, 0:nt], lv, AX.X, ALU.max))
                    dve.tensor_tensor(lv, lv, top[:, 0:nt].unsqueeze(2).to_broadcast([P, nt, NX]),
                                      ALU.subtract).then_inc(lg_r, 1)

                def choose(q):
                    nt = q.nt
                    dve.wait_ge(ex_r, q.g + 1)
                    pv = pr[:, 0:nt]
                    link(dve.tensor_reduce(tot[:, 0:nt], ex[:, 0:nt], AX.X, ALU.add))
                    link(dve.reciprocal(tot[:, 0:nt], tot[:, 0:nt]))
                    link(dve.tensor_tensor(pv, ex[:, 0:nt], tot[:, 0:nt].unsqueeze(2).to_broadcast([P, nt, NX]),
                                           ALU.mult))
                    for t in range(nt):
                        mine = pr[:, t].unsqueeze(2).to_broadcast([P, NX, NX])
                        other = pr[:, t].unsqueeze(1).to_broadcast([P, NX, NX])
                        dve.tensor_tensor(more[:, t], other, mine, ALU.is_gt)
                        ins = dve.tensor_tensor(equal[:, t], other, mine, ALU.is_equal)
                    link(ins)
                    mv_, ev = more[:, 0:nt].rearrange("p t j i -> p t (j i)"), equal[:, 0:nt].rearrange("p t j i -> p t (j i)")
                    link(dve.tensor_tensor(ev, ev, before[:].rearrange("p j i -> p (j i)").unsqueeze(1)
                                           .to_broadcast([P, nt, NX * NX]), ALU.mult))
                    link(dve.tensor_tensor(mv_, mv_, ev, ALU.add))
                    link(dve.tensor_reduce(rank[:, 0:nt], more[:, 0:nt], AX.X, ALU.add))
                    rf, pf = rank[:, 0:nt].rearrange("p t e -> p (t e)"), pr[:, 0:nt].rearrange("p t e -> p (t e)")
                    dve.scalar_tensor_tensor(cw[:, q.a, 0:nt].rearrange("p t e -> p (t e)"), rf, 2.0, pf, ALU.is_lt,
                                             ALU.mult).then_inc(cw_r, 1)

                def turned(q):
                    dve.wait_ge(ct_ps, q.g + 1)
                    dve.tensor_copy(cwT[:, 0:q.n], p_t[1][0:NX, 0:q.n]).then_inc(ct_r, 1)

                def begin(q):
                    dve.wait_ge(md_ps, q.g * (NX + 1) + 1)
                    dve.tensor_tensor(res[:, q.a, 0:q.nt].rearrange("p t d -> p (t d)"), p_md[:, 0:q.nt * D],
                                      x1[:, q.a, 0:q.nt].rearrange("p t d -> p (t d)"), ALU.add).then_inc(md_used, 1)
                    dve.wait_ge(md_used, q.g * (NX + 1) + 1)

                def add_expert(q, e):
                    u = q.g * (NX + 1) + 2 + e
                    dve.wait_ge(md_ps, u)
                    for t in range(q.nt):
                        rv = res[:, q.a, t]
                        ins = dve.scalar_tensor_tensor(rv, p_md[:, t * D:(t + 1) * D], cw[:, q.a, t, e:e + 1], rv,
                                                       ALU.mult, ALU.add)
                    ins.then_inc(md_used, 1)
                    dve.wait_ge(md_used, u)

                front = {2: after_ffn, 3: residual, 4: normal, 5: gate, 6: choose, 7: turned}

                def front0(q):
                    dve.memset(eps[:], EPS).then_inc(consts, 1)
                    dve.tensor_tensor(before[:], K["col"][:, 0:NX].unsqueeze(1).to_broadcast([P, NX, NX]),
                                      K["col"][:, 0:NX].unsqueeze(2).to_broadcast([P, NX, NX]),
                                      ALU.is_lt).then_inc(consts, 1)
                    dve.wait_ge(w_in, W_ALL)
                    attention(q)
                    for e in range(2, NX):
                        front[e](q)

                def turn(q, nx):
                    attention(nx)
                    begin(q)
                    for e in range(NX):
                        if e in front:
                            front[e](nx)
                        add_expert(q, e)
                    dve.sem_inc(res_r)

                def moe_last(q):
                    begin(q)
                    for e in range(NX):
                        add_expert(q, e)
                    dve.sem_inc(res_r)

                links = 7 + 2 + 6 + 1 + 2 + 7
                run(dve, [(t_l, 2 * links), (t_var, 6)], front0, turn, moe_last)

            @block.scalar
            def _(act):
                t_up, t_sq = Tally(up_out), Tally(std_r)

                def root(q):
                    t_sq.n += 1
                    act.wait_ge(var_r, t_sq.value())
                    act.activation(std[:, 0:q.nt], mv[:, 0:q.nt, 1], ACT.Sqrt, bias=eps[:]).then_inc(std_r, 1)

                def hidden(dst, func, bias):
                    i = t_up.n % 2
                    t_up.n += 1
                    act.wait_ge(up_ps, t_up.value())
                    act.activation(dst, p_up[i][:, 0:dst.shape[-1]], func, bias=bias).then_inc(up_out, 1)

                def gelus(q, e):
                    if e >= 2 or not q.first:
                        back = q.g * (NX + 1) + 1 + e - 1 if e >= 2 else (q.g - 1) * (NX + 1) + 1 + NX - 1 + e
                        act.wait_ge(md_ps, back)
                    for b in range(XB):
                        hidden(gT[:, e % 2, b, 0:q.n], ACT.Gelu, xb1c[:, e, b:b + 1])

                def turned(q, which, dst):
                    act.wait_ge(t_ps, q.g * 2 + which + 1)
                    for c in range(DC):
                        ins = act.copy(dst[:, c, 0:q.n], p_t[c][:, 0:q.n])
                    ins.then_inc(t_out, 1)

                def y1_turned(q):
                    turned(q, 0, y1T)

                def relus(q):
                    if not q.first:
                        act.wait_ge(dn_ps, q.g)
                    for b in range(FB):
                        hidden(h1T[:, b, 0:q.n], ACT.Relu, b1c[:, b:b + 1])

                def n_turned(q):
                    if not q.early:
                        act.wait_ge(md_ps, (q.g - 1) * (NX + 1))
                    turned(q, 1, nT[:, q.a])

                def exps(q):
                    act.wait_ge(lg_r, q.g + 1)
                    act.activation(ex[:, 0:q.nt], lg[:, 0:q.nt], ACT.Exp).then_inc(ex_r, 1)

                front = {0: y1_turned, 1: relus, 2: root, 3: root, 4: n_turned, 5: exps}

                def front0(q):
                    act.wait_ge(consts, 2)
                    root(q)
                    for e in range(6):
                        front[e](q)

                def turn(q, nx):
                    root(nx)
                    gelus(q, 0)
                    for e in range(NX):
                        if e < NX - 1:
                            gelus(q, e + 1)
                        if e in front:
                            front[e](nx)

                def moe_last(q):
                    for e in range(NX):
                        gelus(q, e)

                run(act, [(t_up, 2 * (NX * XB + FB)), (t_sq, 6)], front0, turn, moe_last)

            @block.tensor
            def _(pe):
                t_up = Tally(up_ps)

                def hidden(blocks, n):
                    i = t_up.n % 2
                    if t_up.n >= 2 or t_up.k is not None:
                        pe.wait_ge(up_out, t_up.value(1))
                    t_up.n += 1
                    for c, (w, m) in enumerate(blocks):
                        ins = pe.matmul(p_up[i][:, 0:n], w, m, start=c == 0, stop=c == len(blocks) - 1)
                    ins.then_inc(up_ps, 1)

                def up(q, e):
                    if e == 0:
                        pe.wait_ge(t_out, q.g * 2 + 2)
                    for b in range(XB):
                        hidden([(xw1[:, e, c, b * P:(b + 1) * P], nT[:, q.a, c, 0:q.n]) for c in range(DC)], q.n)

                def down(q, e):
                    pe.wait_ge(up_out, gelu_mark(q, e))
                    pe.wait_ge(md_used, q.g * (NX + 1) + 1 + e)
                    for t in range(q.nt):
                        for b in range(XB):
                            ins = pe.matmul(p_md[:, t * D:(t + 1) * D], gT[:, e % 2, b, t * P:(t + 1) * P],
                                            xw2[:, e, b], start=b == 0, stop=b == XB - 1)
                    ins.then_inc(md_ps, 1)

                marks = {}

                def gelu_mark(q, e):
                    n = marks[e]
                    return n if t_up.k is None else t_up.k * t_up.per + n

                def transposes(q, src, ready, which):
                    pe.wait_ge(ready, q.g + 1)
                    if which == 0 and not q.first:
                        pe.wait_ge(ct_r, q.g)
                    if which == 1:
                        pe.wait_ge(t_out, q.g * 2 + 1)
                    for c in range(DC):
                        for t in range(q.nt):
                            ins = pe.transpose(p_t[c][:, t * P:(t + 1) * P], src[:, t, c * P:(c + 1) * P], K["ident"][:])
                    ins.then_inc(t_ps, 1)

                def ffn_up(q):
                    pe.wait_ge(t_out, q.g * 2 + 1)
                    for b in range(FB):
                        hidden([(w1[:, c, b * P:(b + 1) * P], y1T[:, c, 0:q.n]) for c in range(DC)], q.n)

                def ffn_down(q):
                    pe.wait_ge(up_out, t_up.value())
                    if not q.first:
                        pe.wait_ge(dn_used, q.g)
                    for t in range(q.nt):
                        for b in range(FB):
                            ins = pe.matmul(p_dn[:, t * D:(t + 1) * D], h1T[:, b, t * P:(t + 1) * P], w2[:, b],
                                            start=b == 0, stop=b == FB - 1)
                    ins.then_inc(dn_ps, 1)

                def logits(q):
                    pe.wait_ge(t_out, q.g * 2 + 2)
                    for t in range(q.nt):
                        for c in range(DC):
                            ins = pe.matmul(p_t[0][:, t * NX:(t + 1) * NX], nT[:, q.a, c, t * P:(t + 1) * P], gw[:, c],
                                            start=c == 0, stop=c == DC - 1)
                    ins.then_inc(lg_ps, 1)

                def weights_turned(q):
                    pe.wait_ge(cw_r, q.g + 1)
                    for t in range(q.nt):
                        ins = pe.transpose(p_t[1][0:NX, t * P:(t + 1) * P], cw[:, q.a, t], K["ident"][:])
                    ins.then_inc(ct_ps, 1)

                front = {0: lambda q: transposes(q, y1, y1_r, 0), 1: ffn_up, 2: ffn_down,
                         4: lambda q: transposes(q, n_b, n_r, 1), 5: logits, 6: weights_turned}

                def begin(q):
                    pe.wait_ge(ct_r, q.g + 1)
                    if not q.first:
                        pe.wait_ge(md_used, q.g * (NX + 1))
                    for t in range(q.nt):
                        ins = pe.matmul(p_md[:, t * D:(t + 1) * D], cwT[:, t * P:(t + 1) * P], xb2[:],
                                        start=True, stop=True)
                    ins.then_inc(md_ps, 1)

                def front0(q):
                    pe.wait_ge(w_in, W_ALL)
                    for e in front:
                        front[e](q)

                def turn(q, nx):
                    begin(q)
                    up(q, 0)
                    marks[0] = t_up.n
                    for e in range(NX):
                        if e < NX - 1:
                            up(q, e + 1)
                            marks[e + 1] = t_up.n
                        if e in front and nx is not None:
                            front[e](nx)
                        down(q, e)

                run(pe, [(t_up, 2 * (NX * XB + FB))], front0, turn, lambda q: turn(q, None))
def program(nc, A_in, out):
    ctx, sb, pb, sem = make_tools(nc)

    def scratch(name, shape, dt=F32):
        return nc.dram_tensor(name, shape, dt, kind="Internal").ap()

    h0_d, k_d, v_d = (scratch(n, [N, D]) for n in ("h0_d", "k_d", "v_d"))
    sorted_d, win_d = scratch("sorted_d", [P * ST, 2], I32), scratch("win_d", [ST], I32)
    with ctx:
        K = constants(nc, sb)
        big = sb("big", [P, max(NT * (D + H), 2 * CL + 1)])
        q_sb = big[:, 0:NT * D].rearrange("p (t d) -> p t d", t=NT)
        acc = big[:, 0:NT * (D + H)].rearrange("p (t d) -> p t d", t=NT)
        stage_constants(nc, K)
        stage_sort(nc, K, A_in["src"], A_in["dst"], sorted_d, win_d)
        edges, sb2, _, _ = make_tools(nc)
        with edges:
            T = {}
            for x in ("", "_x"):
                T["key" + x], T["lo" + x] = sb2("T_key" + x, [P, ST]), sb2("T_lo" + x, [P, ST])
                T["dst" + x], T["win" + x] = sb2("T_dst" + x, [P, ST], I32), sb2("T_win" + x, [1, ST], I32)
            T["keep"] = sb2("T_keep", [P, ST])
            A = sb2("A", [P, ST, H])
            stage_tables(nc, sorted_d, win_d, T)
            stage_qkv(nc, K, A_in["x"], A_in["L0_gnn_w_qkv"], A_in["L0_gnn_b_qkv"], h0_d, k_d, v_d, q_sb)
            stage_scores(nc, K, T, q_sb, k_d, A)
            stage_softmax(nc, K, T, A, big)
            stage_sums(nc, K, T, A, v_d, acc)
        stage_dense(nc, K, A_in, acc, h0_d, out)


_INS = ["x", "src", "dst"] + ["L0_gnn_" + n for n in ("w_qkv", "b_qkv", "ln1_g", "ln1_b", "ln2_g", "ln2_b", "w1",
                                                      "b1", "w2", "b2")] \
    + ["L0_ffn_" + n for n in ("gate_w", "gate_b", "W1", "b1", "W2", "b2")]


def kernel(**inputs):
    import numpy as _np
    import concourse.bacc as _bacc
    from concourse import mybir as _mybir
    from concourse.bass_utils import run_bass_kernel_spmd as _run

    nc = _bacc.Bacc("TRN2", target_bir_lowering=False, num_devices=1)
    arrays, args = {}, {}
    for name in _INS:
        a = _np.ascontiguousarray(inputs[name])
        arrays[f"in_{name}_dram"] = a
        args[name] = nc.dram_tensor(f"in_{name}_dram", a.shape, _mybir.dt.from_np(a.dtype), kind="ExternalInput").ap()
    out = nc.dram_tensor("out_dram", (6250, 256), _mybir.dt.float32, kind="ExternalOutput").ap()
    program(nc, args, out)
    r = _run(nc, [arrays], core_ids=[0])
    return r.results[0]["out_dram"]
```

```python
import concourse.bass as bass
from concourse import mybir
from contextlib import ExitStack

F32, I32, BF16 = mybir.dt.float32, mybir.dt.int32, mybir.dt.bfloat16
ALU, ACT, AX = mybir.AluOpType, mybir.ActivationFunctionType, mybir.AxisListType

P = 128
N, E, D, H = 6250, 100000, 256, 8
HD = D // H
DC = D // P
F = 4 * D
NX, FX = 8, 512
EPS = 1e-5
SCALE = D ** -0.5

NT = -(-N // P)
GT = 4
NG = N // (GT * P)
REST = N - NG * GT * P
EP = 125
ET = E // EP
EB = 8
CH = 16
ST = -(-(-(-E // P) + NT) // CH) * CH
SC = ST // CH
CL = SC * P
PAD_KEY = -1
NO_LO = 256.0
LOW = -1e30


class Tally:

    def __init__(self, sem):
        self.sem, self.n, self.k, self.per = sem, 0, None, 0

    def value(self, back=0):
        v = self.n - back
        return v if self.k is None else self.k * self.per + v

    def enter(self, k, per):
        self.k, self.per, self.base = k, per, self.n

    def leave(self, turns):
        assert self.n - self.base == self.per, (self.n - self.base, self.per)
        self.n = self.base + self.per * turns
        self.k = None


def linker(eng, tally):

    def link(ins):
        ins.then_inc(tally.sem, 1)
        tally.n += 1
        eng.wait_ge(tally.sem, tally.value())

    return link


def make_tools(nc):
    ctx, sems = ExitStack(), []

    def clear():
        if sems:
            nc.clear_and_free_semaphores(sems)
            nc.all_engine_barrier()

    ctx.callback(clear)

    def sb(name, shape, dt=F32):
        return ctx.enter_context(nc.sbuf_tensor(name, shape, dt))

    def pb(name, shape=(P, 512), dt=F32):
        return ctx.enter_context(nc.psum_tensor(name, list(shape), dt))

    def sem(name):
        sems.append(nc.alloc_semaphore(name=name))
        return sems[-1]

    return ctx, sb, pb, sem


def stage_constants(nc, K):
    ctx, sb, pb, sem = make_tools(nc)
    with ctx:
        made, ints, cast = sem("made"), sem("ints"), sem("cast")
        with nc.Block() as block:

            @block.gpsimd
            def _(pool):
                pool.memset(K["ident"][:], 0.0).then_inc(made, 1)
                pool.memset(K["lower"][:], 1.0).then_inc(made, 1)
                pool.memset(K["ones"][:], 1.0).then_inc(made, 1)
                pool.iota(K["col_i"][:], [[1, P]], base=0, channel_multiplier=0).then_inc(ints, 1)
                pool.iota(K["part_i"][:], [[0, 1]], base=0, channel_multiplier=1).then_inc(ints, 1)
                pool.wait_ge(made, 3)
                pool.affine_select(out=K["ident"][:], in_=K["ident"][:], compare_op=ALU.not_equal, fill=1.0,
                                   base=0, pattern=[[-1, P]], channel_multiplier=1).then_inc(made, 1)
                pool.affine_select(out=K["upper"][:], in_=K["ones"][:], compare_op=ALU.is_gt, fill=0.0,
                                   base=0, pattern=[[-1, P]], channel_multiplier=1).then_inc(made, 1)
                pool.affine_select(out=K["lower"][:], in_=K["ones"][:], compare_op=ALU.is_gt, fill=0.0,
                                   base=0, pattern=[[1, P]], channel_multiplier=-1).then_inc(made, 1)

            @block.vector
            def _(dve):
                dve.wait_ge(ints, 2)
                dve.tensor_copy(K["col"][:], K["col_i"][:])
                dve.tensor_copy(K["part"][:], K["part_i"][:])
                dve.wait_ge(made, 6)
                dve.tensor_copy(K["ident_b"][:], K["ident"][:])
                dve.tensor_copy(K["ones_b"][:], K["ones"][:]).then_inc(cast, 1)
                dve.wait_ge(cast, 1)


def stage_qkv(nc, K, x, w_qkv, b_qkv, h0_d, k_d, v_d, q_sb):
    ctx, sb, pb, sem = make_tools(nc)
    with ctx:
        w_raw, w = sb("w_raw", [P, DC, 3 * D]), sb("w", [P, DC, 3 * D])
        b_raw, b = sb("b_raw", [P, 3 * D]), sb("b", [P, 3 * D])
        xb, h = sb("xb", [P, 2, GT, D]), sb("h", [P, 2, GT, D])
        hT = sb("hT", [P, 2, DC, GT * P])
        kv = sb("kv", [P, 2, GT, 2 * D])
        stats, mv = sb("stats", [P, 2, GT, 6]), sb("mv", [P, 2, GT, 2])
        std, rstd = sb("std", [P, 2, GT]), sb("rstd", [P, 2, GT])
        eps = sb("eps", [P, 1])
        pT = [[pb(f"pT{a}{c}") for c in range(DC)] for a in range(2)]
        pQK = [pb(f"pQK{a}") for a in range(2)]
        pV = [pb(f"pV{a}") for a in range(2)]
        w_in, w_ready, x_in = sem("w_in"), sem("w_ready"), [sem(f"x_in{a}") for a in range(2)]
        stored = [sem(f"stored{a}") for a in range(2)]
        var_ready, std_ready, h_ready = sem("var_ready"), sem("std_ready"), sem("h_ready")
        hT_psum, hT_ready = sem("hT_psum"), sem("hT_ready")
        qkv_psum, qkv_out, dve_link = sem("qkv_psum"), sem("qkv_out"), sem("qkv_link")
        turns = sem("turns")

        def groups(eng, tallies, body):
            for a in range(2):
                body(0, a, GT, True)
            with eng.Fori(1, NG // 2) as k:
                for t, per in tallies:
                    t.enter(k - 1, per)
                for a in range(2):
                    body(k, a, GT, False)
            for t, per in tallies:
                t.leave(NG // 2 - 1)
            body(NG // 2, 0, 1, False)

        def rows(dram, k, a, nt):
            if nt == 1:
                return dram[NG * GT * P:NG * GT * P + REST, :]
            v = dram[0:NG * GT * P, :].rearrange("(g t p) d -> g p t d", t=GT, p=P)
            return v[k * 2 + a]

        with nc.Block() as block:

            @block.sync
            def _(sp):
                sp.dma_start(w_raw[:], w_qkv.rearrange("(c p) n -> p c n", p=P)).then_inc(w_in, 16)
                sp.dma_start(b_raw[:], b_qkv.unsqueeze(0).to_broadcast([P, 3 * D])).then_inc(w_in, 16)

                def body(k, a, nt, first):
                    if not first:
                        sp.wait_ge(h_ready, k * 2 + a - 1)
                    if nt == 1:
                        sp.dma_start(xb[0:REST, a, 0, :], rows(x, k, a, 1)).then_inc(x_in[a], 16)
                    else:
                        sp.dma_start(xb[:, a], rows(x, k, a, nt)).then_inc(x_in[a], 16)

                groups(sp, [], body)

            @block.gpsimd
            def _(pool):
                def body(k, a, nt, first):
                    pool.wait_ge(h_ready, k * 2 + a + 1)
                    pool.wait_ge(qkv_out, k * 2 * GT + a * GT + nt)
                    pool.sem_inc(turns)
                    if nt == 1:
                        pool.dma_start(rows(h0_d, k, a, 1), h[0:REST, a, 0, :]).then_inc(stored[a], 16)
                        pool.dma_start(rows(k_d, k, a, 1), kv[0:REST, a, 0, 0:D]).then_inc(stored[a], 16)
                        pool.dma_start(rows(v_d, k, a, 1), kv[0:REST, a, 0, D:2 * D]).then_inc(stored[a], 16)
                    else:
                        pool.dma_start(rows(h0_d, k, a, nt), h[:, a]).then_inc(stored[a], 16)
                        pool.dma_start(rows(k_d, k, a, nt), kv[:, a, :, 0:D]).then_inc(stored[a], 16)
                        pool.dma_start(rows(v_d, k, a, nt), kv[:, a, :, D:2 * D]).then_inc(stored[a], 16)

                groups(pool, [], body)
                pool.wait_ge(stored[0], 48 * (NG // 2 + 1))
                pool.wait_ge(stored[1], 48 * (NG // 2))

            @block.vector
            def _(dve):
                link = linker(dve, t := Tally(dve_link))
                dve.memset(eps[:], EPS).then_inc(w_ready, 1)
                dve.wait_ge(w_in, 32)
                for c in range(DC):
                    dve.tensor_copy(w[:, c].rearrange("p (s h e) -> p s h e", s=3, h=H),
                                    w_raw[:, c].rearrange("p (h s e) -> p s h e", s=3, h=H)).then_inc(w_ready, 1)
                link(dve.tensor_copy(b[:].rearrange("p (s h e) -> p s h e", s=3, h=H),
                                     b_raw[:].rearrange("p (h s e) -> p s h e", s=3, h=H)))

                def body(k, a, nt, first):
                    dve.wait_ge(x_in[a], k * 16 + 16)
                    for i in range(nt):
                        ins = dve.bn_stats(stats[:, a, i], xb[:, a, i])
                    link(ins)
                    dve.sem_inc(turns)
                    for i in range(nt):
                        ins = dve.bn_aggr(mv[:, a, i], stats[:, a, i])
                    ins.then_inc(var_ready, 1)
                    dve.wait_ge(std_ready, k * 2 + a + 1)
                    link(dve.reciprocal(rstd[:, a, 0:nt], std[:, a, 0:nt]))
                    if not first:
                        dve.wait_ge(hT_psum, k * 2 + a - 1)
                        dve.wait_ge(stored[a], k * 48)
                    for i in range(nt):
                        ins = dve.tensor_scalar(h[:, a, i], xb[:, a, i], mv[:, a, i, 0:1], rstd[:, a, i:i + 1],
                                                ALU.subtract, ALU.mult)
                    ins.then_inc(h_ready, 1)
                    for i in range(nt):
                        tile = (k * 2 + a) * GT + i
                        dve.wait_ge(qkv_psum, tile + 1)
                        dve.tensor_tensor(q_sb[:, tile], pQK[i % 2][:, 0:D], b[:, 0:D], ALU.add)
                        dve.tensor_tensor(kv[:, a, i, 0:D], pQK[i % 2][:, D:2 * D], b[:, D:2 * D], ALU.add)
                        dve.tensor_tensor(kv[:, a, i, D:2 * D], pV[i % 2][:, 0:D], b[:, 2 * D:3 * D],
                                          ALU.add).then_inc(qkv_out, 1)

                groups(dve, [(t, 4)], body)

            @block.scalar
            def _(act):
                act.wait_ge(w_ready, 1)

                def body(k, a, nt, first):
                    act.wait_ge(var_ready, k * 2 + a + 1)
                    act.activation(std[:, a, 0:nt], mv[:, a, 0:nt, 1], ACT.Sqrt, bias=eps[:]).then_inc(std_ready, 1)
                    act.wait_ge(hT_psum, k * 2 + a + 1)
                    if not first:
                        act.wait_ge(qkv_psum, ((k - 1) * 2 + a + 1) * GT)
                    for c in range(DC):
                        ins = act.copy(hT[:, a, c, 0:nt * P], pT[a][c][:, 0:nt * P])
                    ins.then_inc(hT_ready, 1)

                groups(act, [], body)

            @block.tensor
            def _(pe):
                pe.wait_ge(w_ready, 1 + DC)

                def body(k, a, nt, first):
                    pe.wait_ge(h_ready, k * 2 + a + 1)
                    if not first:
                        pe.wait_ge(hT_ready, k * 2 + a - 1)
                    for c in range(DC):
                        for i in range(nt):
                            ins = pe.transpose(pT[a][c][:, i * P:(i + 1) * P], h[:, a, i, c * P:(c + 1) * P],
                                               K["ident"][:])
                    ins.then_inc(hT_psum, 1)
                    pe.wait_ge(hT_ready, k * 2 + a + 1)
                    for i in range(nt):
                        tile = (k * 2 + a) * GT + i
                        if not (first and a == 0 and i < 2):
                            pe.wait_ge(qkv_out, tile - 1)
                        for c in range(DC):
                            pe.matmul(pQK[i % 2][:], hT[:, a, c, i * P:(i + 1) * P], w[:, c, 0:2 * D],
                                      start=c == 0, stop=c == DC - 1)
                        for c in range(DC):
                            ins = pe.matmul(pV[i % 2][:, 0:D], hT[:, a, c, i * P:(i + 1) * P], w[:, c, 2 * D:3 * D],
                                            start=c == 0, stop=c == DC - 1)
                        ins.then_inc(qkv_psum, 1)

                groups(pe, [], body)


def constants(nc, sb):
    K = {n: sb(f"k_{n}", [P, P]) for n in ("ident", "lower", "upper", "ones", "col")}
    K["part"] = sb("k_part", [P, 1])
    K["col_i"], K["part_i"] = sb("k_col_i", [P, P], I32), sb("k_part_i", [P, 1], I32)
    K["ident_b"], K["ones_b"] = sb("k_ident_b", [P, P], BF16), sb("k_ones_b", [P, P], BF16)
    return K


RING = 4
NB = ET // EB


def sort_steps(eng, tallies, step):
    turns = NB // RING
    for r in range(RING):
        step(0, r, "first")
    with eng.Fori(1, turns - 1) as k:
        for t, per in tallies:
            t.enter(k - 1, per)
        for r in range(RING):
            step(k, r, "middle")
    for t, per in tallies:
        t.leave(turns - 2)
    for r in range(RING):
        step(turns - 1, r, "last")


def stage_sort(nc, K, src, dst, sorted_d, win_d):
    ctx, sb, pb, sem = make_tools(nc)
    with ctx:
        src_i, dst_i = sb("src_i", [EP, ET], I32), sb("dst_i", [EP, ET], I32)
        rec = sb("rec", [EP, ET, 2], I32)
        part_i = sb("part_of_key_i", [EP, 2, ET], I32)
        key_f, lo_f, hi_f = sb("key_f", [EP, ET]), sb("lo_f", [EP, ET]), sb("hi_f", [EP, ET])
        hl_b = sb("hl_b", [EP, ET, 2], BF16)
        ohlo = sb("ohlo", [EP, 2, EB, P], BF16)
        ohhi = sb("ohhi", [EP, RING, EB, NT], BF16)
        Hr = sb("Hr", [P, 2, EB + 1, NT])
        ohtS = sb("ohtS", [P, 2, EB, EP])
        hl_st, rec_st = sb("hl_st", [EP, RING, EB, 2], BF16), sb("rec_st", [EP, RING, EB, 2], I32)
        idx_st = sb("idx_st", [EP, RING, EB], I32)
        rk = sb("rk", [EP, 2, EB])
        same, found = sb("same", [EP, EB, EP], BF16), sb("found", [EP, EB * NT])
        looked, pos = sb("looked", [EP, EB]), sb("pos", [EP, EB])
        pos_i, hi_pos, lo_pos = sb("pos_i", [EP, EB], I32), sb("hi_pos", [EP, EB], I32), sb("lo_pos", [EP, EB], I32)
        cnt, zero_row = sb("cnt", [P, NT]), sb("zero_row", [P, NT])
        tot, nt_i, nt_f = sb("tot", [P, NT], I32), sb("nt_i", [P, NT], I32), sb("nt_f", [P, NT])
        t_end, t_start, excl = sb("t_end", [P, NT]), sb("t_start", [P, NT]), sb("excl", [P, NT])
        WP = 64
        WJ = ST // WP
        tv_i, tv_f = sb("tv_i", [WP, WJ], I32), sb("tv_f", [WP, WJ])
        past, win_f, win_i = sb("past", [WP, WJ, NT]), sb("win_f", [WP, WJ]), sb("win_i", [WP, WJ], I32)
        pads = sb("pads", [P, ST, 2], I32)
        cntp = [pb(f"cntp{a}") for a in range(2)]
        oht = [pb(f"oht{a}") for a in range(2)]
        krow = [pb(f"krow{a}") for a in range(2)]
        lk = [pb(f"lk{a}") for a in range(2)]
        HB = EB // 2

        e_in, rec_made, split = sem("e_in"), sem("rec_made"), sem("split")
        filled, pads_made = sem("filled"), sem("pads_made")
        oh_ready, counted, prefix, tv_made = sem("oh_ready"), sem("counted"), sem("prefix"), sem("tv_made")
        win_ready, win_out, dve_link, oh_used = sem("win_ready"), sem("win_out"), sem("dve_link"), sem("oh_used")
        cnt_ready = sem("cnt_ready")

        def one_hots(dve, t0, a, r):
            dve.tensor_tensor(ohlo[:, a], K["col"][0:EP, :].unsqueeze(1).to_broadcast([EP, EB, P]),
                              lo_f[:, bass.ds(t0, EB)].unsqueeze(2).to_broadcast([EP, EB, P]), ALU.is_equal)
            return dve.tensor_tensor(ohhi[:, r], K["col"][0:EP, 0:NT].unsqueeze(1).to_broadcast([EP, EB, NT]),
                                     hi_f[:, bass.ds(t0, EB)].unsqueeze(2).to_broadcast([EP, EB, NT]),
                                     ALU.is_equal)

        with nc.Block() as block:

            @block.sync
            def _(sp):
                sp.dma_start(src_i[:], src.rearrange("(p t) -> p t", p=EP)).then_inc(e_in, 16)
                sp.dma_start(dst_i[:], dst.rearrange("(p t) -> p t", p=EP)).then_inc(e_in, 16)
                sp.wait_ge(pads_made, 2)
                sp.dma_start(sorted_d.rearrange("(p t) c -> p t c", p=P), pads[:]).then_inc(filled, 16)
                sp.wait_ge(win_ready, 1)
                sp.dma_start(win_d.rearrange("(p j) -> p j", p=WP), win_i[:]).then_inc(win_out, 16)
                sp.wait_ge(filled, 16)
                sp.wait_ge(win_out, 16)

            @block.gpsimd
            def _(pool):
                pool.memset(pads[:, :, 0], PAD_KEY).then_inc(pads_made, 1)
                pool.memset(pads[:, :, 1], 0).then_inc(pads_made, 1)
                pool.iota(tv_i[:], [[1, WJ]], base=0, channel_multiplier=WJ).then_inc(tv_made, 1)
                pool.wait_ge(e_in, 32)
                pool.tensor_copy(rec[:, :, 0], src_i[:]).then_inc(rec_made, 1)
                pool.tensor_copy(rec[:, :, 1], dst_i[:]).then_inc(rec_made, 1)

            @block.vector
            def _(dve):
                link = linker(dve, Tally(dve_link))
                dve.wait_ge(e_in, 32)
                dve.tensor_scalar(part_i[:, 0], src_i[:], P - 1, None, ALU.bitwise_and)
                link(dve.tensor_scalar(part_i[:, 1], src_i[:], 7, None, ALU.logical_shift_right))
                dve.tensor_copy(key_f[:], src_i[:])
                dve.tensor_copy(lo_f[:], part_i[:, 0])
                link(dve.tensor_copy(hi_f[:], part_i[:, 1]))
                dve.tensor_scalar(hl_b[:, :, 0], hi_f[:], float(P), None, ALU.mult)
                link(dve.tensor_copy(hl_b[:, :, 1], lo_f[:]))
                for r in range(2):
                    one_hots(dve, r * EB, r, r).then_inc(oh_ready, 1)
                with dve.Fori(1, NB // 2) as k:
                    for a in range(2):
                        dve.wait_ge(oh_used, k * 2 + a - 1)
                        one_hots(dve, (k * 2 + a) * EB, a, a).then_inc(oh_ready, 1)
                dve.wait_ge(oh_used, NB)
                dve.tensor_copy(cnt[:], cntp[0][:, 0:NT]).then_inc(cnt_ready, 1)
                link(dve.memset(zero_row[:], 0.0))
                dve.wait_ge(prefix, 1)
                dve.tensor_copy(excl[:], lk[0][:, 0:NT])
                link(dve.tensor_scalar(tot[:], lk[1][:, 0:NT], float(P - 1), None, ALU.add))
                link(dve.tensor_scalar(nt_i[:], tot[:], 7, None, ALU.logical_shift_right))
                link(dve.tensor_copy(nt_f[:], nt_i[:]))
                link(dve.tensor_tensor_scan(t_end[:], zero_row[:], nt_f[:], 0.0, ALU.add, ALU.add))
                link(dve.tensor_tensor(t_start[:], t_end[:], nt_f[:], ALU.subtract))
                dve.scalar_tensor_tensor(Hr[:, 0, 0], t_start[:], float(P), excl[:], ALU.mult, ALU.add)
                dve.wait_ge(tv_made, 1)
                link(dve.tensor_copy(tv_f[:], tv_i[:]))
                link(dve.tensor_tensor(past[:], t_end[0:WP].unsqueeze(1).to_broadcast([WP, WJ, NT]),
                                       tv_f[:].unsqueeze(2).to_broadcast([WP, WJ, NT]), ALU.is_le))
                link(dve.tensor_reduce(win_f[:], past[:], AX.X, ALU.add))
                dve.tensor_scalar(win_i[:], win_f[:], float(NT - 1), None, ALU.min).then_inc(win_ready, 1)

            @block.tensor
            def _(pe):
                def batch(k, a, first, last):
                    pe.wait_ge(oh_ready, k * 2 + a + 1)
                    for j in range(EB):
                        ins = pe.matmul(cntp[0][:, 0:NT], ohlo[:, a, j], ohhi[:, a, j],
                                        start=first and a == 0 and j == 0, stop=last and a == 1 and j == EB - 1)
                    ins.then_inc(oh_used, 1)

                for a in range(2):
                    batch(0, a, True, False)
                with pe.Fori(1, NB // 2 - 1) as k:
                    for a in range(2):
                        batch(k, a, False, False)
                for a in range(2):
                    batch(NB // 2 - 1, a, False, True)
                pe.wait_ge(cnt_ready, 1)
                pe.matmul(lk[0][:, 0:NT], K["lower"][:], cnt[:], start=True, stop=True)
                pe.matmul(lk[1][:, 0:NT], K["ones"][:], cnt[:], start=True, stop=True).then_inc(prefix, 1)

        oh_r, hist, krow_ps, krow_used = sem("oh_r"), sem("hist"), sem("krow_ps"), sem("krow_used")
        H_ready, oht_ready, lk_ps, lk_used = sem("H_ready"), sem("oht_ready"), sem("lk_ps"), sem("lk_used")
        hl_ready, rec_ready, idx_ready = sem("hl_ready"), sem("rec_ready"), sem("idx_ready")
        scattered = [sem(f"scattered{r}") for r in range(RING)]
        link2, turns = sem("link2"), sem("sort_turns")
        with nc.Block() as block:

            @block.vector
            def _(dve):
                tally = Tally(link2)
                link = linker(dve, tally)

                def ranks(k, r, kind):
                    a, s = r % 2, k * RING + r
                    dve.wait_ge(krow_ps, s + 1)
                    for j in range(EB):
                        ins = dve.scalar_tensor_tensor(
                            same[:, j], krow[j // HB][0:EP, (j % HB) * EP:(j % HB + 1) * EP],
                            key_f[:, bass.ds(s * EB + j, 1)], K["upper"][0:EP, 0:EP], ALU.is_equal, ALU.mult,
                            accum_out=rk[:, a, j:j + 1])
                    ins.then_inc(krow_used, 1)
                    dve.wait_ge(hist, s + 1)
                    if kind != "first" or r >= 1:
                        dve.wait_ge(lk_ps, s)
                    for j in range(EB):
                        to = Hr[:, a, j + 1] if j < EB - 1 else Hr[:, 1 - a, 0]
                        ins = dve.tensor_tensor(to, Hr[:, a, j], cntp[a][:, j * NT:(j + 1) * NT], ALU.add)
                        if j < EB - 1:
                            link(ins)
                    ins.then_inc(H_ready, 1)
                    dve.wait_ge(H_ready, s + 1)

                def places(k, r, kind):
                    a, s = r % 2, k * RING + r
                    dve.wait_ge(lk_ps, s + 1)
                    link(dve.tensor_tensor(found[:], lk[a][0:EP, 0:EB * NT],
                                           ohhi[:, r].rearrange("p j n -> p (j n)"), ALU.mult))
                    link(dve.tensor_reduce(looked[:], found[:].rearrange("p (j n) -> p j n", j=EB), AX.X, ALU.add))
                    link(dve.tensor_tensor(pos_i[:], looked[:], rk[:, a], ALU.add))
                    dve.tensor_scalar(lo_pos[:], pos_i[:], P - 1, None, ALU.bitwise_and)
                    link(dve.tensor_scalar(hi_pos[:], pos_i[:], 7, None, ALU.logical_shift_right))
                    if kind != "first":
                        dve.wait_ge(scattered[r], k * EB * 16)
                    dve.scalar_tensor_tensor(idx_st[:, r], lo_pos[:], float(ST), hi_pos[:], ALU.mult,
                                             ALU.add).then_inc(idx_ready, 1)
                    dve.wait_ge(idx_ready, s + 1)

                per = (EB - 1 + 4) * RING

                def turn(k, kind, back_kind):
                    for r in range(RING):
                        s = k * RING + r
                        if not (kind == "last" and r == RING - 1):
                            if kind != "first" or r >= 1:
                                dve.wait_ge(hist, s)
                            one_hots(dve, (s + 1) * EB, (r + 1) % 2, (r + 1) % RING).then_inc(oh_r, 1)
                        ranks(k, r, kind)
                        if r > 0:
                            places(k, r - 1, kind)
                        elif back_kind:
                            places(k - 1, RING - 1, back_kind)

                one_hots(dve, 0, 0, 0).then_inc(oh_r, 1)
                turn(0, "first", None)
                turn(1, "middle", "first")
                with dve.Fori(2, NB // RING - 1) as k:
                    tally.enter(k - 2, per)
                    turn(k, "middle", "middle")
                tally.leave(NB // RING - 3)
                turn(NB // RING - 1, "last", "middle")
                places(NB // RING - 1, RING - 1, "last")

            @block.tensor
            def _(pe):
                def count(k, r, kind):
                    a, s = r % 2, k * RING + r
                    pe.wait_ge(oh_r, s + 1)
                    if kind != "first" or r >= 2:
                        pe.wait_ge(H_ready, s - 1)
                    if kind != "first" or r >= 1:
                        pe.wait_ge(oht_ready, s)
                    for j in range(EB):
                        pe.matmul(cntp[a][:, j * NT:(j + 1) * NT], ohlo[:, a, j], ohhi[:, r, j], start=True, stop=True)
                        ins = pe.matmul(oht[j // HB][:, (j % HB) * EP:(j % HB + 1) * EP], ohlo[:, a, j],
                                        K["ident_b"][0:EP, 0:EP], start=True, stop=True)
                    ins.then_inc(hist, 1)
                    pe.wait_ge(hl_ready, s + 1)
                    if kind != "first" or r >= 1:
                        pe.wait_ge(krow_used, s)
                    for j in range(EB):
                        for c in range(2):
                            ins = pe.matmul(krow[j // HB][0:EP, (j % HB) * EP:(j % HB + 1) * EP],
                                            hl_st[:, r, j, c:c + 1].to_broadcast([EP, EP]),
                                            K["ident_b"][0:EP, 0:EP], start=c == 0, stop=c == 1)
                    ins.then_inc(krow_ps, 1)

                def look_up(k, r, kind):
                    a, s = r % 2, k * RING + r
                    pe.wait_ge(H_ready, s + 1)
                    pe.wait_ge(oht_ready, s + 1)
                    if kind != "first" or r >= 2:
                        pe.wait_ge(idx_ready, s - 1)
                    for j in range(EB):
                        ins = pe.matmul(lk[a][0:EP, j * NT:(j + 1) * NT], ohtS[:, a, j], Hr[:, a, j],
                                        start=True, stop=True)
                    ins.then_inc(lk_ps, 1)

                def step(k, r, kind):
                    if r < RING - 1:
                        count(k, r + 1, kind)
                    elif kind != "last":
                        count(k + 1, 0, "middle")
                    look_up(k, r, kind)

                count(0, 0, "first")
                sort_steps(pe, [], step)

            @block.scalar
            def _(act):
                def stage_keys(k, r, kind):
                    s = k * RING + r
                    if kind != "first":
                        act.wait_ge(krow_ps, s - RING + 1)
                    act.copy(hl_st[:, r], hl_b[:, bass.ds(s * EB, EB), :]).then_inc(hl_ready, 1)

                def step(k, r, kind):
                    s, a = k * RING + r, r % 2
                    if r < RING - 1:
                        stage_keys(k, r + 1, kind)
                    elif kind != "last":
                        stage_keys(k + 1, 0, "middle")
                    act.wait_ge(hist, s + 1)
                    if kind != "first" or r >= 2:
                        act.wait_ge(lk_ps, s - 1)
                    for b in range(2):
                        ins = act.copy(ohtS[:, a, b * HB:(b + 1) * HB].rearrange("p j e -> p (j e)"),
                                       oht[b][:, 0:HB * EP])
                    ins.then_inc(oht_ready, 1)
                    if kind != "first":
                        act.wait_ge(scattered[r], k * EB * 16)
                    act.copy(rec_st[:, r], rec[:, bass.ds(s * EB, EB), :]).then_inc(rec_ready, 1)

                stage_keys(0, 0, "first")
                sort_steps(act, [], step)

            @block.gpsimd
            def _(pool):
                def step(k, r, kind):
                    s = k * RING + r
                    pool.wait_ge(rec_ready, s + 1)
                    pool.wait_ge(idx_ready, s + 1)
                    pool.sem_inc(turns)
                    for j in range(EB):
                        pool.indirect_dma_start(sorted_d, bass.IndirectOffsetOnAxis(idx_st[:, r, j:j + 1], 0),
                                                rec_st[:, r, j, :], None).then_inc(scattered[r], 16)

                sort_steps(pool, [], step)
                for r in range(RING):
                    pool.wait_ge(scattered[r], 16 * ET // RING)


GB = 4
GR = 4
GN = ST // (GB * GR)


def gather_steps(eng, tallies, step):
    for r in range(GR):
        step(Batch(0, r))
    with eng.Fori(1, GN - 1) as k:
        for t, per in tallies:
            t.enter(k - 1, per)
        for r in range(GR):
            step(Batch(k, r))
    for t, per in tallies:
        t.leave(GN - 2)
    for r in range(GR):
        step(Batch(GN - 1, r))


def windows(nc, engine, table, x):
    _, w = nc.values_load_multi_w_load_instructions(
        table[0:1, bass.ds(x.b * GB, GB)], engines=(engine,), min_val=0, max_val=NT - 1,
        skip_runtime_bounds_check_because="a window's number is below NT as it is made")
    return w


class Batch:

    def __init__(self, k, r):
        self.k, self.r, self.a = k + r // GR, r % GR, r % 2
        self.b = self.k * GR + self.r

    def after(self, d):
        x = Batch(self.k, self.r + d)
        return None if isinstance(x.b, int) and x.b >= GN * GR else x

    def early(self, n):
        return isinstance(self.b, int) and self.b < n


def across(table):
    return table.rearrange("p (g c) -> p c g", c=CH)


def stage_tables(nc, sorted_d, win_d, T):
    ctx, sb, pb, sem = make_tools(nc)
    with ctx:
        rec, low_i = sb("rec_s", [P, ST, 2], I32), sb("low_i", [P, ST], I32)
        pad, win_all = sb("pad", [P, ST]), sb("win_all", [P, ST], I32)
        t_in, dve_link = sem("t_in"), sem("t_link")
        with nc.Block() as block:

            @block.sync
            def _(sp):
                sp.dma_start(rec[:], sorted_d.rearrange("(p t) c -> p t c", p=P)).then_inc(t_in, 16)
                sp.dma_start(T["win"][:], win_d.unsqueeze(0)).then_inc(t_in, 16)
                sp.dma_start(win_all[:], win_d.unsqueeze(0).to_broadcast([P, ST])).then_inc(t_in, 16)

            @block.vector
            def _(dve):
                link = linker(dve, Tally(dve_link))
                dve.wait_ge(t_in, 48)
                dve.memset(T["keep"][:, 0:1], 0.0)
                dve.tensor_tensor(T["keep"][:, 1:ST], win_all[:, 1:ST], win_all[:, 0:ST - 1], ALU.is_equal)
                dve.tensor_copy(T["key"][:], rec[:, :, 0])
                dve.tensor_copy(T["dst"][:], rec[:, :, 1])
                dve.tensor_copy(across(T["win_x"][:]), T["win"][:].rearrange("p (c g) -> p c g", c=CH))
                link(dve.tensor_scalar(low_i[:], rec[:, :, 0], P - 1, None, ALU.bitwise_and))
                link(dve.tensor_copy(T["lo"][:], low_i[:]))
                link(dve.tensor_scalar(pad[:], T["key"][:], 0.0, NO_LO - (P - 1), ALU.is_lt, ALU.mult))
                link(dve.tensor_tensor(T["lo"][:], T["lo"][:], pad[:], ALU.add))
                for name in ("key", "dst", "lo"):
                    ins = dve.tensor_copy(across(T[name + "_x"][:]), T[name][:].rearrange("p (c g) -> p c g", c=CH))
                link(ins)


def gathers(nc, pool, table, got, idx_st, idx_ready, free, arrived, turns):

    def step(x):
        pool.wait_ge(idx_ready, x.b + 1)
        if not x.early(GR):
            pool.wait_ge(free, x.b - GR + 1)
        pool.sem_inc(turns)
        for j in range(GB):
            pool.indirect_dma_start(got[:, x.r, j, :], None, table,
                                    bass.IndirectOffsetOnAxis(idx_st[:, x.r, j:j + 1], 0)).then_inc(arrived[x.r], 16)

    gather_steps(pool, [], step)
    for r in range(GR):
        pool.wait_ge(arrived[r], 16 * GB * GN)


def stage_scores(nc, K, T, q_sb, k_d, A):
    ctx, sb, pb, sem = make_tools(nc)
    with ctx:
        kg = sb("kg", [P, GR, GB, D])
        idx_st, lo_st = sb("idx_g", [P, GR, GB], I32), sb("lo_st", [P, GR, GB], BF16)
        spread = sb("spread", [P, 2, GB, P])
        prod = sb("prod", [P, 2, GB, D])
        p_lo = [pb(f"p_lo{a}") for a in range(2)]
        p_q = [pb(f"p_q{a}", [P, GB * D]) for a in range(2)]
        idx_ready, arrived, k_used = sem("idx_g_ready"), [sem(f"k_in{r}") for r in range(GR)], sem("k_used")
        lo_ready, lo_psum, spread_ready, q_psum = sem("lo_ready"), sem("lo_psum"), sem("spread_ready"), sem("q_psum")
        summed, turns = sem("summed"), sem("g_turns")

        with nc.Block() as block:

            @block.gpsimd
            def _(pool):
                gathers(nc, pool, k_d, kg, idx_st, idx_ready, k_used, arrived, turns)

            @block.scalar
            def _(act):
                def step(x):
                    if not x.early(GR):
                        act.wait_ge(arrived[x.r], x.k * GB * 16)
                        act.wait_ge(lo_psum, x.b - GR + 1)
                    act.copy(lo_st[:, x.r], T["lo_x"][:, bass.ds(x.b * GB, GB)]).then_inc(lo_ready, 1)
                    act.copy(idx_st[:, x.r], T["dst_x"][:, bass.ds(x.b * GB, GB)]).then_inc(idx_ready, 1)

                gather_steps(act, [], step)

            @block.tensor
            def _(pe):
                def rows(x):
                    pe.wait_ge(lo_ready, x.b + 1)
                    if not x.early(2):
                        pe.wait_ge(spread_ready, x.b - 1)
                    for j in range(GB):
                        ins = pe.matmul(p_lo[x.a][:, j * P:(j + 1) * P], lo_st[:, x.r, j:j + 1].to_broadcast([P, P]),
                                        K["ident_b"][:], start=True, stop=True)
                    ins.then_inc(lo_psum, 1)

                def spreads(x):
                    pe.wait_ge(spread_ready, x.b + 1)
                    if not x.early(2):
                        pe.wait_ge(k_used, x.b - 1)
                    ws = windows(nc, mybir.EngineType.PE, T["win_x"], x)
                    for j, w in enumerate(ws):
                        ins = pe.matmul(p_q[x.a][:, j * D:(j + 1) * D], spread[:, x.a, j],
                                        q_sb[:, bass.ds(w, 1), :].rearrange("p o d -> p (o d)"),
                                        start=True, stop=True)
                    ins.then_inc(q_psum, 1)

                def step(x):
                    if x.after(2):
                        rows(x.after(2))
                    if x.after(1):
                        spreads(x.after(1))

                rows(Batch(0, 0))
                rows(Batch(0, 1))
                spreads(Batch(0, 0))
                gather_steps(pe, [], step)

            @block.vector
            def _(dve):
                def one_hot(x):
                    dve.wait_ge(lo_psum, x.b + 1)
                    if not x.early(2):
                        dve.wait_ge(q_psum, x.b - 1)
                    dve.tensor_scalar(spread[:, x.a].rearrange("p j e -> p (j e)"), p_lo[x.a][:], K["part"][:, 0:1],
                                      None, ALU.is_equal).then_inc(spread_ready, 1)

                def step(x):
                    if x.after(1):
                        one_hot(x.after(1))
                    dve.wait_ge(q_psum, x.b + 1)
                    dve.wait_ge(arrived[x.r], (x.k + 1) * GB * 16)
                    dve.tensor_tensor(prod[:, x.a].rearrange("p j d -> p (j d)"), p_q[x.a][:],
                                      kg[:, x.r].rearrange("p j d -> p (j d)"), ALU.mult).then_inc(k_used, 1)
                    dve.wait_ge(k_used, x.b + 1)
                    dve.tensor_reduce(A[:, bass.ds(x.b * GB, GB), :],
                                      prod[:, x.a].rearrange("p j (h e) -> p j h e", h=H), AX.X,
                                      ALU.add).then_inc(summed, 1)

                one_hot(Batch(0, 0))
                gather_steps(dve, [], step)
                dve.wait_ge(summed, GR * GN)


def stage_softmax(nc, K, T, A, big):
    ctx, sb, pb, sem = make_tools(nc)
    with ctx:
        aT, kT = big[:, 0:CL], sb("kT", [P, CL])
        cut = big[:, CL:2 * CL + 1]
        fwd, top = sb("fwd", [P, CL]), sb("top", [P, CL])
        rows = sb("rows", [1, 4, H, CH])
        cont, whole = sb("cont", [1, H, CH + 1]), sb("whole", [1, H, CH])
        gate, end = sb("gate", [1, 2, H, CH]), sb("end", [1, 2, H, CH])
        carry, carry_ch = sb("carry", [1, 2, H, CH]), sb("carry_ch", [1, 2, CH * H])
        carry_c = sb("carry_c", [P, 2])
        key8 = top[:].rearrange("p (g x) -> p g x", g=SC)
        pt = [pb(f"pt{i}") for i in range(4)]
        pr, pc = pb("pr"), pb("pc")
        t_psum, t_out, link_s = sem("t_psum"), sem("t_out"), sem("link_s")
        k_psum, k_out, rows_psum, rows_ready, edges_ready = (sem("k_psum"), sem("k_out"), sem("rows_psum"),
                                                             sem("rows_ready"), sem("edges_ready"))
        carry_psum, diff_ready, exp_ready = sem("carry_psum"), sem("diff_ready"), sem("exp_ready")
        b_psum, b_out, key8_ready = sem("b_psum"), sem("b_out"), sem("key8_ready")
        A4 = A[:].rearrange("p (c g) h -> p c g h", c=CH)
        Ax = A[:].rearrange("p (g c) h -> p g (c h)", c=CH)
        Q = 4
        QN = SC // Q
        W = Q * P

        with nc.Block() as block:

            @block.tensor
            def _(pe):
                pe.wait_ge(key8_ready, 1)
                for i in range(QN):
                    if i >= 2:
                        pe.wait_ge(t_out, i - 1)
                    for g in range(Q):
                        ins = pe.transpose(pt[i % 2][:, g * P:(g + 1) * P], Ax[:, i * Q + g, :], K["ident"][:])
                    ins.then_inc(t_psum, 1)
                    if i >= 2:
                        pe.wait_ge(k_out, i - 1)
                    for g in range(Q):
                        ins = pe.transpose(pt[2 + i % 2][:, g * P:(g + 1) * P],
                                           key8[:, i * Q + g, :], K["ident"][:])
                    ins.then_inc(k_psum, 1)
                pe.wait_ge(edges_ready, 1)
                for i, col in enumerate((fwd[:, CL - 1:CL], top[:, 0:1], kT[:, 0:1], kT[:, CL - 1:CL])):
                    ins = pe.matmul(pr[0:1, i * P:(i + 1) * P], col, K["ident"][:], start=True, stop=True)
                ins.then_inc(rows_psum, 1)
                pe.wait_ge(rows_ready, 1)
                for i in range(2):
                    ins = pe.matmul(pc[:, i:i + 1], carry_ch[0:1, i, :], K["ones"][0:1, 0:1], start=True, stop=True)
                ins.then_inc(carry_psum, 1)
                for i in range(QN):
                    pe.wait_ge(exp_ready, i + 1)
                    if i >= 4:
                        pe.wait_ge(b_out, i - 3)
                    for g in range(Q):
                        ins = pe.transpose(pt[i % 4][:, g * P:(g + 1) * P], aT[:, (i * Q + g) * P:(i * Q + g + 1) * P],
                                           K["ident"][:])
                    ins.then_inc(b_psum, 1)

            @block.scalar
            def _(act):
                for i in range(QN):
                    act.wait_ge(t_psum, i + 1)
                    act.copy(aT[:, i * W:(i + 1) * W], pt[i % 2][:]).then_inc(t_out, 1)
                for i in range(QN):
                    act.wait_ge(diff_ready, i + 1)
                    act.activation(aT[:, i * W:(i + 1) * W], fwd[:, i * W:(i + 1) * W], ACT.Exp,
                                   scale=SCALE).then_inc(exp_ready, 1)

            @block.vector
            def _(dve):
                link = linker(dve, Tally(link_s))
                dve.tensor_copy(top[:].rearrange("p (t h) -> p t h", h=H),
                                T["key_x"][:].unsqueeze(2).to_broadcast([P, ST, H])).then_inc(key8_ready, 1)
                for i in range(QN):
                    dve.wait_ge(k_psum, i + 1)
                    dve.tensor_copy(kT[:, i * W:(i + 1) * W], pt[2 + i % 2][:]).then_inc(k_out, 1)
                dve.wait_ge(k_out, QN)
                dve.memset(cut[:, 0:1], 0.0)
                dve.memset(cut[:, CL:CL + 1], 0.0)
                link(dve.tensor_tensor(cut[:, 1:CL], kT[:, 1:CL], kT[:, 0:CL - 1], ALU.not_equal))
                link(dve.tensor_scalar(cut[:, 1:CL], cut[:, 1:CL], LOW, None, ALU.mult))
                dve.wait_ge(t_out, QN)
                dve.tensor_tensor_scan(fwd[:], cut[:, 0:CL], aT[:], LOW, ALU.add, ALU.max)
                dve.tensor_tensor_scan(top[:, ::-1], cut[:, 1:CL + 1][:, ::-1], aT[:, ::-1], LOW, ALU.add,
                                       ALU.max).then_inc(edges_ready, 1)
                dve.wait_ge(rows_psum, 1)
                link(dve.tensor_copy(rows[:], pr[0:1, 0:4 * P].rearrange("o (r c h) -> o r h c", r=4, h=H)))
                link(dve.memset(cont[:], 0.0))
                dve.tensor_tensor(cont[:, :, 1:CH], rows[:, 2, :, 1:CH], rows[:, 3, :, 0:CH - 1], ALU.is_equal)
                link(dve.tensor_tensor(whole[:], rows[:, 2], rows[:, 3], ALU.is_equal))
                dve.tensor_tensor(gate[:, 0], whole[:], cont[:, :, 0:CH], ALU.mult)
                link(dve.tensor_tensor(gate[:, 1], whole[:], cont[:, :, 1:CH + 1], ALU.mult))
                link(dve.tensor_scalar(gate[:], gate[:], 1.0, -LOW, ALU.subtract, ALU.mult))
                flat = [x.rearrange("o h c -> o (h c)") for x in
                        (gate[:, 0], rows[:, 0], end[:, 0], gate[:, 1], rows[:, 1], end[:, 1])]
                dve.tensor_tensor_scan(flat[2], flat[0], flat[1], LOW, ALU.add, ALU.max)
                link(dve.tensor_tensor_scan(flat[5][:, ::-1], flat[3][:, ::-1], flat[4][:, ::-1], LOW, ALU.add,
                                            ALU.max))
                link(dve.tensor_scalar(cont[:], cont[:], 1.0, -LOW, ALU.subtract, ALU.mult))
                dve.memset(carry[:, 0, :, 0:1], LOW)
                dve.memset(carry[:, 1, :, CH - 1:CH], LOW)
                dve.tensor_tensor(carry[:, 0, :, 1:CH], end[:, 0, :, 0:CH - 1], cont[:, :, 1:CH], ALU.add)
                link(dve.tensor_tensor(carry[:, 1, :, 0:CH - 1], end[:, 1, :, 1:CH], cont[:, :, 1:CH], ALU.add))
                dve.tensor_copy(carry_ch[:].rearrange("o r (c h) -> o r h c", h=H), carry[:]).then_inc(rows_ready, 1)
                dve.wait_ge(carry_psum, 1)
                link(dve.tensor_copy(carry_c[:], pc[:, 0:2]))
                link(dve.tensor_tensor_scan(fwd[:], cut[:, 0:CL], aT[:], carry_c[:, 0:1], ALU.add, ALU.max))
                link(dve.tensor_tensor_scan(top[:, ::-1], cut[:, 1:CL + 1][:, ::-1], fwd[:, ::-1], carry_c[:, 1:2],
                                            ALU.add, ALU.max))
                for i in range(QN):
                    s = slice(i * W, (i + 1) * W)
                    dve.tensor_tensor(fwd[:, s], aT[:, s], top[:, s], ALU.subtract).then_inc(diff_ready, 1)
                for i in range(QN):
                    dve.wait_ge(b_psum, i + 1)
                    dve.tensor_copy(A4[:, :, i * Q:(i + 1) * Q, :].rearrange("p c g h -> p g c h"),
                                    pt[i % 4][:].rearrange("p (g c h) -> p g c h", g=Q, h=H)).then_inc(b_out, 1)
                dve.wait_ge(b_out, QN)


def stage_sums(nc, K, T, A, v_d, acc):
    DX = D + H
    ctx, sb, pb, sem = make_tools(nc)
    with ctx:
        vg = sb("vg", [P, GR, GB, D])
        idx_st = sb("idx_v", [P, GR, GB], I32)
        pick = sb("pick", [P, 2, GB, P])
        wv = sb("wv", [P, 2, GB, DX])
        run = sb("run", [P, 2, GB, DX])
        p_s = [[pb(f"p_s{a}{j}") for j in range(GB)] for a in range(2)]
        idx_ready, arrived, v_used = sem("idx_v_ready"), [sem(f"v_in{r}") for r in range(GR)], sem("v_used")
        kept = sem("kept")
        w_ready, s_psum, added, cleared, turns = (sem("wcol_ready"), sem("s_psum"), sem("added"), sem("cleared"),
                                                  sem("v_turns"))
        with nc.Block() as block:

            @block.gpsimd
            def _(pool):
                gathers(nc, pool, v_d, vg, idx_st, idx_ready, v_used, arrived, turns)

            @block.scalar
            def _(act):
                def targets(x):
                    if not x.early(GR):
                        act.wait_ge(arrived[x.r], x.k * GB * 16)
                    act.copy(idx_st[:, x.r], T["dst"][:, bass.ds(x.b * GB, GB)]).then_inc(idx_ready, 1)

                def weights(x):
                    if not x.early(2):
                        act.wait_ge(s_psum, x.b - 1)
                    act.copy(wv[:, x.a, :, D:DX], A[:, bass.ds(x.b * GB, GB), :]).then_inc(w_ready, 1)

                def step(x):
                    if x.after(GR - 1):
                        targets(x.after(GR - 1))
                    if x.after(1):
                        weights(x.after(1))
                    if not x.early(1):
                        place(x.after(-1))

                def place(x):
                    ws = windows(nc, mybir.EngineType.Activation, T["win"], x)
                    for j, w in enumerate(ws):
                        act.wait_ge(added, x.b * GB + j + 1)
                        if j == 0 and not x.early(1):
                            act.wait_ge(kept, x.b * GB)
                        elif j:
                            act.wait_ge(kept, x.b * GB + j)
                        act.copy(acc[:, bass.ds(w, 1), :].rearrange("p o d -> p (o d)"), run[:, x.a, j]).then_inc(kept, 1)

                for i in range(GR - 1):
                    targets(Batch(0, i))
                weights(Batch(0, 0))
                act.wait_ge(cleared, 2)
                gather_steps(act, [], step)
                place(Batch(GN - 1, GR - 1))
                act.wait_ge(kept, ST)

            @block.tensor
            def _(pe):
                def step(x):
                    pe.wait_ge(w_ready, x.b + 1)
                    pe.wait_ge(v_used, x.b + 1)
                    if not x.early(2):
                        pe.wait_ge(added, (x.b - 1) * GB)
                    for j in range(GB):
                        ins = pe.matmul(p_s[x.a][j][:, 0:DX], pick[:, x.a, j], wv[:, x.a, j], start=True, stop=True)
                    ins.then_inc(s_psum, 1)

                gather_steps(pe, [], step)

            @block.vector
            def _(dve):
                def weigh(x):
                    if not x.early(2):
                        dve.wait_ge(s_psum, x.b - 1)
                    dve.tensor_tensor(pick[:, x.a], K["col"][:].unsqueeze(1).to_broadcast([P, GB, P]),
                                      T["lo"][:, bass.ds(x.b * GB, GB)].unsqueeze(2).to_broadcast([P, GB, P]),
                                      ALU.is_equal)
                    dve.wait_ge(arrived[x.r], (x.k + 1) * GB * 16)
                    dve.tensor_tensor(wv[:, x.a, :, 0:D].rearrange("p j (h e) -> p j h e", h=H),
                                      vg[:, x.r].rearrange("p j (h e) -> p j h e", h=H),
                                      A[:, bass.ds(x.b * GB, GB), :].unsqueeze(3).to_broadcast([P, GB, H, HD]),
                                      ALU.mult).then_inc(v_used, 1)

                def add(x):
                    dve.wait_ge(s_psum, x.b + 1)
                    if not x.early(2):
                        dve.wait_ge(kept, (x.b - 1) * GB)
                    for j in range(GB):
                        last = run[:, x.a, j - 1] if j else run[:, 1 - x.a, GB - 1]
                        dve.scalar_tensor_tensor(run[:, x.a, j], last, T["keep"][:, bass.ds(x.b * GB + j, 1)],
                                                 p_s[x.a][j][:, 0:DX], ALU.mult, ALU.add).then_inc(added, 1)
                        dve.wait_ge(added, x.b * GB + j + 1)

                def step(x):
                    if x.after(1):
                        weigh(x.after(1))
                    add(x)

                dve.memset(run[:], 0.0).then_inc(cleared, 1)
                dve.memset(acc[:], 0.0).then_inc(cleared, 1)
                dve.wait_ge(cleared, 2)
                weigh(Batch(0, 0))
                gather_steps(dve, [], step)


NP = NT * P
XT = -(-2 * N // P) + NX
XG = 8
XR = NX * NP + XT * P


def stage_front(nc, K, A_in, acc, h0_d, n_d, ids_d, R):
    FB = F // P
    G = GT * P
    ctx, sb, pb, sem = make_tools(nc)
    with ctx:
        w1, w2 = sb("w1", [P, DC, F]), sb("w2", [P, FB, D])
        gw, gb = sb("gw", [P, DC, NX]), sb("gb", [P, NX])
        b1c = sb("b1c", [P, FB])
        vec = sb("vec", [P, 5, D])
        xin, hin = sb("xin", [P, 2, GT, D]), sb("hin", [P, GT, D])
        y1 = sb("y1", [P, 2, GT, D])
        y1T, nT = sb("y1T", [P, DC, G]), sb("nT", [P, DC, G])
        h1T = sb("h1T", [P, FB, G])
        rden = sb("rden", [P, GT, H])
        stats, mv, std, rstd = sb("d_stats", [P, GT, 6]), sb("d_mv", [P, GT, 2]), sb("d_std", [P, GT]), sb("d_rstd", [P, GT])
        eps = sb("d_eps", [P, 1])
        lg, ex, pr = sb("lg", [P, GT, NX]), sb("ex", [P, GT, NX]), sb("pr_x", [P, GT, NX])
        top, tot = sb("top_x", [P, GT]), sb("tot_x", [P, GT])
        more, equal, rank = sb("more", [P, GT, NX, NX]), sb("equal", [P, GT, NX, NX]), sb("rank", [P, GT, NX])
        before = sb("before", [P, NX, NX])
        sel, both = sb("sel", [P, 2, GT, NX]), sb("both", [P, GT, NX])
        spot, mine = sb("spot", [P, GT, NX]), sb("mine", [P, GT, NX])
        slot_f = sb("slot_f", [P, GT])
        slot_st, id_st = sb("slot_st", [P, 2, GT, 2], I32), sb("id_st", [P, 2, GT], I32)
        ids, zeros = sb("ids", [P, NT], I32), sb("zeros_i", [P, XR // P], I32)
        room_i = sb("room_i", [P, NX], I32)
        p_up = [pb(f"p_up{i}") for i in range(2)]
        p_dn = pb("p_dn", [P, GT * D])
        p_t = [pb(f"p_t{i}") for i in range(DC)]
        p_g, p_r = pb("p_g"), pb("p_r")

        w_in, consts, iotas, cleared = sem("dw_in"), sem("dconsts"), sem("iotas"), sem("ids_cleared")
        x_in, h_in = [sem(f"fx_in{a}") for a in range(2)], sem("fh_in")
        var_r, std_r = [sem(f"var{i}") for i in range(3)], [sem(f"std{i}") for i in range(3)]
        h_used, y1_r, dn_used, x_used, n_r = sem("h_used"), sem("y1_r"), sem("dn_used"), sem("x_used"), sem("n_r")
        t_ps, t_out = [sem(f"dt_ps{i}") for i in range(2)], [sem(f"dt_out{i}") for i in range(2)]
        up_ps, up_out, dn_ps = sem("up_ps"), sem("up_out"), sem("dn_ps")
        lg_ps, lg_r, ex_r, sel_r, rk_ps, rk_used = (sem("lg_ps"), sem("lg_r"), sem("ex_r"), sem("sel_r"), sem("rk_ps"),
                                                    sem("rk_used"))
        slots_r, ids_r, listed, stored = (sem("slots_r"), sem("ids_r"), [sem(f"listed{a}") for a in range(2)],
                                          [sem(f"n_stored{a}") for a in range(2)])
        dl, turns = sem("dl"), sem("d_turns")

        class At:

            def __init__(self, k, a):
                self.k, self.a = k + a // 2, a % 2
                self.g = self.k * 2 + self.a
                self.known = isinstance(self.g, int)
                self.nt = 1 if self.known and self.g == NG else GT
                self.n = self.nt * P

            def step(self, d):
                x = At(self.k, self.a + d)
                return None if x.known and not 0 <= x.g <= NG else x

            def early(self, n):
                return self.known and self.g < n

        def run(eng, tallies, begin, turn, end):
            begin(At(0, 0))
            turn(At(0, 0))
            turn(At(0, 1))
            last = NG // 2 - 1
            with eng.Fori(1, last) as k:
                for t, per in tallies:
                    t.enter(k - 1, per)
                turn(At(k, 0))
                turn(At(k, 1))
            for t, per in tallies:
                t.leave(last - 1)
            for a in range(3):
                turn(At(last, a))
            end(At(last, 2))

        def rows(dram, q):
            if q.nt == 1:
                return dram[NG * G:NG * G + REST, :]
            return dram[0:NG * G, :].rearrange("(g t p) d -> g p t d", t=GT, p=P)[q.g]

        def part(q, buf):
            return buf[0:REST, 0, :] if q.nt == 1 else buf

        with nc.Block() as block:

            @block.sync
            def _(sp):
                def col(v):
                    return v.rearrange("(b p) -> p b", p=P)

                def row(v):
                    return v.unsqueeze(0).to_broadcast([P, v.shape[0]])

                def load_h(q):
                    if not q.early(1):
                        sp.wait_ge(h_used, q.g)
                        sp.sem_inc(turns)
                    sp.dma_start(part(q, hin[:]), rows(h0_d, q)).then_inc(h_in, 16)

                def load_x(q):
                    if not q.early(2):
                        sp.wait_ge(x_used, q.g - 1)
                        sp.sem_inc(turns)
                    sp.dma_start(part(q, xin[:, q.a]), rows(A_in["x"], q)).then_inc(x_in[q.a], 16)

                def store(q):
                    sp.wait_ge(n_r, q.g + 1)
                    sp.sem_inc(turns)
                    sp.dma_start(rows(n_d, q), part(q, y1[:, q.a])).then_inc(stored[q.a], 16)

                def begin(q):
                    load_h(q)
                    for i, name in enumerate(("ln1_g", "ln1_b", "ln2_g", "ln2_b", "b2")):
                        sp.dma_start(vec[:, i], row(A_in["L0_gnn_" + name])).then_inc(w_in, 16)
                    sp.dma_start(w1[:], A_in["L0_gnn_w1"].rearrange("(c p) f -> p c f", p=P)).then_inc(w_in, 16)
                    sp.dma_start(w2[:], A_in["L0_gnn_w2"].rearrange("(c p) f -> p c f", p=P)).then_inc(w_in, 16)
                    sp.dma_start(gw[:], A_in["L0_ffn_gate_w"].rearrange("(c p) f -> p c f", p=P)).then_inc(w_in, 16)
                    sp.dma_start(gb[:], row(A_in["L0_ffn_gate_b"])).then_inc(w_in, 16)
                    with nc.allow_non_contiguous_dma(reason="biases by partition, once"):
                        sp.dma_start(b1c[:], col(A_in["L0_gnn_b1"])).then_inc(w_in, 16)
                    sp.wait_ge(iotas, 2)
                    sp.dma_start(ids_d.rearrange("(p r) o -> p (r o)", p=P), zeros[:]).then_inc(cleared, 16)
                    load_x(q)
                    for e in range(NX):
                        sp.dma_start(R["w1"][:, e], A_in["L0_ffn_W1"][e].rearrange("(c p) f -> p c f", p=P)).then_inc(R["in"], 16)
                        sp.dma_start(R["w2"][:, e], A_in["L0_ffn_W2"][e].rearrange("(c p) f -> p c f", p=P)).then_inc(R["in"], 16)

                def turn(q):
                    if q.step(-1):
                        store(q.step(-1))
                    if q.step(1):
                        load_h(q.step(1))
                        load_x(q.step(1))

                run(sp, [], begin, turn, store)
                for a in range(2):
                    sp.wait_ge(stored[a], 16 * (NG // 2 + 1 - a))
                sp.wait_ge(R["in"], 32 * NX)

            W_ALL = 16 * 10

            @block.gpsimd
            def _(pool):
                pool.iota(ids[:], [[P, NT]], base=0, channel_multiplier=1).then_inc(iotas, 1)
                pool.memset(zeros[:], 0).then_inc(iotas, 1)
                pool.iota(room_i[:], [[NP, NX]], base=0, channel_multiplier=0).then_inc(iotas, 1)
                pool.wait_ge(cleared, 16)

                def list_nodes(q):
                    pool.wait_ge(slots_r, q.g + 1)
                    pool.wait_ge(ids_r, q.g + 1)
                    pool.sem_inc(turns)
                    n = REST if q.nt == 1 else P
                    for t in range(q.nt):
                        for j in range(2):
                            pool.indirect_dma_start(ids_d, bass.IndirectOffsetOnAxis(slot_st[0:n, q.a, t, j:j + 1], 0),
                                                    id_st[0:n, q.a, t:t + 1], None).then_inc(listed[q.a], 16)

                run(pool, [], lambda q: None, lambda q: q.step(-1) and list_nodes(q.step(-1)), list_nodes)
                pool.wait_ge(listed[0], 16 * 2 * (GT * NG // 2 + 1))
                pool.wait_ge(listed[1], 16 * 2 * (GT * NG // 2))

            @block.vector
            def _(dve):
                t_l = Tally(dl)
                link = linker(dve, t_l)

                def wide(i, nt):
                    return vec[:, i].unsqueeze(1).to_broadcast([P, nt, D])

                def norm_in(src, nt, which):
                    for i in range(nt):
                        ins = dve.bn_stats(stats[:, i], src[:, i])
                    link(ins)
                    dve.sem_inc(turns)
                    for i in range(nt):
                        ins = dve.bn_aggr(mv[:, i], stats[:, i])
                    ins.then_inc(var_r[which], 1)

                def norm_out(dst, src, q, which):
                    dve.wait_ge(std_r[which], q.g + 1)
                    link(dve.reciprocal(rstd[:, 0:q.nt], std[:, 0:q.nt]))
                    for i in range(q.nt):
                        ins = dve.tensor_scalar(dst[:, i], src[:, i], mv[:, i, 0:1], rstd[:, i:i + 1], ALU.subtract,
                                                ALU.mult)
                    return ins

                def attention(q):
                    nt = q.nt
                    dve.wait_ge(h_in, q.g * 16 + 16)
                    av = acc[:, bass.ds(q.g * GT, nt), :]
                    link(dve.tensor_scalar(rden[:, 0:nt], av[:, :, D:D + H], 1e-30, None, ALU.max))
                    link(dve.reciprocal(rden[:, 0:nt], rden[:, 0:nt]))
                    if not q.early(2):
                        dve.wait_ge(t_ps[1], q.g - 1)
                        dve.wait_ge(stored[q.a], q.k * 16)
                    yv = y1[:, q.a, 0:nt]
                    link(dve.tensor_tensor(yv.rearrange("p t (h e) -> p t h e", h=H),
                                           av[:, :, 0:D].rearrange("p t (h e) -> p t h e", h=H),
                                           rden[:, 0:nt].unsqueeze(3).to_broadcast([P, nt, H, HD]), ALU.mult))
                    dve.tensor_tensor(yv, yv, hin[:, 0:nt], ALU.add).then_inc(h_used, 1)
                    dve.wait_ge(h_used, q.g + 1)
                    norm_in(y1[:, q.a], nt, 0)

                def first_norm(q):
                    yv = y1[:, q.a, 0:q.nt]
                    link(norm_out(y1[:, q.a], y1[:, q.a], q, 0))
                    link(dve.tensor_tensor(yv, yv, wide(0, q.nt), ALU.mult))
                    dve.tensor_tensor(yv, yv, wide(1, q.nt), ALU.add).then_inc(y1_r, 1)

                def after_ffn(q):
                    yv = y1[:, q.a, 0:q.nt]
                    dve.wait_ge(dn_ps, q.g + 1)
                    dve.wait_ge(t_ps[0], q.g + 1)
                    dve.wait_ge(y1_r, q.g + 1)
                    dve.tensor_tensor(yv.rearrange("p t d -> p (t d)"), p_dn[:, 0:q.nt * D],
                                      yv.rearrange("p t d -> p (t d)"), ALU.add).then_inc(dn_used, 1)
                    dve.wait_ge(dn_used, q.g + 1)
                    link(dve.tensor_tensor(yv, yv, wide(4, q.nt), ALU.add))
                    norm_in(y1[:, q.a], q.nt, 1)

                def residual(q):
                    nt = q.nt
                    yv, xv = y1[:, q.a, 0:nt], acc[:, bass.ds(q.g * GT, nt), 0:D]
                    link(norm_out(y1[:, q.a], y1[:, q.a], q, 1))
                    link(dve.tensor_tensor(yv, yv, wide(2, nt), ALU.mult))
                    link(dve.tensor_tensor(yv, yv, wide(3, nt), ALU.add))
                    dve.wait_ge(x_in[q.a], q.k * 16 + 16)
                    dve.tensor_tensor(yv, yv, xin[:, q.a, 0:nt], ALU.add).then_inc(x_used, 1)
                    dve.wait_ge(x_used, q.g + 1)
                    dve.tensor_copy(xv, yv)
                    norm_in(y1[:, q.a], nt, 2)

                def normal(q):
                    norm_out(y1[:, q.a], y1[:, q.a], q, 2).then_inc(n_r, 1)

                def gate(q):
                    nt = q.nt
                    dve.wait_ge(lg_ps, q.g + 1)
                    lv = lg[:, 0:nt]
                    link(dve.tensor_tensor(lv, p_g[:, 0:nt * NX].rearrange("p (t e) -> p t e", e=NX),
                                           gb[:].unsqueeze(1).to_broadcast([P, nt, NX]), ALU.add))
                    link(dve.tensor_reduce(top[:, 0:nt], lv, AX.X, ALU.max))
                    dve.tensor_tensor(lv, lv, top[:, 0:nt].unsqueeze(2).to_broadcast([P, nt, NX]),
                                      ALU.subtract).then_inc(lg_r, 1)

                def choose(q):
                    nt = q.nt
                    dve.wait_ge(ex_r, q.g + 1)
                    pv = pr[:, 0:nt]
                    link(dve.tensor_reduce(tot[:, 0:nt], ex[:, 0:nt], AX.X, ALU.add))
                    link(dve.reciprocal(tot[:, 0:nt], tot[:, 0:nt]))
                    link(dve.tensor_tensor(pv, ex[:, 0:nt], tot[:, 0:nt].unsqueeze(2).to_broadcast([P, nt, NX]),
                                           ALU.mult))
                    for t in range(nt):
                        own = pr[:, t].unsqueeze(2).to_broadcast([P, NX, NX])
                        other = pr[:, t].unsqueeze(1).to_broadcast([P, NX, NX])
                        dve.tensor_tensor(more[:, t], other, own, ALU.is_gt)
                        ins = dve.tensor_tensor(equal[:, t], other, own, ALU.is_equal)
                    link(ins)
                    mv_, ev = more[:, 0:nt].rearrange("p t j i -> p t (j i)"), equal[:, 0:nt].rearrange("p t j i -> p t (j i)")
                    link(dve.tensor_tensor(ev, ev, before[:].rearrange("p j i -> p (j i)").unsqueeze(1)
                                           .to_broadcast([P, nt, NX * NX]), ALU.mult))
                    link(dve.tensor_tensor(mv_, mv_, ev, ALU.add))
                    link(dve.tensor_reduce(rank[:, 0:nt], more[:, 0:nt], AX.X, ALU.add))
                    if not q.early(1):
                        dve.wait_ge(rk_ps, q.g)
                    for j in range(2):
                        dve.tensor_scalar(sel[:, j, 0:nt], rank[:, 0:nt], float(j), None, ALU.is_equal)
                    ins = dve.tensor_scalar(both[:, 0:nt], rank[:, 0:nt], 2.0, None, ALU.is_lt)
                    ins.then_inc(sel_r, 1)
                    dve.wait_ge(sel_r, q.g + 1)
                    for j in range(2):
                        link(dve.tensor_tensor(mine[:, 0:nt], sel[:, j, 0:nt], pv, ALU.mult))
                        link(dve.tensor_reduce(R["share"][:, bass.ds(q.g * GT, nt), j], mine[:, 0:nt], AX.X, ALU.add))

                def places(q):
                    nt = q.nt
                    dve.wait_ge(rk_ps, q.g + 1)
                    for t in range(nt):
                        dve.tensor_tensor(spot[:, t], p_r[:, t * NX:(t + 1) * NX], R["taken"][:], ALU.add)
                        link(dve.tensor_tensor(R["taken"][:], p_r[:, (GT + t) * NX:(GT + t + 1) * NX], R["taken"][:],
                                               ALU.add))
                    dve.sem_inc(rk_used)
                    if not q.early(2):
                        dve.wait_ge(listed[q.a], q.k * (2 * GT * 16))
                    for j in range(2):
                        link(dve.tensor_tensor(mine[:, 0:nt], sel[:, j, 0:nt], spot[:, 0:nt], ALU.mult))
                        link(dve.tensor_reduce(slot_f[:, 0:nt], mine[:, 0:nt], AX.X, ALU.add))
                        dve.tensor_copy(R["slots"][:].rearrange("p (t j) -> p t j", j=2)[:, bass.ds(q.g * GT, nt), j], slot_f[:, 0:nt])
                        link(dve.tensor_copy(slot_st[:, q.a, 0:nt, j], slot_f[:, 0:nt]))
                    dve.sem_inc(slots_r)

                def begin(q):
                    dve.memset(eps[:], EPS).then_inc(consts, 1)
                    dve.tensor_tensor(before[:], K["col"][:, 0:NX].unsqueeze(1).to_broadcast([P, NX, NX]),
                                      K["col"][:, 0:NX].unsqueeze(2).to_broadcast([P, NX, NX]),
                                      ALU.is_lt).then_inc(consts, 1)
                    dve.wait_ge(iotas, 3)
                    link(dve.tensor_copy(R["taken"][:], room_i[:]))
                    dve.wait_ge(w_in, W_ALL)
                    attention(q)
                    first_norm(q)

                def finish_norms(q):
                    after_ffn(q)
                    residual(q)
                    normal(q)

                def turn(q):
                    pv, nx = q.step(-1), q.step(1)
                    if pv:
                        finish_norms(pv)
                    if nx:
                        attention(nx)
                    if pv:
                        gate(pv)
                    if nx:
                        first_norm(nx)
                    if pv:
                        choose(pv)
                        places(pv)

                def end(q):
                    finish_norms(q)
                    gate(q)
                    choose(q)
                    places(q)

                per_group = 3 + 1 + 1 + 2 + 2 + 3 + 1 + 1 + 2 + 7 + 4 + GT + 7
                run(dve, [(t_l, 2 * per_group)], begin, turn, end)

            @block.scalar
            def _(act):
                t_up = Tally(up_out)

                def root(q, which):
                    act.wait_ge(var_r[which], q.g + 1)
                    act.activation(std[:, 0:q.nt], mv[:, 0:q.nt, 1], ACT.Sqrt, bias=eps[:]).then_inc(std_r[which], 1)

                def relus(q, blocks):
                    if not q.early(1):
                        act.wait_ge(dn_ps, q.g)
                    for b in blocks:
                        i = t_up.n % 2
                        t_up.n += 1
                        act.wait_ge(up_ps, t_up.value())
                        act.activation(h1T[:, b, 0:q.n], p_up[i][:, 0:q.n], ACT.Relu, bias=b1c[:, b:b + 1]).then_inc(up_out, 1)

                def turned(q, which, dst):
                    act.wait_ge(t_ps[which], q.g + 1)
                    for c in range(DC):
                        ins = act.copy(dst[:, c, 0:q.n], p_t[c][:, 0:q.n])
                    ins.then_inc(t_out[which], 1)

                def n_turned(q):
                    if not q.early(1):
                        act.wait_ge(lg_ps, q.g)
                    turned(q, 1, nT)

                def exps(q):
                    act.wait_ge(lg_r, q.g + 1)
                    act.activation(ex[:, 0:q.nt], lg[:, 0:q.nt], ACT.Exp).then_inc(ex_r, 1)
                    if not q.early(2):
                        act.wait_ge(listed[q.a], q.k * (2 * GT * 16))
                    act.copy(id_st[:, q.a, 0:q.nt], ids[:, bass.ds(q.g * GT, q.nt)]).then_inc(ids_r, 1)

                def begin(q):
                    act.wait_ge(consts, 2)
                    act.wait_ge(iotas, 3)
                    root(q, 0)
                    turned(q, 0, y1T)

                def turn(q):
                    pv, nx = q.step(-1), q.step(1)
                    if pv:
                        root(pv, 1)
                    relus(q, range(FB // 2))
                    if pv:
                        root(pv, 2)
                    relus(q, range(FB // 2, FB))
                    if pv:
                        n_turned(pv)
                    if nx:
                        root(nx, 0)
                    if pv:
                        exps(pv)
                    if nx:
                        turned(nx, 0, y1T)

                def end(q):
                    root(q, 1)
                    root(q, 2)
                    n_turned(q)
                    exps(q)

                run(act, [(t_up, 2 * FB)], begin, turn, end)

            @block.tensor
            def _(pe):
                t_up = Tally(up_ps)

                def transposes(q, which):
                    pe.wait_ge(n_r if which else y1_r, q.g + 1)
                    if which:
                        pe.wait_ge(t_out[0], q.g + 2 if q.step(1) else q.g + 1)
                    elif not q.early(2):
                        pe.wait_ge(t_out[1], q.g - 1)
                    for c in range(DC):
                        for t in range(q.nt):
                            ins = pe.transpose(p_t[c][:, t * P:(t + 1) * P], y1[:, q.a, t, c * P:(c + 1) * P], K["ident"][:])
                    ins.then_inc(t_ps[which], 1)

                def ffn_up(q):
                    pe.wait_ge(t_out[0], q.g + 1)
                    for b in range(FB):
                        i = t_up.n % 2
                        if t_up.n >= 2 or t_up.k is not None:
                            pe.wait_ge(up_out, t_up.value(1))
                        t_up.n += 1
                        for c in range(DC):
                            ins = pe.matmul(p_up[i][:, 0:q.n], w1[:, c, b * P:(b + 1) * P], y1T[:, c, 0:q.n],
                                            start=c == 0, stop=c == DC - 1)
                        ins.then_inc(up_ps, 1)

                def ffn_down(q, tiles, first, last):
                    if first:
                        pe.wait_ge(up_out, t_up.value())
                        if not q.early(1):
                            pe.wait_ge(dn_used, q.g)
                    for t in tiles:
                        for b in range(FB):
                            ins = pe.matmul(p_dn[:, t * D:(t + 1) * D], h1T[:, b, t * P:(t + 1) * P], w2[:, b],
                                            start=b == 0, stop=b == FB - 1)
                    if last:
                        ins.then_inc(dn_ps, 1)

                def logits(q):
                    pe.wait_ge(t_out[1], q.g + 1)
                    for t in range(q.nt):
                        for c in range(DC):
                            ins = pe.matmul(p_g[:, t * NX:(t + 1) * NX], nT[:, c, t * P:(t + 1) * P], gw[:, c],
                                            start=c == 0, stop=c == DC - 1)
                    ins.then_inc(lg_ps, 1)

                def counts(q):
                    pe.wait_ge(sel_r, q.g + 1)
                    if not q.early(1):
                        pe.wait_ge(rk_used, q.g)
                    n = REST if q.nt == 1 else P
                    for t in range(q.nt):
                        pe.matmul(p_r[:, t * NX:(t + 1) * NX], K["lower"][0:n, :], both[0:n, t], start=True, stop=True)
                        ins = pe.matmul(p_r[:, (GT + t) * NX:(GT + t + 1) * NX], K["ones"][0:n, :], both[0:n, t],
                                        start=True, stop=True)
                    ins.then_inc(rk_ps, 1)

                def begin(q):
                    pe.wait_ge(w_in, W_ALL)
                    transposes(q, 0)

                def turn(q):
                    pv, nx = q.step(-1), q.step(1)
                    ffn_up(q)
                    if pv:
                        transposes(pv, 1)
                        logits(pv)
                    half = (q.nt + 1) // 2
                    ffn_down(q, range(half), True, half == q.nt)
                    if pv:
                        counts(pv)
                    if half < q.nt:
                        ffn_down(q, range(half, q.nt), False, True)
                    if nx:
                        transposes(nx, 0)

                def end(q):
                    transposes(q, 1)
                    logits(q)
                    counts(q)

                run(pe, [(t_up, 2 * FB)], begin, turn, end)


def stage_experts(nc, K, A_in, n_d, ids_d, tile_d, y_d, R):
    XB = FX // P
    ctx, sb, pb, sem = make_tools(nc)
    with ctx:
        b1, b2 = sb("xb1", [P, NX, FX]), sb("xb2", [P, NX, D])
        room_i, room = sb("xroom_i", [P, NX], I32), sb("xroom", [P, NX])
        cnt, cnt_i, nt_i, nt_f = sb("xcnt", [P, NX]), sb("xcnt_i", [P, NX], I32), sb("xnt_i", [P, NX], I32), sb("xnt_f", [P, NX])
        zero, t_end, size = sb("xzero", [P, NX]), sb("xt_end", [P, NX]), sb("xsize", [P, NX])
        it_i, it = sb("it_i", [P, 1], I32), sb("it", [P, 1])
        past, gone = sb("xpast", [P, NX]), sb("xgone", [P, NX])
        info = sb("xinfo", [P, 4])
        info_i = sb("xinfo_i", [P, 2], I32)
        first, steps = sb("xfirst", [P, NX]), sb("xsteps", [P, NX])
        rows_f, above = sb("xrows_f", [P, 2 * NT]), sb("xabove", [P, 2 * NT])
        tab = sb("xtab", [1, 2, P], I32)
        idx = sb("xidx", [P, XG, 1], I32)
        xg, xT = sb("xg", [P, XG, D]), sb("xTx", [P, 2, DC * P])
        hb, g = sb("xhb", [P, 2, FX]), sb("xg_act", [P, 2, FX])
        gT = sb("xgT", [P, 2, XB * P])
        y = sb("xy", [P, 2, D])
        p_x = [pb(f"p_x{a}") for a in range(2)]
        p_h = [pb(f"p_h{a}") for a in range(2)]
        p_g = [pb(f"p_gT{a}") for a in range(2)]
        p_y = [pb(f"p_y{a}") for a in range(2)]
        b_in, it_r, link_x, info_r, tab_in = sem("xb_in"), sem("it_r"), sem("link_x"), sem("info_r"), sem("tab_in")
        i_in, g_in, stored = [[sem(f"x{n}{r}") for r in range(XG)] for n in ("i_in", "g_in", "stored")]
        xT_ps, xT_r, h_ps, h_r, g_r, gT_ps, gT_r, y_ps, y_r = (sem("x" + n) for n in (
            "xT_ps", "xT_r", "h_ps", "h_r", "g_r", "gT_ps", "gT_r", "y_ps", "y_r"))
        turns = sem("x_turns")
        assert XT % 2 == 0

        class Tile:

            def __init__(self, k, r):
                self.k, self.r, self.a = k + r // XG, r % XG, r % 2
                self.i = self.k * XG + self.r

            def after(self, d):
                x = Tile(self.k, self.r + d)
                return None if isinstance(x.i, int) and not 0 <= x.i < XT else x

            def early(self, n):
                return isinstance(self.i, int) and self.i < n

        def run(eng, step):
            whole = XT // XG
            for r in range(XG):
                step(Tile(0, r))
            with eng.Fori(1, whole - 1) as k:
                for r in range(XG):
                    step(Tile(k, r))
            for r in range(XG + XT % XG):
                step(Tile(whole - 1, r))

        def value(engine, which, x, top):
            _, w = nc.values_load_multi_w_load_instructions(
                tab[0:1, which, bass.ds(x.i, 1)], engines=(engine,), min_val=0, max_val=top,
                skip_runtime_bounds_check_because="made below its bound")
            return w[0]

        with nc.Block() as block:

            @block.sync
            def _(sp):
                sp.dma_start(b1[:], A_in["L0_ffn_b1"].unsqueeze(0).to_broadcast([P, NX, FX])).then_inc(b_in, 16)
                sp.dma_start(b2[:], A_in["L0_ffn_b2"].unsqueeze(0).to_broadcast([P, NX, D])).then_inc(b_in, 16)
                sp.wait_ge(info_r, 1)
                with nc.allow_non_contiguous_dma(reason="a table of a few words"):
                    sp.dma_start(tile_d.rearrange("w p -> p w"), info_i[:]).then_inc(tab_in, 16)
                sp.wait_ge(tab_in, 16)
                sp.dma_start(tab[:], tile_d.unsqueeze(0)).then_inc(tab_in, 16)
                sp.wait_ge(tab_in, 32)

                def ids(x):
                    row = value(mybir.EngineType.SP, 1, x, XR - P)
                    if not x.early(XG):
                        sp.wait_ge(g_in[x.r], x.k * 16)
                        sp.sem_inc(turns)
                    sp.dma_start(idx[:, x.r], ids_d[bass.ds(row, P), :]).then_inc(i_in[x.r], 16)

                def store(x):
                    sp.wait_ge(y_r, x.i + 1)
                    sp.sem_inc(turns)
                    sp.dma_start(y_d.rearrange("(t p) d -> t p d", p=P)[x.i], y[:, x.a]).then_inc(stored[x.r], 16)

                def step(x):
                    if x.after(XG - 2):
                        ids(x.after(XG - 2))
                    store(x)

                for r in range(XG - 2):
                    ids(Tile(0, r))
                run(sp, step)
                for r in range(XG):
                    sp.wait_ge(stored[r], 16 * (XT // XG + (r < XT % XG)))

            @block.gpsimd
            def _(pool):
                pool.iota(it_i[:], [[0, 1]], base=0, channel_multiplier=1).then_inc(it_r, 1)
                pool.iota(room_i[:], [[NP, NX]], base=0, channel_multiplier=0).then_inc(it_r, 1)

                def step(x):
                    pool.wait_ge(i_in[x.r], x.k * 16 + 16)
                    if not x.early(XG):
                        pool.wait_ge(xT_ps, x.i + 1 - XG)
                    pool.sem_inc(turns)
                    pool.indirect_dma_start(xg[:, x.r], None, n_d, bass.IndirectOffsetOnAxis(idx[:, x.r], 0)).then_inc(g_in[x.r], 16)

                run(pool, step)

            @block.vector
            def _(dve):
                link = linker(dve, Tally(link_x))
                dve.wait_ge(it_r, 2)
                dve.tensor_copy(it[:], it_i[:])
                dve.memset(zero[:], 0.0)
                link(dve.tensor_copy(room[:], room_i[:]))
                link(dve.tensor_tensor(cnt[:], R["taken"][:], room[:], ALU.subtract))
                link(dve.tensor_scalar(cnt_i[:], cnt[:], float(P - 1), None, ALU.add))
                link(dve.tensor_scalar(nt_i[:], cnt_i[:], 7, None, ALU.logical_shift_right))
                link(dve.tensor_copy(nt_f[:], nt_i[:]))
                link(dve.tensor_tensor_scan(t_end[:], zero[:], nt_f[:], 0.0, ALU.add, ALU.add))
                link(dve.tensor_scalar(past[:], t_end[:], it[:, 0:1], None, ALU.is_le))
                dve.tensor_reduce(info[:, 0:1], past[:], AX.X, ALU.add)
                link(dve.tensor_tensor(gone[:], past[:], nt_f[:], ALU.mult))
                link(dve.tensor_reduce(info[:, 1:2], gone[:], AX.X, ALU.add))
                link(dve.tensor_tensor(info[:, 2:3], it[:], info[:, 1:2], ALU.subtract))
                link(dve.tensor_scalar(info[:, 2:3], info[:, 2:3], float(P), None, ALU.mult))
                link(dve.scalar_tensor_tensor(info[:, 3:4], info[:, 0:1], float(NP), info[:, 2:3], ALU.mult, ALU.add))
                dve.tensor_scalar(info_i[:, 0:1], info[:, 0:1], float(NX - 1), None, ALU.min)
                link(dve.tensor_copy(info_i[:, 1:2], info[:, 3:4]))
                dve.sem_inc(info_r)
                link(dve.tensor_tensor(first[:], t_end[:], nt_f[:], ALU.subtract))
                link(dve.scalar_tensor_tensor(first[:], first[:], float(P), room[:], ALU.mult, ALU.subtract))
                dve.tensor_copy(steps[:, 0:1], first[:, 0:1])
                link(dve.tensor_tensor(steps[:, 1:NX], first[:, 1:NX], first[:, 0:NX - 1], ALU.subtract))
                link(dve.tensor_copy(rows_f[:], R["slots"][:]))
                for e in range(NX):
                    link(dve.tensor_scalar(above[:], R["slots"][:], float(e * NP), None, ALU.is_ge))
                    link(dve.scalar_tensor_tensor(rows_f[:], above[:], steps[:, e:e + 1], rows_f[:], ALU.mult, ALU.add))
                link(dve.tensor_copy(R["rows"][:], rows_f[:]))
                dve.wait_ge(b_in, 32)
                dve.wait_ge(tab_in, 32)

                def hidden(x):
                    e = value(mybir.EngineType.DVE, 0, x, NX - 1)
                    dve.wait_ge(h_ps, x.i + 1)
                    if not x.early(2):
                        dve.wait_ge(g_r, x.i - 1)
                    dve.tensor_tensor(hb[:, x.a], p_h[x.a][:], b1[:, bass.ds(e, 1), :].rearrange("p o f -> p (o f)"),
                                      ALU.add).then_inc(h_r, 1)
                    return e

                def result(x):
                    e = value(mybir.EngineType.DVE, 0, x, NX - 1)
                    dve.wait_ge(y_ps, x.i + 1)
                    if not x.early(2):
                        b = x.after(-2)
                        dve.wait_ge(stored[b.r], b.k * 16 + 16)
                    dve.tensor_tensor(y[:, x.a], p_y[x.a][:, 0:D], b2[:, bass.ds(e, 1), :].rearrange("p o f -> p (o f)"),
                                      ALU.add).then_inc(y_r, 1)

                def step(x):
                    if x.after(2):
                        hidden(x.after(2))
                    result(x)

                hidden(Tile(0, 0))
                hidden(Tile(0, 1))
                run(dve, step)

            @block.scalar
            def _(act):
                def turned(x):
                    act.wait_ge(xT_ps, x.i + 1)
                    if not x.early(2):
                        act.wait_ge(h_ps, x.i - 1)
                    act.copy(xT[:, x.a], p_x[x.a][:, 0:DC * P]).then_inc(xT_r, 1)

                def gelu(x):
                    act.wait_ge(h_r, x.i + 1)
                    if not x.early(2):
                        act.wait_ge(gT_ps, x.i - 1)
                    act.activation(g[:, x.a], hb[:, x.a], ACT.Gelu).then_inc(g_r, 1)

                def gelu_turned(x):
                    act.wait_ge(gT_ps, x.i + 1)
                    if not x.early(2):
                        act.wait_ge(y_ps, x.i - 1)
                    act.copy(gT[:, x.a], p_g[x.a][:]).then_inc(gT_r, 1)

                def step(x):
                    if x.after(1):
                        gelu_turned(x.after(1))
                    if x.after(2):
                        gelu(x.after(2))
                    if x.after(3):
                        turned(x.after(3))

                turned(Tile(0, 0))
                turned(Tile(0, 1))
                gelu(Tile(0, 0))
                gelu_turned(Tile(0, 0))
                gelu(Tile(0, 1))
                turned(Tile(0, 2))
                run(act, step)

            @block.tensor
            def _(pe):
                pe.wait_ge(tab_in, 32)

                def turn_rows(x):
                    pe.wait_ge(g_in[x.r], x.k * 16 + 16)
                    if not x.early(2):
                        pe.wait_ge(xT_r, x.i - 1)
                    for c in range(DC):
                        ins = pe.transpose(p_x[x.a][:, c * P:(c + 1) * P], xg[:, x.r, c * P:(c + 1) * P], K["ident"][:])
                    ins.then_inc(xT_ps, 1)

                def up(x):
                    e = value(mybir.EngineType.PE, 0, x, NX - 1)
                    pe.wait_ge(xT_r, x.i + 1)
                    if not x.early(2):
                        pe.wait_ge(h_r, x.i - 1)
                    for c in range(DC):
                        ins = pe.matmul(p_h[x.a][:], xT[:, x.a, c * P:(c + 1) * P],
                                        R["w1"][:, bass.ds(e, 1), c, :].rearrange("p o f -> p (o f)"),
                                        start=c == 0, stop=c == DC - 1)
                    ins.then_inc(h_ps, 1)

                def turn_hidden(x):
                    pe.wait_ge(g_r, x.i + 1)
                    if not x.early(2):
                        pe.wait_ge(gT_r, x.i - 1)
                    for b in range(XB):
                        ins = pe.transpose(p_g[x.a][:, b * P:(b + 1) * P], g[:, x.a, b * P:(b + 1) * P], K["ident"][:])
                    ins.then_inc(gT_ps, 1)

                def down(x):
                    e = value(mybir.EngineType.PE, 0, x, NX - 1)
                    pe.wait_ge(gT_r, x.i + 1)
                    if not x.early(2):
                        pe.wait_ge(y_r, x.i - 1)
                    for b in range(XB):
                        ins = pe.matmul(p_y[x.a][:, 0:D], gT[:, x.a, b * P:(b + 1) * P],
                                        R["w2"][:, bass.ds(e, 1), b, :].rearrange("p o f -> p (o f)"),
                                        start=b == 0, stop=b == XB - 1)
                    ins.then_inc(y_ps, 1)

                def step(x):
                    if x.after(2):
                        up(x.after(2))
                    if x.after(1):
                        turn_hidden(x.after(1))
                    if x.after(3):
                        turn_rows(x.after(3))
                    down(x)

                for r in range(3):
                    turn_rows(Tile(0, r))
                    if r < 2:
                        up(Tile(0, r))
                    if r == 1:
                        turn_hidden(Tile(0, 0))
                run(pe, step)


def stage_combine(nc, K, acc, y_d, out, R):
    ctx, sb, pb, sem = make_tools(nc)
    with ctx:
        CR = 4
        yg, res, idx = sb("c_y", [P, CR, 2, D]), sb("c_res", [P, CR, D]), sb("c_idx", [P, CR, 2], I32)
        idx_r, arrived, used, res_r = sem("c_idx_r"), [sem(f"c_in{r}") for r in range(CR)], sem("c_used"), sem("c_res_r")
        stored, turns, half = [sem(f"c_st{r}") for r in range(CR)], sem("c_turns"), sem("c_half")

        def run(eng, step):
            for r in range(CR):
                step(0, r, P)
            with eng.Fori(1, NT // CR) as k:
                for r in range(CR):
                    step(k, r, P)
            step(NT // CR, 0, REST)

        def early(k):
            return isinstance(k, int) and k == 0

        with nc.Block() as block:

            @block.gpsimd
            def _(pool):
                def step(k, r, n):
                    pool.wait_ge(idx_r, k * CR + r + 1)
                    if not early(k):
                        pool.wait_ge(used, (k - 1) * CR + r + 1)
                    pool.sem_inc(turns)
                    for j in range(2):
                        pool.indirect_dma_start(yg[0:n, r, j], None, y_d,
                                                bass.IndirectOffsetOnAxis(idx[0:n, r, j:j + 1], 0)).then_inc(arrived[r], 16)

                run(pool, step)

            @block.scalar
            def _(act):
                def step(k, r, n):
                    if not early(k):
                        act.wait_ge(arrived[r], k * 32)
                    act.copy(idx[:, r], R["rows"][:, bass.ds((k * CR + r) * 2, 2)]).then_inc(idx_r, 1)

                run(act, step)

            @block.vector
            def _(dve):
                def step(k, r, n):
                    t = k * CR + r
                    dve.wait_ge(arrived[r], k * 32 + 32)
                    if not early(k):
                        dve.wait_ge(stored[r], k * 16)
                    x1 = acc[0:n, bass.ds(t, 1), 0:D].rearrange("p o d -> p (o d)")
                    share = R["share"][0:n, bass.ds(t, 1), :].rearrange("p o j -> p (o j)")
                    dve.scalar_tensor_tensor(res[0:n, r], yg[0:n, r, 0], share[:, 0:1], x1, ALU.mult,
                                             ALU.add).then_inc(half, 1)
                    dve.wait_ge(half, t + 1)
                    dve.scalar_tensor_tensor(res[0:n, r], yg[0:n, r, 1], share[:, 1:2], res[0:n, r], ALU.mult,
                                             ALU.add).then_inc(used, 1)

                run(dve, step)

            @block.sync
            def _(sp):
                def step(k, r, n):
                    sp.wait_ge(used, k * CR + r + 1)
                    sp.sem_inc(turns)
                    to = out[0:(NT - 1) * P, :].rearrange("(t p) d -> t p d", p=P)[k * CR + r] if n == P else \
                        out[(NT - 1) * P:N, :]
                    sp.dma_start(to, res[0:n, r]).then_inc(stored[r], 16)

                run(sp, step)
                for r in range(CR):
                    sp.wait_ge(stored[r], 16 * (NT // CR + (r == 0)))
def program(nc, A_in, out):
    ctx, sb, pb, sem = make_tools(nc)

    def scratch(name, shape, dt=F32):
        return nc.dram_tensor(name, shape, dt, kind="Internal").ap()

    h0_d, k_d, v_d, n_d = (scratch(n, [N, D]) for n in ("h0_d", "k_d", "v_d", "n_d"))
    ids_d, tile_d, y_d = scratch("ids_d", [XR, 1], I32), scratch("tile_d", [2, P], I32), scratch("y_d", [XT * P, D])
    sorted_d, win_d = scratch("sorted_d", [P * ST, 2], I32), scratch("win_d", [ST], I32)
    with ctx:
        K = constants(nc, sb)
        big = sb("big", [P, max(NT * (D + H), 2 * CL + 1)])
        q_sb = big[:, 0:NT * D].rearrange("p (t d) -> p t d", t=NT)
        acc = big[:, 0:NT * (D + H)].rearrange("p (t d) -> p t d", t=NT)
        stage_constants(nc, K)
        stage_sort(nc, K, A_in["src"], A_in["dst"], sorted_d, win_d)
        edges, sb2, _, _ = make_tools(nc)
        with edges:
            T = {}
            for x in ("", "_x"):
                T["key" + x], T["lo" + x] = sb2("T_key" + x, [P, ST]), sb2("T_lo" + x, [P, ST])
                T["dst" + x], T["win" + x] = sb2("T_dst" + x, [P, ST], I32), sb2("T_win" + x, [1, ST], I32)
            T["keep"] = sb2("T_keep", [P, ST])
            A = sb2("A", [P, ST, H])
            stage_tables(nc, sorted_d, win_d, T)
            stage_qkv(nc, K, A_in["x"], A_in["L0_gnn_w_qkv"], A_in["L0_gnn_b_qkv"], h0_d, k_d, v_d, q_sb)
            stage_scores(nc, K, T, q_sb, k_d, A)
            stage_softmax(nc, K, T, A, big)
            stage_sums(nc, K, T, A, v_d, acc)
        R = {"w1": sb("xw1", [P, NX, DC, FX]), "w2": sb("xw2", [P, NX, FX // P, D]), "in": sem("xw_in"),
             "share": sb("share", [P, NT, 2]), "slots": sb("slots", [P, NT * 2]), "rows": sb("y_rows", [P, NT * 2], I32), "taken": sb("taken", [P, NX])}
        stage_front(nc, K, A_in, acc, h0_d, n_d, ids_d, R)
        stage_experts(nc, K, A_in, n_d, ids_d, tile_d, y_d, R)
        stage_combine(nc, K, acc, y_d, out, R)


_INS = ["x", "src", "dst"] + ["L0_gnn_" + n for n in ("w_qkv", "b_qkv", "ln1_g", "ln1_b", "ln2_g", "ln2_b", "w1",
                                                      "b1", "w2", "b2")] \
    + ["L0_ffn_" + n for n in ("gate_w", "gate_b", "W1", "b1", "W2", "b2")]


def kernel(**inputs):
    import numpy as _np
    import concourse.bacc as _bacc
    from concourse import mybir as _mybir
    from concourse.bass_utils import run_bass_kernel_spmd as _run

    nc = _bacc.Bacc("TRN2", target_bir_lowering=False, num_devices=1)
    arrays, args = {}, {}
    for name in _INS:
        a = _np.ascontiguousarray(inputs[name])
        arrays[f"in_{name}_dram"] = a
        args[name] = nc.dram_tensor(f"in_{name}_dram", a.shape, _mybir.dt.from_np(a.dtype), kind="ExternalInput").ap()
    out = nc.dram_tensor("out_dram", (6250, 256), _mybir.dt.float32, kind="ExternalOutput").ap()
    program(nc, args, out)
    r = _run(nc, [arrays], core_ids=[0])
    return r.results[0]["out_dram"]
```

```python
import concourse.bass as bass
from concourse import mybir
from contextlib import ExitStack

F32, I32, BF16 = mybir.dt.float32, mybir.dt.int32, mybir.dt.bfloat16
ALU, ACT, AX = mybir.AluOpType, mybir.ActivationFunctionType, mybir.AxisListType

P = 128
N, E, D, H = 6250, 100000, 256, 8
HD = D // H
DC = D // P
F = 4 * D
NX, FX = 8, 512
EPS = 1e-5
SCALE = D ** -0.5

NT = -(-N // P)
GT = 4
NG = N // (GT * P)
REST = N - NG * GT * P
EP = 125
ET = E // EP
EB = 8
CH = 16
ST = -(-(-(-E // P) + NT) // CH) * CH
SC = ST // CH
CL = SC * P
PAD_KEY = -1
NO_LO = 256.0
LOW = -1e30


class Tally:

    def __init__(self, sem):
        self.sem, self.n, self.k, self.per = sem, 0, None, 0

    def value(self, back=0):
        v = self.n - back
        return v if self.k is None else self.k * self.per + v

    def enter(self, k, per):
        self.k, self.per, self.base = k, per, self.n

    def leave(self, turns):
        assert self.n - self.base == self.per, (self.n - self.base, self.per)
        self.n = self.base + self.per * turns
        self.k = None


def linker(eng, tally):

    def link(ins):
        ins.then_inc(tally.sem, 1)
        tally.n += 1
        eng.wait_ge(tally.sem, tally.value())

    return link


def make_tools(nc):
    ctx, sems = ExitStack(), []

    def clear():
        if sems:
            nc.clear_and_free_semaphores(sems)
            nc.all_engine_barrier()

    ctx.callback(clear)

    def sb(name, shape, dt=F32):
        return ctx.enter_context(nc.sbuf_tensor(name, shape, dt))

    def pb(name, shape=(P, 512), dt=F32):
        return ctx.enter_context(nc.psum_tensor(name, list(shape), dt))

    def sem(name):
        sems.append(nc.alloc_semaphore(name=name))
        return sems[-1]

    return ctx, sb, pb, sem


def stage_constants(nc, K):
    ctx, sb, pb, sem = make_tools(nc)
    with ctx:
        made, ints, cast = sem("made"), sem("ints"), sem("cast")
        with nc.Block() as block:

            @block.gpsimd
            def _(pool):
                pool.memset(K["ident"][:], 0.0).then_inc(made, 1)
                pool.memset(K["lower"][:], 1.0).then_inc(made, 1)
                pool.memset(K["ones"][:], 1.0).then_inc(made, 1)
                pool.iota(K["col_i"][:], [[1, P]], base=0, channel_multiplier=0).then_inc(ints, 1)
                pool.iota(K["part_i"][:], [[0, 1]], base=0, channel_multiplier=1).then_inc(ints, 1)
                pool.wait_ge(made, 3)
                pool.affine_select(out=K["ident"][:], in_=K["ident"][:], compare_op=ALU.not_equal, fill=1.0,
                                   base=0, pattern=[[-1, P]], channel_multiplier=1).then_inc(made, 1)
                pool.affine_select(out=K["upper"][:], in_=K["ones"][:], compare_op=ALU.is_gt, fill=0.0,
                                   base=0, pattern=[[-1, P]], channel_multiplier=1).then_inc(made, 1)
                pool.affine_select(out=K["lower"][:], in_=K["ones"][:], compare_op=ALU.is_gt, fill=0.0,
                                   base=0, pattern=[[1, P]], channel_multiplier=-1).then_inc(made, 1)

            @block.vector
            def _(dve):
                dve.wait_ge(ints, 2)
                dve.tensor_copy(K["col"][:], K["col_i"][:])
                dve.tensor_copy(K["part"][:], K["part_i"][:])
                dve.wait_ge(made, 6)
                dve.tensor_copy(K["ident_b"][:], K["ident"][:])
                dve.tensor_copy(K["ones_b"][:], K["ones"][:]).then_inc(cast, 1)
                dve.wait_ge(cast, 1)


class Projections:

    def __init__(self, nc, K, sb, sem, banks, x, w_qkv, b_qkv, h0_d, k_d, v_d, q_sb):
        self.nc, self.K, self.x, self.w_qkv, self.b_qkv = nc, K, x, w_qkv, b_qkv
        self.h0_d, self.k_d, self.v_d, self.q_sb = h0_d, k_d, v_d, q_sb
        self.w_raw, self.w = sb("w_raw", [P, DC, 3 * D]), sb("w", [P, DC, 3 * D])
        self.b_raw, self.b = sb("b_raw", [P, 3 * D]), sb("b", [P, 3 * D])
        self.xb, self.h = sb("xb", [P, 2, GT, D]), sb("h", [P, 2, GT, D])
        self.hT = sb("hT", [P, 2, DC, GT * P])
        self.kv = sb("kv", [P, 2, GT, 2 * D])
        self.stats, self.mv = sb("stats", [P, 2, GT, 6]), sb("mv", [P, 2, GT, 2])
        self.std, self.rstd = sb("std", [P, 2, GT]), sb("rstd", [P, 2, GT])
        self.eps = sb("eps", [P, 1])
        self.pT, self.pQK, self.pV = banks
        self.w_in, self.w_ready, self.x_in = sem("w_in"), sem("w_ready"), [sem(f"x_in{a}") for a in range(2)]
        self.stored = [sem(f"stored{a}") for a in range(2)]
        self.var_ready, self.std_ready, self.h_ready = sem("var_ready"), sem("std_ready"), sem("h_ready")
        self.hT_psum, self.hT_ready = sem("hT_psum"), sem("hT_ready")
        self.qkv_psum, self.qkv_out, self.turns = sem("qkv_psum"), sem("qkv_out"), sem("turns")
        self.tally = Tally(sem("qkv_link"))

    @staticmethod
    def group(k, a):
        known = isinstance(k, int)
        if known and 2 * k + a > NG:
            return None
        return k, a, 1 if known and k == NG // 2 else GT, known and k == 0

    def run(self, eng, tallied, body):
        group = self.group

        def pair(k):
            body(group(k, 0), group(k, 1))
            body(group(k, 1), group(k + 1, 0))

        pair(0)
        with eng.Fori(1, NG // 2 - 1) as k:
            if tallied:
                self.tally.enter(k - 1, 4)
            pair(k)
        if tallied:
            self.tally.leave(NG // 2 - 2)
        pair(NG // 2 - 1)
        body(group(NG // 2, 0), None)

    def rows(self, dram, k, a, nt):
        if nt == 1:
            return dram[NG * GT * P:NG * GT * P + REST, :]
        return dram[0:NG * GT * P, :].rearrange("(g t p) d -> g p t d", t=GT, p=P)[k * 2 + a]

    def load_weights(self, sp):
        sp.dma_start(self.w_raw[:], self.w_qkv.rearrange("(c p) n -> p c n", p=P)).then_inc(self.w_in, 16)
        sp.dma_start(self.b_raw[:], self.b_qkv.unsqueeze(0).to_broadcast([P, 3 * D])).then_inc(self.w_in, 16)

    def load(self, sp, k, a, nt, first):
        if not first:
            sp.wait_ge(self.h_ready, k * 2 + a - 1)
            sp.sem_inc(self.turns)
        to = self.xb[0:REST, a, 0, :] if nt == 1 else self.xb[:, a]
        sp.dma_start(to, self.rows(self.x, k, a, nt)).then_inc(self.x_in[a], 16)

    def store(self, sp, k, a, nt, first):
        sp.wait_ge(self.h_ready, k * 2 + a + 1)
        sp.sem_inc(self.turns)
        sp.wait_ge(self.qkv_out, k * 2 * GT + a * GT + nt)
        sp.sem_inc(self.turns)
        n, t = (REST, 0) if nt == 1 else (P, slice(0, nt))
        for dram, made in ((self.h0_d, self.h[0:n, a, t, :]), (self.k_d, self.kv[0:n, a, t, 0:D]),
                           (self.v_d, self.kv[0:n, a, t, D:2 * D])):
            sp.dma_start(self.rows(dram, k, a, nt), made).then_inc(self.stored[a], 16)

    def all_stored(self, sp):
        sp.wait_ge(self.stored[0], 48 * (NG // 2 + 1))
        sp.wait_ge(self.stored[1], 48 * (NG // 2))

    def begin(self, dve):
        link = linker(dve, self.tally)
        dve.memset(self.eps[:], EPS).then_inc(self.w_ready, 1)
        dve.wait_ge(self.w_in, 32)
        for c in range(DC):
            dve.tensor_copy(self.w[:, c].rearrange("p (s h e) -> p s h e", s=3, h=H),
                            self.w_raw[:, c].rearrange("p (h s e) -> p s h e", s=3, h=H)).then_inc(self.w_ready, 1)
        link(dve.tensor_copy(self.b[:].rearrange("p (s h e) -> p s h e", s=3, h=H),
                             self.b_raw[:].rearrange("p (h s e) -> p s h e", s=3, h=H)))

    def norm(self, dve, k, a, nt, first):
        link = linker(dve, self.tally)
        dve.wait_ge(self.x_in[a], k * 16 + 16)
        for i in range(nt):
            ins = dve.bn_stats(self.stats[:, a, i], self.xb[:, a, i])
        link(ins)
        dve.sem_inc(self.turns)
        for i in range(nt):
            ins = dve.bn_aggr(self.mv[:, a, i], self.stats[:, a, i])
        ins.then_inc(self.var_ready, 1)
        dve.wait_ge(self.std_ready, k * 2 + a + 1)
        link(dve.reciprocal(self.rstd[:, a, 0:nt], self.std[:, a, 0:nt]))
        if not first:
            dve.wait_ge(self.hT_psum, k * 2 + a - 1)
            dve.wait_ge(self.stored[a], k * 48)
        for i in range(nt):
            ins = dve.tensor_scalar(self.h[:, a, i], self.xb[:, a, i], self.mv[:, a, i, 0:1], self.rstd[:, a, i:i + 1],
                                    ALU.subtract, ALU.mult)
        ins.then_inc(self.h_ready, 1)

    def bias(self, dve, k, a, i):
        tile, b, kv = (k * 2 + a) * GT + i, self.b, self.kv
        dve.wait_ge(self.qkv_psum, tile + 1)
        dve.tensor_tensor(self.q_sb[:, tile], self.pQK[i % 2][:, 0:D], b[:, 0:D], ALU.add)
        dve.tensor_tensor(kv[:, a, i, 0:D], self.pQK[i % 2][:, D:2 * D], b[:, D:2 * D], ALU.add)
        dve.tensor_tensor(kv[:, a, i, D:2 * D], self.pV[i % 2][:, 0:D], b[:, 2 * D:3 * D],
                          ALU.add).then_inc(self.qkv_out, 1)

    def root(self, act, k, a, nt, first):
        act.wait_ge(self.var_ready, k * 2 + a + 1)
        act.activation(self.std[:, a, 0:nt], self.mv[:, a, 0:nt, 1], ACT.Sqrt, bias=self.eps[:]).then_inc(self.std_ready, 1)

    def turn(self, act, k, a, nt, first):
        act.wait_ge(self.hT_psum, k * 2 + a + 1)
        if not first:
            act.wait_ge(self.qkv_psum, ((k - 1) * 2 + a + 1) * GT)
        for c in range(DC):
            ins = act.copy(self.hT[:, a, c, 0:nt * P], self.pT[c][:, 0:nt * P])
        ins.then_inc(self.hT_ready, 1)

    def transposes(self, pe, k, a, nt, first):
        pe.wait_ge(self.h_ready, k * 2 + a + 1)
        if not (first and a == 0):
            pe.wait_ge(self.hT_ready, k * 2 + a)
        for c in range(DC):
            for i in range(nt):
                ins = pe.transpose(self.pT[c][:, i * P:(i + 1) * P], self.h[:, a, i, c * P:(c + 1) * P],
                                   self.K["ident"][:])
        ins.then_inc(self.hT_psum, 1)

    def multiply(self, pe, k, a, i, first):
        tile = (k * 2 + a) * GT + i
        if i == 0:
            pe.wait_ge(self.hT_ready, k * 2 + a + 1)
        if not (first and a == 0 and i < 2):
            pe.wait_ge(self.qkv_out, tile - 1)
        for c in range(DC):
            pe.matmul(self.pQK[i % 2][:], self.hT[:, a, c, i * P:(i + 1) * P], self.w[:, c, 0:2 * D],
                      start=c == 0, stop=c == DC - 1)
        for c in range(DC):
            ins = pe.matmul(self.pV[i % 2][:, 0:D], self.hT[:, a, c, i * P:(i + 1) * P], self.w[:, c, 2 * D:3 * D],
                            start=c == 0, stop=c == DC - 1)
        ins.then_inc(self.qkv_psum, 1)


def constants(nc, sb):
    K = {n: sb(f"k_{n}", [P, P]) for n in ("ident", "lower", "upper", "ones", "col")}
    K["part"] = sb("k_part", [P, 1])
    K["col_i"], K["part_i"] = sb("k_col_i", [P, P], I32), sb("k_part_i", [P, 1], I32)
    K["ident_b"], K["ones_b"] = sb("k_ident_b", [P, P], BF16), sb("k_ones_b", [P, P], BF16)
    return K


RING = 4
NB = ET // EB


def sort_steps(eng, tallies, step):
    turns = NB // RING
    for r in range(RING):
        step(0, r, "first")
    with eng.Fori(1, turns - 1) as k:
        for t, per in tallies:
            t.enter(k - 1, per)
        for r in range(RING):
            step(k, r, "middle")
    for t, per in tallies:
        t.leave(turns - 2)
    for r in range(RING):
        step(turns - 1, r, "last")


def stage_sort(nc, K, src, dst, sorted_d, win_d, projections):
    ctx, sb, pb, sem = make_tools(nc)
    with ctx:
        src_i, dst_i = sb("src_i", [EP, ET], I32), sb("dst_i", [EP, ET], I32)
        rec = sb("rec", [EP, ET, 2], I32)
        part_i = sb("part_of_key_i", [EP, 2, ET], I32)
        key_f, lo_f, hi_f = sb("key_f", [EP, ET]), sb("lo_f", [EP, ET]), sb("hi_f", [EP, ET])
        hl_b = sb("hl_b", [EP, ET, 2], BF16)
        ohlo = sb("ohlo", [EP, 2, EB, P], BF16)
        ohhi = sb("ohhi", [EP, RING, EB, NT], BF16)
        Hr = sb("Hr", [P, 2, EB + 1, NT])
        ohtS = sb("ohtS", [P, 2, EB, EP])
        hl_st, rec_st = sb("hl_st", [EP, RING, EB, 2], BF16), sb("rec_st", [EP, RING, EB, 2], I32)
        idx_st = sb("idx_st", [EP, RING, EB], I32)
        rk = sb("rk", [EP, 2, EB])
        same, found = sb("same", [EP, EB, EP], BF16), sb("found", [EP, EB * NT])
        looked = sb("looked", [EP, EB])
        pos_i, hi_pos, lo_pos = sb("pos_i", [EP, EB], I32), sb("hi_pos", [EP, EB], I32), sb("lo_pos", [EP, EB], I32)
        cnt, zero_row = sb("cnt", [P, NT]), sb("zero_row", [P, NT])
        tot, nt_i, nt_f = sb("tot", [P, NT], I32), sb("nt_i", [P, NT], I32), sb("nt_f", [P, NT])
        t_end, t_start, excl = sb("t_end", [P, NT]), sb("t_start", [P, NT]), sb("excl", [P, NT])
        WP = 64
        WJ = ST // WP
        tv_i, tv_f = sb("tv_i", [WP, WJ], I32), sb("tv_f", [WP, WJ])
        past, win_f, win_i = sb("past", [WP, WJ, NT]), sb("win_f", [WP, WJ]), sb("win_i", [WP, WJ], I32)
        pads = sb("pads", [P, ST, 2], I32)
        away, square = sb("away", [EP, 2, EB, NT]), sb("square", [EP, 2, EB, NT])
        cntp = [pb(f"cntp{a}") for a in range(2)]
        oht = [pb(f"oht{a}") for a in range(2)]
        krow = [pb(f"krow{a}") for a in range(2)]
        lk = [pb(f"lk{a}") for a in range(2)]
        HB = EB // 2
        qkv = projections(sb, sem, (oht, krow, (cntp[1], lk[1])))

        def counted_with(k, a, i, nt):
            m = (k * 2 + a) * GT + i
            return range(m, NB // 2) if nt == 1 else [m]

        e_in, rec_made, split = sem("e_in"), sem("rec_made"), sem("split")
        filled, pads_made = sem("filled"), sem("pads_made")
        oh_ready, prefix, tv_made = sem("oh_ready"), sem("prefix"), sem("tv_made")
        win_ready, win_out, dve_link, oh_used = sem("win_ready"), sem("win_out"), sem("dve_link"), sem("oh_used")
        cnt_ready, ohhi_ready = sem("cnt_ready"), sem("ohhi_ready")
        away_made, squared = sem("away_made"), sem("squared")

        def one_hots_lo(eng, t0, a):
            return eng.tensor_tensor(ohlo[:, a], K["col"][0:EP, :].unsqueeze(1).to_broadcast([EP, EB, P]),
                                     lo_f[:, bass.ds(t0, EB)].unsqueeze(2).to_broadcast([EP, EB, P]), ALU.is_equal)

        def windows_and(t0):
            return (K["col"][0:EP, 0:NT].unsqueeze(1).to_broadcast([EP, EB, NT]),
                    hi_f[:, bass.ds(t0, EB)].unsqueeze(2).to_broadcast([EP, EB, NT]))

        def one_hots(dve, t0, a, r):
            one_hots_lo(dve, t0, a)
            return dve.tensor_tensor(ohhi[:, r], *windows_and(t0), ALU.is_equal)

        def slot(m, r, i):
            return 2 * ((m if isinstance(m, int) else i) % 2) + r

        with nc.Block() as block:

            @block.sync
            def _(sp):
                sp.dma_start(src_i[:], src.rearrange("(p t) -> p t", p=EP)).then_inc(e_in, 16)
                sp.dma_start(dst_i[:], dst.rearrange("(p t) -> p t", p=EP)).then_inc(e_in, 16)
                qkv.load_weights(sp)
                sp.wait_ge(pads_made, 2)
                sp.dma_start(sorted_d.rearrange("(p t) c -> p t c", p=P), pads[:]).then_inc(filled, 16)

                def body(group, after):
                    qkv.store(sp, *group)
                    two_on = qkv.group(group[0] + 1, group[1])
                    if two_on:
                        qkv.load(sp, *two_on)

                for a in range(2):
                    qkv.load(sp, *qkv.group(0, a))
                qkv.run(sp, False, body)
                qkv.all_stored(sp)
                sp.wait_ge(win_ready, 1)
                sp.dma_start(win_d.rearrange("(p j) -> p j", p=WP), win_i[:]).then_inc(win_out, 16)
                sp.wait_ge(filled, 16)
                sp.wait_ge(win_out, 16)

            @block.gpsimd
            def _(pool):
                pool.memset(pads[:, :, 0], PAD_KEY).then_inc(pads_made, 1)
                pool.memset(pads[:, :, 1], 0).then_inc(pads_made, 1)
                pool.iota(tv_i[:], [[1, WJ]], base=0, channel_multiplier=WJ).then_inc(tv_made, 1)
                pool.wait_ge(e_in, 32)
                pool.tensor_copy(rec[:, :, 0], src_i[:]).then_inc(rec_made, 1)
                pool.tensor_copy(rec[:, :, 1], dst_i[:]).then_inc(rec_made, 1)
                pool.wait_ge(split, 1)

                def body(group, after):
                    k, a, nt, _ = group
                    for i in range(nt):
                        for m in counted_with(k, a, i, nt):
                            for r in range(2):
                                if not (isinstance(m, int) and m == 0):
                                    pool.wait_ge(ohhi_ready, m * 2 + r - 1)
                                pool.tensor_tensor(away[:, r], *windows_and((m * 2 + r) * EB),
                                                   ALU.subtract).then_inc(away_made, 1)
                                pool.wait_ge(away_made, m * 2 + r + 1)
                                pool.tensor_tensor(square[:, r], away[:, r], away[:, r], ALU.mult).then_inc(squared, 1)

                qkv.run(pool, False, body)

            @block.vector
            def _(dve):
                link = linker(dve, Tally(dve_link))
                dve.wait_ge(e_in, 32)
                dve.tensor_scalar(part_i[:, 0], src_i[:], P - 1, None, ALU.bitwise_and)
                link(dve.tensor_scalar(part_i[:, 1], src_i[:], 7, None, ALU.logical_shift_right))
                dve.tensor_copy(key_f[:], src_i[:])
                dve.tensor_copy(lo_f[:], part_i[:, 0])
                link(dve.tensor_copy(hi_f[:], part_i[:, 1]))
                dve.sem_inc(split)
                dve.tensor_scalar(hl_b[:, :, 0], hi_f[:], float(P), None, ALU.mult)
                link(dve.tensor_copy(hl_b[:, :, 1], lo_f[:]))

                def body(group, after):
                    k, a, nt, _ = group
                    for i in range(nt):
                        if after and i == nt - 1:
                            qkv.norm(dve, *after)
                        for m in counted_with(k, a, i, nt):
                            for r in range(2):
                                if not (isinstance(m, int) and m == 0):
                                    dve.wait_ge(oh_used, m * 2 + r - 1)
                                one_hots_lo(dve, (m * 2 + r) * EB, r).then_inc(oh_ready, 1)
                        qkv.bias(dve, k, a, i)

                qkv.begin(dve)
                qkv.norm(dve, 0, 0, GT, True)
                qkv.run(dve, True, body)
                dve.wait_ge(oh_used, NB)
                dve.tensor_copy(cnt[:], cntp[0][:, 0:NT]).then_inc(cnt_ready, 1)
                link(dve.memset(zero_row[:], 0.0))
                dve.wait_ge(prefix, 1)
                dve.tensor_copy(excl[:], lk[0][:, 0:NT])
                link(dve.tensor_scalar(tot[:], lk[0][:, NT:2 * NT], float(P - 1), None, ALU.add))
                link(dve.tensor_scalar(nt_i[:], tot[:], 7, None, ALU.logical_shift_right))
                link(dve.tensor_copy(nt_f[:], nt_i[:]))
                link(dve.tensor_tensor_scan(t_end[:], zero_row[:], nt_f[:], 0.0, ALU.add, ALU.add))
                link(dve.tensor_tensor(t_start[:], t_end[:], nt_f[:], ALU.subtract))
                dve.scalar_tensor_tensor(Hr[:, 0, 0], t_start[:], float(P), excl[:], ALU.mult, ALU.add)
                dve.wait_ge(tv_made, 1)
                link(dve.tensor_copy(tv_f[:], tv_i[:]))
                link(dve.tensor_tensor(past[:], t_end[0:WP].unsqueeze(1).to_broadcast([WP, WJ, NT]),
                                       tv_f[:].unsqueeze(2).to_broadcast([WP, WJ, NT]), ALU.is_le))
                link(dve.tensor_reduce(win_f[:], past[:], AX.X, ALU.add))
                dve.tensor_scalar(win_i[:], win_f[:], float(NT - 1), None, ALU.min).then_inc(win_ready, 1)

            @block.tensor
            def _(pe):
                def count_pair(m, i):
                    known = isinstance(m, int)
                    for r in range(2):
                        pe.wait_ge(oh_ready, m * 2 + r + 1)
                        pe.wait_ge(ohhi_ready, m * 2 + r + 1)
                        for j in range(EB):
                            ins = pe.matmul(cntp[0][:, 0:NT], ohlo[:, r, j], ohhi[:, slot(m, r, i), j],
                                            start=known and m == 0 and r == 0 and j == 0,
                                            stop=known and m == NB // 2 - 1 and r == 1 and j == EB - 1)
                        ins.then_inc(oh_used, 1)

                def body(group, after):
                    k, a, nt, first = group
                    for i in range(nt):
                        qkv.multiply(pe, k, a, i, first)
                        if after and i == nt - 1:
                            qkv.transposes(pe, *after)
                        for m in counted_with(k, a, i, nt):
                            count_pair(m, i)

                pe.wait_ge(qkv.w_ready, 1 + DC)
                qkv.transposes(pe, 0, 0, GT, True)
                qkv.run(pe, False, body)
                pe.wait_ge(cnt_ready, 1)
                pe.matmul(lk[0][:, 0:NT], K["lower"][:], cnt[:], start=True, stop=True)
                pe.matmul(lk[0][:, NT:2 * NT], K["ones"][:], cnt[:], start=True, stop=True).then_inc(prefix, 1)

            @block.scalar
            def _(act):
                act.wait_ge(qkv.w_ready, 1)

                def body(group, after):
                    k, a, nt, _ = group
                    for i in range(nt):
                        if after and i == nt - 1:
                            qkv.root(act, *after)
                        for m in counted_with(k, a, i, nt):
                            for r in range(2):
                                act.wait_ge(squared, m * 2 + r + 1)
                                if not (isinstance(m, int) and m < 2):
                                    act.wait_ge(oh_used, m * 2 + r - 3)
                                act.activation(ohhi[:, slot(m, r, i)], square[:, r], ACT.Relu,
                                               bias=K["ones"][0:EP, 0:1], scale=-1.0).then_inc(ohhi_ready, 1)
                    if after:
                        qkv.turn(act, *after)

                qkv.root(act, 0, 0, GT, True)
                qkv.turn(act, 0, 0, GT, True)
                qkv.run(act, False, body)

        oh_r, hist, krow_ps, krow_used = sem("oh_r"), sem("hist"), sem("krow_ps"), sem("krow_used")
        H_ready, oht_ready, lk_ps = sem("H_ready"), sem("oht_ready"), sem("lk_ps")
        hl_ready, rec_ready, idx_ready = sem("hl_ready"), sem("rec_ready"), sem("idx_ready")
        scattered = [sem(f"scattered{r}") for r in range(RING)]
        link2, turns = sem("link2"), sem("sort_turns")
        with nc.Block() as block:

            @block.vector
            def _(dve):
                tally = Tally(link2)
                link = linker(dve, tally)

                def ranks(k, r, kind):
                    a, s = r % 2, k * RING + r
                    dve.wait_ge(krow_ps, s + 1)
                    for j in range(EB):
                        ins = dve.scalar_tensor_tensor(
                            same[:, j], krow[j // HB][0:EP, (j % HB) * EP:(j % HB + 1) * EP],
                            key_f[:, bass.ds(s * EB + j, 1)], K["upper"][0:EP, 0:EP], ALU.is_equal, ALU.mult,
                            accum_out=rk[:, a, j:j + 1])
                    ins.then_inc(krow_used, 1)
                    dve.wait_ge(hist, s + 1)
                    if kind != "first" or r >= 1:
                        dve.wait_ge(lk_ps, s)
                    for j in range(EB):
                        to = Hr[:, a, j + 1] if j < EB - 1 else Hr[:, 1 - a, 0]
                        ins = dve.tensor_tensor(to, Hr[:, a, j], cntp[a][:, j * NT:(j + 1) * NT], ALU.add)
                        if j < EB - 1:
                            link(ins)
                    ins.then_inc(H_ready, 1)
                    dve.wait_ge(H_ready, s + 1)

                def places(k, r, kind):
                    a, s = r % 2, k * RING + r
                    dve.wait_ge(lk_ps, s + 1)
                    link(dve.tensor_tensor(found[:], lk[a][0:EP, 0:EB * NT],
                                           ohhi[:, r].rearrange("p j n -> p (j n)"), ALU.mult))
                    link(dve.tensor_reduce(looked[:], found[:].rearrange("p (j n) -> p j n", j=EB), AX.X, ALU.add))
                    link(dve.tensor_tensor(pos_i[:], looked[:], rk[:, a], ALU.add))
                    dve.tensor_scalar(lo_pos[:], pos_i[:], P - 1, None, ALU.bitwise_and)
                    link(dve.tensor_scalar(hi_pos[:], pos_i[:], 7, None, ALU.logical_shift_right))
                    if kind != "first":
                        dve.wait_ge(scattered[r], k * EB * 16)
                    dve.scalar_tensor_tensor(idx_st[:, r], lo_pos[:], float(ST), hi_pos[:], ALU.mult,
                                             ALU.add).then_inc(idx_ready, 1)
                    dve.wait_ge(idx_ready, s + 1)

                per = (EB - 1 + 4) * RING

                def turn(k, kind, back_kind):
                    for r in range(RING):
                        s = k * RING + r
                        if not (kind == "last" and r == RING - 1):
                            if kind != "first" or r >= 1:
                                dve.wait_ge(hist, s)
                            one_hots(dve, (s + 1) * EB, (r + 1) % 2, (r + 1) % RING).then_inc(oh_r, 1)
                        ranks(k, r, kind)
                        if r > 0:
                            places(k, r - 1, kind)
                        elif back_kind:
                            places(k - 1, RING - 1, back_kind)

                one_hots(dve, 0, 0, 0).then_inc(oh_r, 1)
                turn(0, "first", None)
                turn(1, "middle", "first")
                with dve.Fori(2, NB // RING - 1) as k:
                    tally.enter(k - 2, per)
                    turn(k, "middle", "middle")
                tally.leave(NB // RING - 3)
                turn(NB // RING - 1, "last", "middle")
                places(NB // RING - 1, RING - 1, "last")

            @block.tensor
            def _(pe):
                def count(k, r, kind):
                    a, s = r % 2, k * RING + r
                    pe.wait_ge(oh_r, s + 1)
                    if kind != "first" or r >= 2:
                        pe.wait_ge(H_ready, s - 1)
                    if kind != "first" or r >= 1:
                        pe.wait_ge(oht_ready, s)
                    for j in range(EB):
                        pe.matmul(cntp[a][:, j * NT:(j + 1) * NT], ohlo[:, a, j], ohhi[:, r, j], start=True, stop=True)
                        ins = pe.matmul(oht[j // HB][:, (j % HB) * EP:(j % HB + 1) * EP], ohlo[:, a, j],
                                        K["ident_b"][0:EP, 0:EP], start=True, stop=True)
                    ins.then_inc(hist, 1)
                    pe.wait_ge(hl_ready, s + 1)
                    if kind != "first" or r >= 1:
                        pe.wait_ge(krow_used, s)
                    for j in range(EB):
                        for c in range(2):
                            ins = pe.matmul(krow[j // HB][0:EP, (j % HB) * EP:(j % HB + 1) * EP],
                                            hl_st[:, r, j, c:c + 1].to_broadcast([EP, EP]),
                                            K["ident_b"][0:EP, 0:EP], start=c == 0, stop=c == 1)
                    ins.then_inc(krow_ps, 1)

                def look_up(k, r, kind):
                    a, s = r % 2, k * RING + r
                    pe.wait_ge(H_ready, s + 1)
                    pe.wait_ge(oht_ready, s + 1)
                    if kind != "first" or r >= 2:
                        pe.wait_ge(idx_ready, s - 1)
                    for j in range(EB):
                        ins = pe.matmul(lk[a][0:EP, j * NT:(j + 1) * NT], ohtS[:, a, j], Hr[:, a, j],
                                        start=True, stop=True)
                    ins.then_inc(lk_ps, 1)

                def step(k, r, kind):
                    if r < RING - 1:
                        count(k, r + 1, kind)
                    elif kind != "last":
                        count(k + 1, 0, "middle")
                    look_up(k, r, kind)

                count(0, 0, "first")
                sort_steps(pe, [], step)

            @block.scalar
            def _(act):
                def stage_keys(k, r, kind):
                    s = k * RING + r
                    if kind != "first":
                        act.wait_ge(krow_ps, s - RING + 1)
                    act.copy(hl_st[:, r], hl_b[:, bass.ds(s * EB, EB), :]).then_inc(hl_ready, 1)

                def step(k, r, kind):
                    s, a = k * RING + r, r % 2
                    if r < RING - 1:
                        stage_keys(k, r + 1, kind)
                    elif kind != "last":
                        stage_keys(k + 1, 0, "middle")
                    act.wait_ge(hist, s + 1)
                    if kind != "first" or r >= 2:
                        act.wait_ge(lk_ps, s - 1)
                    for b in range(2):
                        ins = act.copy(ohtS[:, a, b * HB:(b + 1) * HB].rearrange("p j e -> p (j e)"),
                                       oht[b][:, 0:HB * EP])
                    ins.then_inc(oht_ready, 1)
                    if kind != "first":
                        act.wait_ge(scattered[r], k * EB * 16)
                    act.copy(rec_st[:, r], rec[:, bass.ds(s * EB, EB), :]).then_inc(rec_ready, 1)

                stage_keys(0, 0, "first")
                sort_steps(act, [], step)

            @block.gpsimd
            def _(pool):
                def step(k, r, kind):
                    s = k * RING + r
                    pool.wait_ge(rec_ready, s + 1)
                    pool.wait_ge(idx_ready, s + 1)
                    pool.sem_inc(turns)
                    for j in range(EB):
                        pool.indirect_dma_start(sorted_d, bass.IndirectOffsetOnAxis(idx_st[:, r, j:j + 1], 0),
                                                rec_st[:, r, j, :], None).then_inc(scattered[r], 16)

                sort_steps(pool, [], step)
                for r in range(RING):
                    pool.wait_ge(scattered[r], 16 * ET // RING)


GB = 4
GR = 4
GN = ST // (GB * GR)


def gather_steps(eng, tallies, step):
    for r in range(GR):
        step(Batch(0, r))
    with eng.Fori(1, GN - 1) as k:
        for t, per in tallies:
            t.enter(k - 1, per)
        for r in range(GR):
            step(Batch(k, r))
    for t, per in tallies:
        t.leave(GN - 2)
    for r in range(GR):
        step(Batch(GN - 1, r))


def windows(nc, engine, table, x):
    _, w = nc.values_load_multi_w_load_instructions(
        table[0:1, bass.ds(x.b * GB, GB)], engines=(engine,), min_val=0, max_val=NT - 1,
        skip_runtime_bounds_check_because="a window's number is below NT as it is made")
    return w


class Batch:

    def __init__(self, k, r):
        self.k, self.r, self.a = k + r // GR, r % GR, r % 2
        self.b = self.k * GR + self.r

    def after(self, d):
        x = Batch(self.k, self.r + d)
        return None if isinstance(x.b, int) and x.b >= GN * GR else x

    def early(self, n):
        return isinstance(self.b, int) and self.b < n


def across(table):
    return table.rearrange("p (g c) -> p c g", c=CH)


NP = NT * P
XT = -(-2 * N // P) + NX
XG = 8
XR = NX * NP + XT * P


def stage_tables(nc, sorted_d, win_d, T, ids_d):
    ctx, sb, pb, sem = make_tools(nc)
    with ctx:
        rec, low_i = sb("rec_s", [P, ST, 2], I32), sb("low_i", [P, ST], I32)
        pad, win_all = sb("pad", [P, ST]), sb("win_all", [P, ST], I32)
        spare = sb("spare", [P, XR // P, 2], I32)
        t_in, dve_link, spare_r, emptied = sem("t_in"), sem("t_link"), sem("spare_r"), sem("emptied")
        with nc.Block() as block:

            @block.sync
            def _(sp):
                sp.dma_start(rec[:], sorted_d.rearrange("(p t) c -> p t c", p=P)).then_inc(t_in, 16)
                sp.dma_start(T["win"][:], win_d.unsqueeze(0)).then_inc(t_in, 16)
                sp.dma_start(win_all[:], win_d.unsqueeze(0).to_broadcast([P, ST])).then_inc(t_in, 16)
                sp.wait_ge(spare_r, 2)
                sp.dma_start(ids_d.rearrange("(p r) c -> p r c", p=P), spare[:]).then_inc(emptied, 16)
                sp.wait_ge(emptied, 16)

            @block.gpsimd
            def _(pool):
                pool.memset(spare[:, :, 0], 0).then_inc(spare_r, 1)
                pool.iota(spare[:, :, 1], [[1, XR // P]], base=2 * N, channel_multiplier=XR // P).then_inc(spare_r, 1)

            @block.vector
            def _(dve):
                link = linker(dve, Tally(dve_link))
                dve.wait_ge(t_in, 48)
                dve.memset(T["keep"][:, 0:1], 0.0)
                dve.tensor_tensor(T["keep"][:, 1:ST], win_all[:, 1:ST], win_all[:, 0:ST - 1], ALU.is_equal)
                dve.tensor_copy(T["key"][:], rec[:, :, 0])
                dve.tensor_copy(T["dst"][:], rec[:, :, 1])
                dve.tensor_copy(across(T["win_x"][:]), T["win"][:].rearrange("p (c g) -> p c g", c=CH))
                link(dve.tensor_scalar(low_i[:], rec[:, :, 0], P - 1, None, ALU.bitwise_and))
                link(dve.tensor_copy(T["lo"][:], low_i[:]))
                link(dve.tensor_scalar(pad[:], T["key"][:], 0.0, NO_LO - (P - 1), ALU.is_lt, ALU.mult))
                link(dve.tensor_tensor(T["lo"][:], T["lo"][:], pad[:], ALU.add))
                for name in ("key", "dst", "lo"):
                    ins = dve.tensor_copy(across(T[name + "_x"][:]), T[name][:].rearrange("p (c g) -> p c g", c=CH))
                link(ins)


def gathers(pool, table, got, idx_st, idx_ready, free, arrived, turns, begun=0):

    def step(x):
        if x.early(begun):
            return
        pool.wait_ge(idx_ready, x.b + 1)
        if not x.early(GR):
            pool.wait_ge(free, x.b - GR + 1)
        pool.sem_inc(turns)
        for j in range(GB):
            pool.indirect_dma_start(got[:, x.r, j, :], None, table,
                                    bass.IndirectOffsetOnAxis(idx_st[:, x.r, j:j + 1], 0)).then_inc(arrived[x.r], 16)

    gather_steps(pool, [], step)
    for r in range(GR):
        pool.wait_ge(arrived[r], 16 * GB * GN)


def stage_scores(nc, K, T, q_sb, k_d, A):
    ctx, sb, pb, sem = make_tools(nc)
    with ctx:
        kg = sb("kg", [P, GR, GB, D])
        idx_st, lo_st = sb("idx_g", [P, GR, GB], I32), sb("lo_st", [P, GR, GB], BF16)
        spread = sb("spread", [P, 2, GB, P])
        prod = sb("prod", [P, 2, GB, D])
        p_lo = [pb(f"p_lo{a}") for a in range(2)]
        p_q = [pb(f"p_q{a}", [P, GB * D]) for a in range(2)]
        idx_ready, arrived, k_used = sem("idx_g_ready"), [sem(f"k_in{r}") for r in range(GR)], sem("k_used")
        lo_ready, lo_psum, spread_ready, q_psum = sem("lo_ready"), sem("lo_psum"), sem("spread_ready"), sem("q_psum")
        summed, turns = sem("summed"), sem("g_turns")

        with nc.Block() as block:

            @block.gpsimd
            def _(pool):
                gathers(pool, k_d, kg, idx_st, idx_ready, k_used, arrived, turns)

            @block.scalar
            def _(act):
                def step(x):
                    if not x.early(GR):
                        act.wait_ge(arrived[x.r], x.k * GB * 16)
                        act.wait_ge(lo_psum, x.b - GR + 1)
                    act.copy(lo_st[:, x.r], T["lo_x"][:, bass.ds(x.b * GB, GB)]).then_inc(lo_ready, 1)
                    act.copy(idx_st[:, x.r], T["dst_x"][:, bass.ds(x.b * GB, GB)]).then_inc(idx_ready, 1)

                gather_steps(act, [], step)

            @block.tensor
            def _(pe):
                def rows(x):
                    pe.wait_ge(lo_ready, x.b + 1)
                    if not x.early(2):
                        pe.wait_ge(spread_ready, x.b - 1)
                    for j in range(GB):
                        ins = pe.matmul(p_lo[x.a][:, j * P:(j + 1) * P], lo_st[:, x.r, j:j + 1].to_broadcast([P, P]),
                                        K["ident_b"][:], start=True, stop=True)
                    ins.then_inc(lo_psum, 1)

                def spreads(x):
                    pe.wait_ge(spread_ready, x.b + 1)
                    if not x.early(2):
                        pe.wait_ge(k_used, x.b - 1)
                    ws = windows(nc, mybir.EngineType.PE, T["win_x"], x)
                    for j, w in enumerate(ws):
                        ins = pe.matmul(p_q[x.a][:, j * D:(j + 1) * D], spread[:, x.a, j],
                                        q_sb[:, bass.ds(w, 1), :].rearrange("p o d -> p (o d)"),
                                        start=True, stop=True)
                    ins.then_inc(q_psum, 1)

                def step(x):
                    if x.after(2):
                        rows(x.after(2))
                    if x.after(1):
                        spreads(x.after(1))

                rows(Batch(0, 0))
                rows(Batch(0, 1))
                spreads(Batch(0, 0))
                gather_steps(pe, [], step)

            @block.vector
            def _(dve):
                def one_hot(x):
                    dve.wait_ge(lo_psum, x.b + 1)
                    if not x.early(2):
                        dve.wait_ge(q_psum, x.b - 1)
                    dve.tensor_scalar(spread[:, x.a].rearrange("p j e -> p (j e)"), p_lo[x.a][:], K["part"][:, 0:1],
                                      None, ALU.is_equal).then_inc(spread_ready, 1)

                def step(x):
                    if x.after(1):
                        one_hot(x.after(1))
                    dve.wait_ge(q_psum, x.b + 1)
                    dve.wait_ge(arrived[x.r], (x.k + 1) * GB * 16)
                    dve.tensor_tensor(prod[:, x.a].rearrange("p j d -> p (j d)"), p_q[x.a][:],
                                      kg[:, x.r].rearrange("p j d -> p (j d)"), ALU.mult).then_inc(k_used, 1)
                    dve.wait_ge(k_used, x.b + 1)
                    dve.tensor_reduce(A[:, bass.ds(x.b * GB, GB), :],
                                      prod[:, x.a].rearrange("p j (h e) -> p j h e", h=H), AX.X,
                                      ALU.add).then_inc(summed, 1)

                one_hot(Batch(0, 0))
                gather_steps(dve, [], step)
                dve.wait_ge(summed, GR * GN)


def stage_softmax(nc, K, T, A, big, v_d, V):
    ctx, sb, pb, sem = make_tools(nc)
    with ctx:
        aT, kT = big[:, 0:CL], sb("kT", [P, CL])
        cut = big[:, CL:2 * CL + 1]
        fwd, top = sb("fwd", [P, CL]), sb("top", [P, CL])
        RW = H * CH
        old = {n: T[n][0:1, :] for n in ("lo_x", "key_x")}
        rows = old["lo_x"][:, 0:4 * RW].rearrange("o (r h c) -> o r h c", r=4, h=H)
        cont, whole = sb("cont", [1, H, CH + 1]), sb("whole", [1, H, CH])
        gate = old["lo_x"][:, 4 * RW:6 * RW].rearrange("o (r h c) -> o r h c", r=2, h=H)
        end, carry = (old["key_x"][:, 2 * i * RW:2 * (i + 1) * RW].rearrange("o (r h c) -> o r h c", r=2, h=H)
                      for i in range(2))
        carry_ch = old["key_x"][:, 4 * RW:6 * RW].rearrange("o (r x) -> o r x", r=2)
        carry_c = sb("carry_c", [P, 2])
        key8 = top[:].rearrange("p (g x) -> p g x", g=SC)
        pt = [pb(f"pt{i}") for i in range(4)]
        pr, pc = pb("pr"), pb("pc")
        t_psum, t_out, link_s = sem("t_psum"), sem("t_out"), sem("link_s")
        k_psum, k_out, rows_psum, rows_ready, edges_ready = (sem("k_psum"), sem("k_out"), sem("rows_psum"),
                                                             sem("rows_ready"), sem("edges_ready"))
        carry_psum, diff_ready, exp_ready = sem("carry_psum"), sem("diff_ready"), sem("exp_ready")
        b_psum, b_out, key8_ready, cut_cleared = sem("b_psum"), sem("b_out"), sem("key8_ready"), sem("cut_cleared")
        A4 = A[:].rearrange("p (c g) h -> p c g h", c=CH)
        Ax = A[:].rearrange("p (g c) h -> p g (c h)", c=CH)
        Q = 4
        QN = SC // Q
        W = Q * P

        with nc.Block() as block:

            @block.tensor
            def _(pe):
                pe.wait_ge(key8_ready, 1)
                for i in range(QN):
                    if i >= 2:
                        pe.wait_ge(t_out, i - 1)
                    for g in range(Q):
                        ins = pe.transpose(pt[i % 2][:, g * P:(g + 1) * P], Ax[:, i * Q + g, :], K["ident"][:])
                    ins.then_inc(t_psum, 1)
                    if i >= 2:
                        pe.wait_ge(k_out, i - 1)
                    for g in range(Q):
                        ins = pe.transpose(pt[2 + i % 2][:, g * P:(g + 1) * P],
                                           key8[:, i * Q + g, :], K["ident"][:])
                    ins.then_inc(k_psum, 1)
                pe.wait_ge(edges_ready, 1)
                for i, col in enumerate((fwd[:, CL - 1:CL], top[:, 0:1], kT[:, 0:1], kT[:, CL - 1:CL])):
                    ins = pe.matmul(pr[0:1, i * P:(i + 1) * P], col, K["ident"][:], start=True, stop=True)
                ins.then_inc(rows_psum, 1)
                pe.wait_ge(rows_ready, 1)
                for i in range(2):
                    ins = pe.matmul(pc[:, i:i + 1], carry_ch[0:1, i, :], K["ones"][0:1, 0:1], start=True, stop=True)
                ins.then_inc(carry_psum, 1)
                for i in range(QN):
                    pe.wait_ge(exp_ready, i + 1)
                    if i >= 4:
                        pe.wait_ge(b_out, i - 3)
                    for g in range(Q):
                        ins = pe.transpose(pt[i % 4][:, g * P:(g + 1) * P], aT[:, (i * Q + g) * P:(i * Q + g + 1) * P],
                                           K["ident"][:])
                    ins.then_inc(b_psum, 1)

            @block.gpsimd
            def _(pool):
                for x in (Batch(0, r) for r in range(GR)):
                    pool.wait_ge(V["idx_ready"], x.b + 1)
                    for j in range(GB):
                        pool.indirect_dma_start(V["rows"][:, x.r, j, :], None, v_d,
                                                bass.IndirectOffsetOnAxis(V["idx"][:, x.r, j:j + 1], 0)
                                                ).then_inc(V["arrived"][x.r], 16)
                pool.wait_ge(diff_ready, 1)
                pool.memset(cut, 0.0).then_inc(cut_cleared, 1)
                pool.wait_ge(cut_cleared, 1)
                for r in range(GR):
                    pool.wait_ge(V["arrived"][r], GB * 16)

            @block.scalar
            def _(act):
                for x in (Batch(0, r) for r in range(GR)):
                    act.copy(V["idx"][:, x.r], T["dst"][:, x.b * GB:(x.b + 1) * GB]).then_inc(V["idx_ready"], 1)
                for i in range(QN):
                    act.wait_ge(t_psum, i + 1)
                    act.copy(aT[:, i * W:(i + 1) * W], pt[i % 2][:]).then_inc(t_out, 1)
                for i in range(QN):
                    act.wait_ge(diff_ready, i + 1)
                    act.activation(aT[:, i * W:(i + 1) * W], fwd[:, i * W:(i + 1) * W], ACT.Exp,
                                   scale=SCALE).then_inc(exp_ready, 1)

            @block.vector
            def _(dve):
                link = linker(dve, Tally(link_s))
                dve.tensor_copy(top[:].rearrange("p (t h) -> p t h", h=H),
                                T["key_x"][:].unsqueeze(2).to_broadcast([P, ST, H])).then_inc(key8_ready, 1)
                for i in range(QN):
                    dve.wait_ge(k_psum, i + 1)
                    dve.tensor_copy(kT[:, i * W:(i + 1) * W], pt[2 + i % 2][:]).then_inc(k_out, 1)
                dve.wait_ge(k_out, QN)
                dve.memset(cut[:, 0:1], 0.0)
                dve.memset(cut[:, CL:CL + 1], 0.0)
                link(dve.tensor_tensor(cut[:, 1:CL], kT[:, 1:CL], kT[:, 0:CL - 1], ALU.not_equal))
                link(dve.tensor_scalar(cut[:, 1:CL], cut[:, 1:CL], LOW, None, ALU.mult))
                dve.wait_ge(t_out, QN)
                dve.tensor_tensor_scan(fwd[:], cut[:, 0:CL], aT[:], LOW, ALU.add, ALU.max)
                dve.tensor_tensor_scan(top[:, ::-1], cut[:, 1:CL + 1][:, ::-1], aT[:, ::-1], LOW, ALU.add,
                                       ALU.max).then_inc(edges_ready, 1)
                dve.wait_ge(rows_psum, 1)
                link(dve.tensor_copy(rows[:], pr[0:1, 0:4 * P].rearrange("o (r c h) -> o r h c", r=4, h=H)))
                link(dve.memset(cont[:], 0.0))
                dve.tensor_tensor(cont[:, :, 1:CH], rows[:, 2, :, 1:CH], rows[:, 3, :, 0:CH - 1], ALU.is_equal)
                link(dve.tensor_tensor(whole[:], rows[:, 2], rows[:, 3], ALU.is_equal))
                dve.tensor_tensor(gate[:, 0], whole[:], cont[:, :, 0:CH], ALU.mult)
                link(dve.tensor_tensor(gate[:, 1], whole[:], cont[:, :, 1:CH + 1], ALU.mult))
                link(dve.tensor_scalar(gate[:], gate[:], 1.0, -LOW, ALU.subtract, ALU.mult))
                flat = [x.rearrange("o h c -> o (h c)") for x in
                        (gate[:, 0], rows[:, 0], end[:, 0], gate[:, 1], rows[:, 1], end[:, 1])]
                dve.tensor_tensor_scan(flat[2], flat[0], flat[1], LOW, ALU.add, ALU.max)
                link(dve.tensor_tensor_scan(flat[5][:, ::-1], flat[3][:, ::-1], flat[4][:, ::-1], LOW, ALU.add,
                                            ALU.max))
                link(dve.tensor_scalar(cont[:], cont[:], 1.0, -LOW, ALU.subtract, ALU.mult))
                dve.memset(carry[:, 0, :, 0:1], LOW)
                dve.memset(carry[:, 1, :, CH - 1:CH], LOW)
                dve.tensor_tensor(carry[:, 0, :, 1:CH], end[:, 0, :, 0:CH - 1], cont[:, :, 1:CH], ALU.add)
                link(dve.tensor_tensor(carry[:, 1, :, 0:CH - 1], end[:, 1, :, 1:CH], cont[:, :, 1:CH], ALU.add))
                dve.tensor_copy(carry_ch[:].rearrange("o r (c h) -> o r h c", h=H), carry[:]).then_inc(rows_ready, 1)
                dve.wait_ge(carry_psum, 1)
                link(dve.tensor_copy(carry_c[:], pc[:, 0:2]))
                link(dve.tensor_tensor_scan(fwd[:], cut[:, 0:CL], aT[:], carry_c[:, 0:1], ALU.add, ALU.max))
                link(dve.tensor_tensor_scan(top[:, ::-1], cut[:, 1:CL + 1][:, ::-1], fwd[:, ::-1], carry_c[:, 1:2],
                                            ALU.add, ALU.max))
                for i in range(QN):
                    s = slice(i * W, (i + 1) * W)
                    dve.tensor_tensor(fwd[:, s], aT[:, s], top[:, s], ALU.subtract).then_inc(diff_ready, 1)
                for i in range(QN):
                    dve.wait_ge(b_psum, i + 1)
                    dve.tensor_copy(A4[:, :, i * Q:(i + 1) * Q, :].rearrange("p c g h -> p g c h"),
                                    pt[i % 4][:].rearrange("p (g c h) -> p g c h", g=Q, h=H)).then_inc(b_out, 1)
                dve.wait_ge(b_out, QN)


def stage_sums(nc, K, T, A, v_d, V, acc):
    DX = D + H
    ctx, sb, pb, sem = make_tools(nc)
    with ctx:
        vg, idx_st, idx_ready, arrived = V["rows"], V["idx"], V["idx_ready"], V["arrived"]
        pick = sb("pick", [P, 2, GB, P])
        wv = sb("wv", [P, 2, GB, DX])
        run = sb("run", [P, 2, GB, DX])
        p_s = [[pb(f"p_s{a}{j}") for j in range(GB)] for a in range(2)]
        v_used, kept = sem("v_used"), sem("kept")
        w_ready, s_psum, added, cleared, turns = (sem("wcol_ready"), sem("s_psum"), sem("added"), sem("cleared"),
                                                  sem("v_turns"))
        with nc.Block() as block:

            @block.gpsimd
            def _(pool):
                gathers(pool, v_d, vg, idx_st, idx_ready, v_used, arrived, turns, begun=GR)

            @block.scalar
            def _(act):
                def targets(x):
                    if not x.early(GR):
                        act.wait_ge(arrived[x.r], x.k * GB * 16)
                    act.copy(idx_st[:, x.r], T["dst"][:, bass.ds(x.b * GB, GB)]).then_inc(idx_ready, 1)

                def weights(x):
                    if not x.early(2):
                        act.wait_ge(s_psum, x.b - 1)
                    act.copy(wv[:, x.a, :, D:DX], A[:, bass.ds(x.b * GB, GB), :]).then_inc(w_ready, 1)

                def step(x):
                    if x.after(GR):
                        targets(x.after(GR))
                    if not x.early(1):
                        place(x.after(-1))
                    if x.after(2):
                        weights(x.after(2))

                def place(x):
                    if x.early(1):
                        act.wait_ge(cleared, 2)
                    ws = windows(nc, mybir.EngineType.Activation, T["win"], x)
                    for j, w in enumerate(ws):
                        act.wait_ge(added, x.b * GB + j + 1)
                        if j == 0 and not x.early(1):
                            act.wait_ge(kept, x.b * GB)
                        elif j:
                            act.wait_ge(kept, x.b * GB + j)
                        act.copy(acc[:, bass.ds(w, 1), :].rearrange("p o d -> p (o d)"), run[:, x.a, j]).then_inc(kept, 1)

                for i in range(2):
                    weights(Batch(0, i))
                gather_steps(act, [], step)
                place(Batch(GN - 1, GR - 1))
                act.wait_ge(kept, ST)

            @block.tensor
            def _(pe):
                def step(x):
                    pe.wait_ge(w_ready, x.b + 1)
                    pe.wait_ge(v_used, x.b + 1)
                    if not x.early(2):
                        pe.wait_ge(added, (x.b - 1) * GB)
                    for j in range(GB):
                        ins = pe.matmul(p_s[x.a][j][:, 0:DX], pick[:, x.a, j], wv[:, x.a, j], start=True, stop=True)
                    ins.then_inc(s_psum, 1)

                gather_steps(pe, [], step)

            @block.vector
            def _(dve):
                def pick_slots(x):
                    if not x.early(2):
                        dve.wait_ge(s_psum, x.b - 1)
                    dve.tensor_tensor(pick[:, x.a], K["col"][:].unsqueeze(1).to_broadcast([P, GB, P]),
                                      T["lo"][:, bass.ds(x.b * GB, GB)].unsqueeze(2).to_broadcast([P, GB, P]),
                                      ALU.is_equal)

                def weigh(x):
                    dve.wait_ge(arrived[x.r], (x.k + 1) * GB * 16)
                    dve.tensor_tensor(wv[:, x.a, :, 0:D].rearrange("p j (h e) -> p j h e", h=H),
                                      vg[:, x.r].rearrange("p j (h e) -> p j h e", h=H),
                                      A[:, bass.ds(x.b * GB, GB), :].unsqueeze(3).to_broadcast([P, GB, H, HD]),
                                      ALU.mult).then_inc(v_used, 1)

                def add(x, j):
                    if j == 0:
                        dve.wait_ge(s_psum, x.b + 1)
                        if not x.early(2):
                            dve.wait_ge(kept, (x.b - 1) * GB)
                    if j or not x.early(1):
                        dve.wait_ge(added, x.b * GB + j)
                    last = run[:, x.a, j - 1] if j else run[:, 1 - x.a, GB - 1]
                    dve.scalar_tensor_tensor(run[:, x.a, j], last, T["keep"][:, bass.ds(x.b * GB + j, 1)],
                                             p_s[x.a][j][:, 0:DX], ALU.mult, ALU.add).then_inc(added, 1)

                def step(x):
                    ahead = x.after(2)
                    for j in range(GB):
                        add(x, j)
                        if ahead and j == 0:
                            pick_slots(ahead)
                        if ahead and j == 1:
                            weigh(ahead)

                for i in range(2):
                    pick_slots(Batch(0, i))
                    weigh(Batch(0, i))
                dve.memset(run[:], 0.0).then_inc(cleared, 1)
                dve.memset(acc[:].rearrange("p t d -> p (t d)")[:, 0:CL], 0.0).then_inc(cleared, 1)
                dve.wait_ge(cleared, 2)
                gather_steps(dve, [], step)


def stage_front(nc, K, A_in, acc, h0_d, n_d, ids_d, R):
    FB = F // P
    G = GT * P
    ctx, sb, pb, sem = make_tools(nc)
    with ctx:
        w1, w2 = sb("w1", [P, DC, F]), sb("w2", [P, FB, D])
        gw, gb = sb("gw", [P, DC, NX]), sb("gb", [P, NX])
        b1c = sb("b1c", [P, FB])
        vec = sb("vec", [P, 5, D])
        xin, hin = sb("xin", [P, GT, D]), sb("hin", [P, GT, D])
        y1 = sb("y1", [P, 2, GT, D])
        nb = sb("nb", [P, GT, D])
        y1T, nT = sb("y1T", [P, DC, G]), sb("nT", [P, DC, G])
        h1T = sb("h1T", [P, FB, G])
        rden = sb("rden", [P, GT, H])
        stats, mv, std, rstd = sb("d_stats", [P, GT, 6]), sb("d_mv", [P, GT, 2]), sb("d_std", [P, GT]), sb("d_rstd", [P, GT])
        eps, warm = sb("d_eps", [P, 1]), sb("warm", [P, 1])
        lg, ex, pr = sb("lg", [P, GT, NX]), sb("ex", [P, GT, NX]), sb("pr_x", [P, GT, NX])
        top, tot = sb("top_x", [P, GT]), sb("tot_x", [P, GT])
        more, equal, rank = sb("more", [P, GT, NX, NX]), sb("equal", [P, GT, NX, NX]), sb("rank", [P, GT, NX])
        before = sb("before", [P, NX, NX])
        sel, both = sb("sel", [P, 2, GT, NX]), sb("both", [P, GT, NX])
        spot, mine = sb("spot", [P, GT, NX]), sb("mine", [P, GT, NX])
        slot_f = sb("slot_f", [P, GT])
        slot_st, id_st = sb("slot_st", [P, 2, GT, 2], I32), sb("id_st", [P, 2, GT, 4], I32)
        ids = sb("ids", [P, NT, 4], I32)
        room_i = sb("room_i", [P, NX], I32)
        p_up = [pb(f"p_up{i}") for i in range(2)]
        p_dn = pb("p_dn", [P, GT * D])
        p_t = [pb(f"p_t{i}") for i in range(DC)]
        p_g, p_r = pb("p_g"), pb("p_r")

        vec_in, warmed = sem("dvec_in"), sem("warmed")
        w_in, consts, iotas = sem("dw_in"), sem("dconsts"), sem("iotas")
        x_in, h_in = sem("fx_in"), sem("fh_in")
        var_r, std_r = [sem(f"var{i}") for i in range(3)], [sem(f"std{i}") for i in range(3)]
        h_used, y1_r, dn_used, x_used, n_r = sem("h_used"), sem("y1_r"), sem("dn_used"), sem("x_used"), sem("n_r")
        t_ps, t_out = [sem(f"dt_ps{i}") for i in range(2)], [sem(f"dt_out{i}") for i in range(2)]
        up_ps, up_out, dn_ps = sem("up_ps"), sem("up_out"), sem("dn_ps")
        lg_ps, lg_r, ex_r, sel_r, rk_ps, rk_used = (sem("lg_ps"), sem("lg_r"), sem("ex_r"), sem("sel_r"), sem("rk_ps"),
                                                    sem("rk_used"))
        slots_r, ids_r, listed, stored = (sem("slots_r"), sem("ids_r"), [sem(f"listed{a}") for a in range(2)],
                                          sem("n_stored"))
        dl, turns = sem("dl"), sem("d_turns")

        class At:

            def __init__(self, k, a):
                self.k, self.a = k + a // 2, a % 2
                self.g = self.k * 2 + self.a
                self.known = isinstance(self.g, int)
                self.nt = 1 if self.known and self.g == NG else GT
                self.n = self.nt * P

            def step(self, d):
                x = At(self.k, self.a + d)
                return None if x.known and not 0 <= x.g <= NG else x

            def early(self, n):
                return self.known and self.g < n

        def run(eng, tallies, begin, turn, end):
            begin(At(0, 0))
            for g in range(4):
                turn(At(0, g))
            last = NG // 2 - 1
            with eng.Fori(2, last) as k:
                for t, per in tallies:
                    t.enter(k - 2, per)
                turn(At(k, 0))
                turn(At(k, 1))
            for t, per in tallies:
                t.leave(last - 2)
            for a in range(3):
                turn(At(last, a))
            end(At(last, 2))

        def rows(dram, q):
            if q.nt == 1:
                return dram[NG * G:NG * G + REST, :]
            return dram[0:NG * G, :].rearrange("(g t p) d -> g p t d", t=GT, p=P)[q.g]

        def part(q, buf):
            return buf[0:REST, 0, :] if q.nt == 1 else buf

        with nc.Block() as block:

            @block.sync
            def _(sp):
                def col(v):
                    return v.rearrange("(b p) -> p b", p=P)

                def row(v):
                    return v.unsqueeze(0).to_broadcast([P, v.shape[0]])

                def load_h(q):
                    if not q.early(1):
                        sp.wait_ge(h_used, q.g)
                        sp.sem_inc(turns)
                    sp.dma_start(part(q, hin[:]), rows(h0_d, q)).then_inc(h_in, 16)

                def load_x(q):
                    if not q.early(1):
                        sp.wait_ge(x_used, q.g)
                        sp.sem_inc(turns)
                    sp.dma_start(part(q, xin[:]), rows(A_in["x"], q)).then_inc(x_in, 16)

                def store(q):
                    sp.wait_ge(n_r, q.g + 1)
                    sp.sem_inc(turns)
                    sp.dma_start(rows(n_d, q), part(q, nb[:])).then_inc(stored, 16)

                def begin(q):
                    load_h(q)
                    for i, name in enumerate(("ln1_g", "ln1_b", "ln2_g", "ln2_b", "b2")):
                        sp.dma_start(vec[:, i], row(A_in["L0_gnn_" + name])).then_inc(vec_in, 16)
                    sp.dma_start(gb[:], row(A_in["L0_ffn_gate_b"])).then_inc(vec_in, 16)
                    load_x(q)
                    with nc.allow_non_contiguous_dma(reason="biases by partition, once"):
                        sp.dma_start(b1c[:], col(A_in["L0_gnn_b1"])).then_inc(w_in, 16)
                    sp.dma_start(w1[:], A_in["L0_gnn_w1"].rearrange("(c p) f -> p c f", p=P)).then_inc(w_in, 16)
                    sp.dma_start(w2[:], A_in["L0_gnn_w2"].rearrange("(c p) f -> p c f", p=P)).then_inc(w_in, 16)
                    sp.dma_start(gw[:], A_in["L0_ffn_gate_w"].rearrange("(c p) f -> p c f", p=P)).then_inc(w_in, 16)
                    sp.dma_start(R["b1"][:], A_in["L0_ffn_b1"].unsqueeze(0).to_broadcast([P, NX, FX])).then_inc(R["in"], 16)

                def expert_weights(e):
                    sp.dma_start(R["w1"][:, e], A_in["L0_ffn_W1"][e].rearrange("(c p) f -> p c f", p=P)).then_inc(R["in"], 16)
                    sp.dma_start(R["w2"][:, e], A_in["L0_ffn_W2"][e].rearrange("(c p) f -> p c f", p=P)).then_inc(R["in"], 16)

                def turn(q):
                    if q.step(1):
                        load_h(q.step(1))
                    if not q.early(1):
                        load_x(q)
                        store(q.step(-1))
                    if q.early(4):
                        for e in range(NX // 4 * q.g, NX // 4 * (q.g + 1)):
                            expert_weights(e)

                run(sp, [], begin, turn, store)
                sp.wait_ge(stored, 16 * (NG + 1))
                sp.wait_ge(R["in"], 32 * NX + 16)

            W_ALL, VEC_ALL = 16 * 4, 16 * 6

            @block.gpsimd
            def _(pool):
                for j in range(2):
                    pool.iota(ids[:, :, 2 * j], [[P, NT]], base=0, channel_multiplier=1).then_inc(iotas, 1)
                    pool.iota(ids[:, :, 2 * j + 1], [[2 * P, NT]], base=j, channel_multiplier=2).then_inc(iotas, 1)
                pool.iota(room_i[:], [[NP, NX]], base=0, channel_multiplier=0).then_inc(iotas, 1)

                def list_nodes(q):
                    pool.wait_ge(slots_r, q.g + 1)
                    pool.wait_ge(ids_r, q.g + 1)
                    pool.sem_inc(turns)
                    n = REST if q.nt == 1 else P
                    for t in range(q.nt):
                        for j in range(2):
                            pool.indirect_dma_start(ids_d, bass.IndirectOffsetOnAxis(slot_st[0:n, q.a, t, j:j + 1], 0),
                                                    id_st[0:n, q.a, t, 2 * j:2 * j + 2], None).then_inc(listed[q.a], 16)

                def end(q):
                    list_nodes(q.step(-1))
                    list_nodes(q)

                run(pool, [], lambda q: None, lambda q: q.step(-2) and list_nodes(q.step(-2)), end)
                pool.wait_ge(listed[0], 16 * 2 * (GT * NG // 2 + 1))
                pool.wait_ge(listed[1], 16 * 2 * (GT * NG // 2))

            @block.vector
            def _(dve):
                t_l = Tally(dl)
                link = linker(dve, t_l)

                def wide(i, nt):
                    return vec[:, i].unsqueeze(1).to_broadcast([P, nt, D])

                def norm_in(src, nt, which):
                    for i in range(nt):
                        ins = dve.bn_stats(stats[:, i], src[:, i])
                    link(ins)
                    dve.sem_inc(turns)
                    for i in range(nt):
                        ins = dve.bn_aggr(mv[:, i], stats[:, i])
                    ins.then_inc(var_r[which], 1)

                def norm_out(dst, src, q, which):
                    dve.wait_ge(std_r[which], q.g + 1)
                    link(dve.reciprocal(rstd[:, 0:q.nt], std[:, 0:q.nt]))
                    for i in range(q.nt):
                        ins = dve.tensor_scalar(dst[:, i], src[:, i], mv[:, i, 0:1], rstd[:, i:i + 1], ALU.subtract,
                                                ALU.mult)
                    return ins

                def attention(q):
                    nt = q.nt
                    dve.wait_ge(h_in, q.g * 16 + 16)
                    av = acc[:, bass.ds(q.g * GT, nt), :]
                    link(dve.tensor_scalar(rden[:, 0:nt], av[:, :, D:D + H], 1e-30, None, ALU.max))
                    link(dve.reciprocal(rden[:, 0:nt], rden[:, 0:nt]))
                    if not q.early(2):
                        dve.wait_ge(n_r, q.g - 1)
                    yv = y1[:, q.a, 0:nt]
                    link(dve.tensor_tensor(yv.rearrange("p t (h e) -> p t h e", h=H),
                                           av[:, :, 0:D].rearrange("p t (h e) -> p t h e", h=H),
                                           rden[:, 0:nt].unsqueeze(3).to_broadcast([P, nt, H, HD]), ALU.mult))
                    dve.tensor_tensor(yv, yv, hin[:, 0:nt], ALU.add).then_inc(h_used, 1)
                    dve.wait_ge(h_used, q.g + 1)
                    norm_in(y1[:, q.a], nt, 0)

                def first_norm(q):
                    yv = y1[:, q.a, 0:q.nt]
                    link(norm_out(y1[:, q.a], y1[:, q.a], q, 0))
                    link(dve.tensor_tensor(yv, yv, wide(0, q.nt), ALU.mult))
                    dve.tensor_tensor(yv, yv, wide(1, q.nt), ALU.add).then_inc(y1_r, 1)

                def after_ffn(q):
                    yv = y1[:, q.a, 0:q.nt]
                    dve.wait_ge(dn_ps, q.g + 1)
                    dve.wait_ge(t_ps[0], q.g + 1)
                    dve.wait_ge(y1_r, q.g + 1)
                    dve.tensor_tensor(yv.rearrange("p t d -> p (t d)"), p_dn[:, 0:q.nt * D],
                                      yv.rearrange("p t d -> p (t d)"), ALU.add).then_inc(dn_used, 1)
                    dve.wait_ge(dn_used, q.g + 1)
                    link(dve.tensor_tensor(yv, yv, wide(4, q.nt), ALU.add))
                    norm_in(y1[:, q.a], q.nt, 1)

                def residual(q):
                    nt = q.nt
                    yv, xv = y1[:, q.a, 0:nt], acc[:, bass.ds(q.g * GT, nt), 0:D]
                    link(norm_out(y1[:, q.a], y1[:, q.a], q, 1))
                    link(dve.tensor_tensor(yv, yv, wide(2, nt), ALU.mult))
                    link(dve.tensor_tensor(yv, yv, wide(3, nt), ALU.add))
                    dve.wait_ge(x_in, q.g * 16 + 16)
                    dve.tensor_tensor(yv, yv, xin[:, 0:nt], ALU.add).then_inc(x_used, 1)
                    dve.wait_ge(x_used, q.g + 1)
                    dve.tensor_copy(xv, yv)
                    norm_in(y1[:, q.a], nt, 2)

                def normal(q):
                    if not q.early(1):
                        dve.wait_ge(t_ps[1], q.g)
                        dve.wait_ge(stored, q.g * 16)
                    norm_out(nb, y1[:, q.a], q, 2).then_inc(n_r, 1)

                def gate(q):
                    nt = q.nt
                    dve.wait_ge(lg_ps, q.g + 1)
                    lv = lg[:, 0:nt]
                    link(dve.tensor_tensor(lv, p_g[:, 0:nt * NX].rearrange("p (t e) -> p t e", e=NX),
                                           gb[:].unsqueeze(1).to_broadcast([P, nt, NX]), ALU.add))
                    link(dve.tensor_reduce(top[:, 0:nt], lv, AX.X, ALU.max))
                    dve.tensor_tensor(lv, lv, top[:, 0:nt].unsqueeze(2).to_broadcast([P, nt, NX]),
                                      ALU.subtract).then_inc(lg_r, 1)

                def choose(q):
                    nt = q.nt
                    dve.wait_ge(ex_r, q.g + 1)
                    pv = pr[:, 0:nt]
                    link(dve.tensor_reduce(tot[:, 0:nt], ex[:, 0:nt], AX.X, ALU.add))
                    link(dve.reciprocal(tot[:, 0:nt], tot[:, 0:nt]))
                    link(dve.tensor_tensor(pv, ex[:, 0:nt], tot[:, 0:nt].unsqueeze(2).to_broadcast([P, nt, NX]),
                                           ALU.mult))
                    for t in range(nt):
                        own = pr[:, t].unsqueeze(2).to_broadcast([P, NX, NX])
                        other = pr[:, t].unsqueeze(1).to_broadcast([P, NX, NX])
                        dve.tensor_tensor(more[:, t], other, own, ALU.is_gt)
                        ins = dve.tensor_tensor(equal[:, t], other, own, ALU.is_equal)
                    link(ins)
                    mv_, ev = more[:, 0:nt].rearrange("p t j i -> p t (j i)"), equal[:, 0:nt].rearrange("p t j i -> p t (j i)")
                    link(dve.tensor_tensor(ev, ev, before[:].rearrange("p j i -> p (j i)").unsqueeze(1)
                                           .to_broadcast([P, nt, NX * NX]), ALU.mult))
                    link(dve.tensor_tensor(mv_, mv_, ev, ALU.add))
                    link(dve.tensor_reduce(rank[:, 0:nt], more[:, 0:nt], AX.X, ALU.add))
                    if not q.early(1):
                        dve.wait_ge(rk_ps, q.g)
                    for j in range(2):
                        dve.tensor_scalar(sel[:, j, 0:nt], rank[:, 0:nt], float(j), None, ALU.is_equal)
                    ins = dve.tensor_scalar(both[:, 0:nt], rank[:, 0:nt], 2.0, None, ALU.is_lt)
                    ins.then_inc(sel_r, 1)
                    dve.wait_ge(sel_r, q.g + 1)
                    for j in range(2):
                        link(dve.tensor_tensor(mine[:, 0:nt], sel[:, j, 0:nt], pv, ALU.mult))
                        link(dve.tensor_reduce(R["share"][:, bass.ds(q.g * GT, nt), j], mine[:, 0:nt], AX.X, ALU.add))

                def places(q):
                    nt = q.nt
                    dve.wait_ge(rk_ps, q.g + 1)
                    for t in range(nt):
                        dve.tensor_tensor(spot[:, t], p_r[:, t * NX:(t + 1) * NX], R["taken"][:], ALU.add)
                        link(dve.tensor_tensor(R["taken"][:], p_r[:, (GT + t) * NX:(GT + t + 1) * NX], R["taken"][:],
                                               ALU.add))
                    dve.sem_inc(rk_used)
                    if not q.early(2):
                        dve.wait_ge(listed[q.a], q.k * (2 * GT * 16))
                    for j in range(2):
                        link(dve.tensor_tensor(mine[:, 0:nt], sel[:, j, 0:nt], spot[:, 0:nt], ALU.mult))
                        link(dve.tensor_reduce(slot_f[:, 0:nt], mine[:, 0:nt], AX.X, ALU.add))
                        link(dve.tensor_copy(slot_st[:, q.a, 0:nt, j], slot_f[:, 0:nt]))
                    dve.sem_inc(slots_r)

                def begin(q):
                    dve.memset(eps[:], EPS).then_inc(consts, 1)
                    dve.tensor_tensor(before[:], K["col"][:, 0:NX].unsqueeze(1).to_broadcast([P, NX, NX]),
                                      K["col"][:, 0:NX].unsqueeze(2).to_broadcast([P, NX, NX]),
                                      ALU.is_lt).then_inc(consts, 1)
                    dve.wait_ge(iotas, 5)
                    link(dve.tensor_copy(R["taken"][:], room_i[:]))
                    dve.wait_ge(vec_in, VEC_ALL)
                    attention(q)
                    first_norm(q)

                def finish_norms(q):
                    after_ffn(q)
                    residual(q)
                    normal(q)

                def turn(q):
                    pv, nx = q.step(-1), q.step(1)
                    if pv:
                        finish_norms(pv)
                    if q.step(-2):
                        places(q.step(-2))
                    if nx:
                        attention(nx)
                    if pv:
                        gate(pv)
                    if nx:
                        first_norm(nx)
                    if pv:
                        choose(pv)

                def end(q):
                    finish_norms(q)
                    places(q.step(-1))
                    gate(q)
                    choose(q)
                    places(q)

                per_group = 3 + 1 + 1 + 2 + 2 + 3 + 1 + 1 + 2 + 7 + 4 + GT + 7
                run(dve, [(t_l, 2 * per_group)], begin, turn, end)

            @block.scalar
            def _(act):
                t_up = Tally(up_out)

                def root(q, which):
                    act.wait_ge(var_r[which], q.g + 1)
                    act.activation(std[:, 0:q.nt], mv[:, 0:q.nt, 1], ACT.Sqrt, bias=eps[:]).then_inc(std_r[which], 1)

                def relus(q, blocks):
                    if not q.early(1):
                        act.wait_ge(dn_ps, q.g)
                    for b in blocks:
                        i = t_up.n % 2
                        t_up.n += 1
                        act.wait_ge(up_ps, t_up.value())
                        act.activation(h1T[:, b, 0:q.n], p_up[i][:, 0:q.n], ACT.Relu, bias=b1c[:, b:b + 1]).then_inc(up_out, 1)

                def turned(q, which, dst):
                    act.wait_ge(t_ps[which], q.g + 1)
                    for c in range(DC):
                        ins = act.copy(dst[:, c, 0:q.n], p_t[c][:, 0:q.n])
                    ins.then_inc(t_out[which], 1)

                def n_turned(q):
                    if not q.early(1):
                        act.wait_ge(lg_ps, q.g)
                    turned(q, 1, nT)

                def exps(q):
                    act.wait_ge(lg_r, q.g + 1)
                    act.activation(ex[:, 0:q.nt], lg[:, 0:q.nt], ACT.Exp).then_inc(ex_r, 1)
                    if not q.early(2):
                        act.wait_ge(listed[q.a], q.k * (2 * GT * 16))
                    act.copy(id_st[:, q.a, 0:q.nt], ids[:, bass.ds(q.g * GT, q.nt)]).then_inc(ids_r, 1)

                def begin(q):
                    act.wait_ge(consts, 2)
                    act.wait_ge(iotas, 5)
                    root(q, 0)
                    turned(q, 0, y1T)
                    act.wait_ge(w_in, W_ALL)

                def turn(q):
                    pv, nx = q.step(-1), q.step(1)
                    relus(q, range(FB // 4))
                    if pv:
                        root(pv, 1)
                    relus(q, range(FB // 4, FB * 3 // 4))
                    if pv:
                        root(pv, 2)
                    relus(q, range(FB * 3 // 4, FB))
                    if pv:
                        n_turned(pv)
                    if nx:
                        root(nx, 0)
                    if pv:
                        exps(pv)
                        if not q.early(2):
                            act.wait_ge(warmed, q.g - 1)
                        act.activation(warm[:], eps[:], ACT.Sqrt).then_inc(warmed, 1)
                    if nx:
                        turned(nx, 0, y1T)

                def end(q):
                    root(q, 1)
                    root(q, 2)
                    n_turned(q)
                    exps(q)

                run(act, [(t_up, 2 * FB)], begin, turn, end)

            @block.tensor
            def _(pe):
                t_up = Tally(up_ps)

                def transposes(q, which):
                    pe.wait_ge(n_r if which else y1_r, q.g + 1)
                    if which:
                        pe.wait_ge(t_out[0], q.g + 2 if q.step(1) else q.g + 1)
                    elif not q.early(2):
                        pe.wait_ge(t_out[1], q.g - 1)
                    src = nb if which else y1[:, q.a]
                    for c in range(DC):
                        for t in range(q.nt):
                            ins = pe.transpose(p_t[c][:, t * P:(t + 1) * P], src[:, t, c * P:(c + 1) * P], K["ident"][:])
                    ins.then_inc(t_ps[which], 1)

                def ffn_up(q):
                    pe.wait_ge(t_out[0], q.g + 1)
                    for b in range(FB):
                        i = t_up.n % 2
                        if t_up.n >= 2 or t_up.k is not None:
                            pe.wait_ge(up_out, t_up.value(1))
                        t_up.n += 1
                        for c in range(DC):
                            ins = pe.matmul(p_up[i][:, 0:q.n], w1[:, c, b * P:(b + 1) * P], y1T[:, c, 0:q.n],
                                            start=c == 0, stop=c == DC - 1)
                        ins.then_inc(up_ps, 1)

                def ffn_down(q, tiles, first, last):
                    if first:
                        pe.wait_ge(up_out, t_up.value())
                        if not q.early(1):
                            pe.wait_ge(dn_used, q.g)
                    for t in tiles:
                        for b in range(FB):
                            ins = pe.matmul(p_dn[:, t * D:(t + 1) * D], h1T[:, b, t * P:(t + 1) * P], w2[:, b],
                                            start=b == 0, stop=b == FB - 1)
                    if last:
                        ins.then_inc(dn_ps, 1)

                def logits(q):
                    pe.wait_ge(t_out[1], q.g + 1)
                    for t in range(q.nt):
                        for c in range(DC):
                            ins = pe.matmul(p_g[:, t * NX:(t + 1) * NX], nT[:, c, t * P:(t + 1) * P], gw[:, c],
                                            start=c == 0, stop=c == DC - 1)
                    ins.then_inc(lg_ps, 1)

                def counts(q):
                    pe.wait_ge(sel_r, q.g + 1)
                    if not q.early(1):
                        pe.wait_ge(rk_used, q.g)
                    n = REST if q.nt == 1 else P
                    for i, over in enumerate(("lower", "ones")):
                        ins = pe.matmul(p_r[:, i * GT * NX:(i * GT + q.nt) * NX], K[over][0:n, :],
                                        both[0:n, 0:q.nt].rearrange("p t e -> p (t e)"), start=True, stop=True)
                    ins.then_inc(rk_ps, 1)

                def begin(q):
                    transposes(q, 0)
                    pe.wait_ge(w_in, W_ALL)

                def turn(q):
                    pv, nx = q.step(-1), q.step(1)
                    ffn_up(q)
                    if pv:
                        transposes(pv, 1)
                    ffn_down(q, range(1), True, q.nt == 1)
                    if pv:
                        logits(pv)
                    if q.nt > 1:
                        ffn_down(q, range(1, q.nt), False, True)
                    if nx:
                        transposes(nx, 0)
                    if pv:
                        counts(pv)

                def end(q):
                    transposes(q, 1)
                    logits(q)
                    counts(q)

                run(pe, [(t_up, 2 * FB)], begin, turn, end)


def stage_experts(nc, K, A_in, n_d, ids_d, tile_d, y_d, R):
    XB = FX // P
    ctx, sb, pb, sem = make_tools(nc)
    with ctx:
        b1, b2 = R["b1"], sb("xb2", [P, NX, D])
        room_i, room = sb("xroom_i", [P, NX], I32), sb("xroom", [P, NX])
        cnt, cnt_i, nt_i, nt_f = sb("xcnt", [P, NX]), sb("xcnt_i", [P, NX], I32), sb("xnt_i", [P, NX], I32), sb("xnt_f", [P, NX])
        zero, t_end = sb("xzero", [P, NX]), sb("xt_end", [P, NX])
        it_i, it = sb("it_i", [P, 1], I32), sb("it", [P, 1])
        past, gone = sb("xpast", [P, NX]), sb("xgone", [P, NX])
        info = sb("xinfo", [P, 4])
        info_i = sb("xinfo_i", [P, 2], I32)
        tab = sb("xtab", [1, 2, P], I32)
        idx = sb("xidx", [P, XG, 2], I32)
        xg, xT = sb("xg", [P, XG, D]), sb("xTx", [P, 2, DC * P])
        hb, g = sb("xhb", [P, 2, FX]), sb("xg_act", [P, 2, FX])
        gT = sb("xgT", [P, 2, XB * P])
        YR = 4
        y = sb("xy", [P, YR, D])
        p_x = [pb(f"p_x{a}") for a in range(2)]
        p_h = [pb(f"p_h{a}") for a in range(2)]
        p_g = [pb(f"p_gT{a}") for a in range(2)]
        p_y = [pb(f"p_y{a}") for a in range(2)]
        b_in, it_r, link_x, info_r, tab_in = sem("xb_in"), sem("it_r"), sem("link_x"), sem("info_r"), sem("tab_in")
        i_in, g_in, stored = [[sem(f"x{n}{r}") for r in range(XG)] for n in ("i_in", "g_in", "stored")]
        xT_ps, xT_r, h_ps, h_r, g_r, gT_ps, gT_r, y_ps, y_r = (sem("x" + n) for n in (
            "xT_ps", "xT_r", "h_ps", "h_r", "g_r", "gT_ps", "gT_r", "y_ps", "y_r"))
        turns = sem("x_turns")
        AHEAD = XG - 3
        assert XT % 2 == 0

        class Tile:

            def __init__(self, k, r):
                self.k, self.r, self.a = k + r // XG, r % XG, r % 2
                self.i = self.k * XG + self.r

            def after(self, d):
                x = Tile(self.k, self.r + d)
                return None if isinstance(x.i, int) and not 0 <= x.i < XT else x

            def early(self, n):
                return isinstance(self.i, int) and self.i < n

        def run(eng, step):
            whole = XT // XG
            for r in range(XG):
                step(Tile(0, r))
            with eng.Fori(1, whole - 1) as k:
                for r in range(XG):
                    step(Tile(k, r))
            for r in range(XG + XT % XG):
                step(Tile(whole - 1, r))

        def value(engine, which, x, top):
            _, w = nc.values_load_multi_w_load_instructions(
                tab[0:1, which, bass.ds(x.i, 1)], engines=(engine,), min_val=0, max_val=top,
                skip_runtime_bounds_check_because="made below its bound")
            return w[0]

        with nc.Block() as block:

            @block.sync
            def _(sp):
                sp.wait_ge(info_r, 1)
                with nc.allow_non_contiguous_dma(reason="a table of a few words"):
                    sp.dma_start(tile_d.rearrange("w p -> p w"), info_i[:]).then_inc(tab_in, 16)
                sp.wait_ge(tab_in, 16)
                sp.dma_start(tab[:], tile_d.unsqueeze(0)).then_inc(tab_in, 16)
                sp.wait_ge(tab_in, 32)

                def ids(x):
                    row = value(mybir.EngineType.SP, 1, x, XR - P)
                    if not x.early(XG):
                        sp.wait_ge(stored[x.r], x.k * 16)
                        sp.sem_inc(turns)
                    sp.dma_start(idx[:, x.r], ids_d[bass.ds(row, P), :]).then_inc(i_in[x.r], 16)
                    if isinstance(x.i, int) and x.i == XG - 1:
                        sp.dma_start(b2[:], A_in["L0_ffn_b2"].unsqueeze(0).to_broadcast([P, NX, D])).then_inc(b_in, 16)

                run(sp, ids)

            @block.gpsimd
            def _(pool):
                pool.iota(it_i[:], [[0, 1]], base=0, channel_multiplier=1).then_inc(it_r, 1)
                pool.iota(room_i[:], [[NP, NX]], base=0, channel_multiplier=0).then_inc(it_r, 1)

                def gather(x):
                    pool.wait_ge(i_in[x.r], x.k * 16 + 16)
                    if not x.early(XG):
                        pool.wait_ge(xT_ps, x.i + 1 - XG)
                    pool.sem_inc(turns)
                    pool.indirect_dma_start(xg[:, x.r], None, n_d,
                                            bass.IndirectOffsetOnAxis(idx[:, x.r, 0:1], 0)).then_inc(g_in[x.r], 16)

                def step(x):
                    if x.after(AHEAD):
                        gather(x.after(AHEAD))
                    pool.wait_ge(y_r, x.i + 1)
                    pool.sem_inc(turns)
                    pool.indirect_dma_start(y_d, bass.IndirectOffsetOnAxis(idx[:, x.r, 1:2], 0), y[:, x.r % YR],
                                            None).then_inc(stored[x.r], 16)

                for r in range(AHEAD):
                    gather(Tile(0, r))
                run(pool, step)
                for r in range(XG):
                    pool.wait_ge(stored[r], 16 * (XT // XG + (r < XT % XG)))

            @block.vector
            def _(dve):
                link = linker(dve, Tally(link_x))
                dve.wait_ge(it_r, 2)
                dve.tensor_copy(it[:], it_i[:])
                dve.memset(zero[:], 0.0)
                link(dve.tensor_copy(room[:], room_i[:]))
                link(dve.tensor_tensor(cnt[:], R["taken"][:], room[:], ALU.subtract))
                link(dve.tensor_scalar(cnt_i[:], cnt[:], float(P - 1), None, ALU.add))
                link(dve.tensor_scalar(nt_i[:], cnt_i[:], 7, None, ALU.logical_shift_right))
                link(dve.tensor_copy(nt_f[:], nt_i[:]))
                link(dve.tensor_tensor_scan(t_end[:], zero[:], nt_f[:], 0.0, ALU.add, ALU.add))
                link(dve.tensor_scalar(past[:], t_end[:], it[:, 0:1], None, ALU.is_le))
                dve.tensor_reduce(info[:, 0:1], past[:], AX.X, ALU.add)
                link(dve.tensor_tensor(gone[:], past[:], nt_f[:], ALU.mult))
                link(dve.tensor_reduce(info[:, 1:2], gone[:], AX.X, ALU.add))
                link(dve.tensor_tensor(info[:, 2:3], it[:], info[:, 1:2], ALU.subtract))
                link(dve.tensor_scalar(info[:, 2:3], info[:, 2:3], float(P), None, ALU.mult))
                link(dve.scalar_tensor_tensor(info[:, 3:4], info[:, 0:1], float(NP), info[:, 2:3], ALU.mult, ALU.add))
                dve.tensor_scalar(info_i[:, 0:1], info[:, 0:1], float(NX - 1), None, ALU.min)
                link(dve.tensor_copy(info_i[:, 1:2], info[:, 3:4]))
                dve.sem_inc(info_r)
                dve.wait_ge(tab_in, 32)

                def hidden(x):
                    e = value(mybir.EngineType.DVE, 0, x, NX - 1)
                    dve.wait_ge(h_ps, x.i + 1)
                    if not x.early(2):
                        dve.wait_ge(g_r, x.i - 1)
                    dve.tensor_tensor(hb[:, x.a], p_h[x.a][:], b1[:, bass.ds(e, 1), :].rearrange("p o f -> p (o f)"),
                                      ALU.add).then_inc(h_r, 1)
                    return e

                def result(x):
                    e = value(mybir.EngineType.DVE, 0, x, NX - 1)
                    dve.wait_ge(y_ps, x.i + 1)
                    if not x.early(YR):
                        b = x.after(-YR)
                        dve.wait_ge(stored[b.r], b.k * 16 + 16)
                    dve.tensor_tensor(y[:, x.r % YR], p_y[x.a][:, 0:D], b2[:, bass.ds(e, 1), :].rearrange("p o f -> p (o f)"),
                                      ALU.add).then_inc(y_r, 1)

                def step(x):
                    if x.after(2):
                        hidden(x.after(2))
                    result(x)

                hidden(Tile(0, 0))
                hidden(Tile(0, 1))
                dve.wait_ge(b_in, 16)
                run(dve, step)

            @block.scalar
            def _(act):
                def turned(x):
                    act.wait_ge(xT_ps, x.i + 1)
                    if not x.early(2):
                        act.wait_ge(h_ps, x.i - 1)
                    act.copy(xT[:, x.a], p_x[x.a][:, 0:DC * P]).then_inc(xT_r, 1)

                def gelu(x):
                    act.wait_ge(h_r, x.i + 1)
                    if not x.early(2):
                        act.wait_ge(gT_ps, x.i - 1)
                    act.activation(g[:, x.a], hb[:, x.a], ACT.Gelu).then_inc(g_r, 1)

                def gelu_turned(x):
                    act.wait_ge(gT_ps, x.i + 1)
                    if not x.early(2):
                        act.wait_ge(y_ps, x.i - 1)
                    act.copy(gT[:, x.a], p_g[x.a][:]).then_inc(gT_r, 1)

                def step(x):
                    if x.after(1):
                        gelu_turned(x.after(1))
                    if x.after(2):
                        gelu(x.after(2))
                    if x.after(3):
                        turned(x.after(3))

                turned(Tile(0, 0))
                turned(Tile(0, 1))
                gelu(Tile(0, 0))
                gelu_turned(Tile(0, 0))
                gelu(Tile(0, 1))
                turned(Tile(0, 2))
                run(act, step)

            @block.tensor
            def _(pe):
                pe.wait_ge(tab_in, 32)

                def turn_rows(x):
                    pe.wait_ge(g_in[x.r], x.k * 16 + 16)
                    if not x.early(2):
                        pe.wait_ge(xT_r, x.i - 1)
                    for c in range(DC):
                        ins = pe.transpose(p_x[x.a][:, c * P:(c + 1) * P], xg[:, x.r, c * P:(c + 1) * P], K["ident"][:])
                    ins.then_inc(xT_ps, 1)

                def up(x):
                    e = value(mybir.EngineType.PE, 0, x, NX - 1)
                    pe.wait_ge(xT_r, x.i + 1)
                    if not x.early(2):
                        pe.wait_ge(h_r, x.i - 1)
                    for c in range(DC):
                        ins = pe.matmul(p_h[x.a][:], xT[:, x.a, c * P:(c + 1) * P],
                                        R["w1"][:, bass.ds(e, 1), c, :].rearrange("p o f -> p (o f)"),
                                        start=c == 0, stop=c == DC - 1)
                    ins.then_inc(h_ps, 1)

                def turn_hidden(x):
                    pe.wait_ge(g_r, x.i + 1)
                    if not x.early(2):
                        pe.wait_ge(gT_r, x.i - 1)
                    for b in range(XB):
                        ins = pe.transpose(p_g[x.a][:, b * P:(b + 1) * P], g[:, x.a, b * P:(b + 1) * P], K["ident"][:])
                    ins.then_inc(gT_ps, 1)

                def down(x):
                    e = value(mybir.EngineType.PE, 0, x, NX - 1)
                    pe.wait_ge(gT_r, x.i + 1)
                    if not x.early(2):
                        pe.wait_ge(y_r, x.i - 1)
                    for b in range(XB):
                        ins = pe.matmul(p_y[x.a][:, 0:D], gT[:, x.a, b * P:(b + 1) * P],
                                        R["w2"][:, bass.ds(e, 1), b, :].rearrange("p o f -> p (o f)"),
                                        start=b == 0, stop=b == XB - 1)
                    ins.then_inc(y_ps, 1)

                def step(x):
                    if x.after(2):
                        up(x.after(2))
                    if x.after(1):
                        turn_hidden(x.after(1))
                    if x.after(3):
                        turn_rows(x.after(3))
                    down(x)

                for r in range(3):
                    turn_rows(Tile(0, r))
                    if r < 2:
                        up(Tile(0, r))
                    if r == 1:
                        turn_hidden(Tile(0, 0))
                run(pe, step)


def stage_combine(nc, acc, y_d, out, R):
    ctx, sb, pb, sem = make_tools(nc)
    with ctx:
        CR = 3
        yg, res = sb("c_y", [P, CR, GT, 2 * D]), sb("c_res", [P, CR, GT, D])
        arrived, stored = [sem(f"c_in{r}") for r in range(CR)], [sem(f"c_st{r}") for r in range(CR)]
        first, res_r, turns = sem("c_first"), sem("c_res_r"), sem("c_turns")
        turns_n = NG // CR
        assert NG % CR == 0

        def run(eng, step):
            for r in range(CR):
                step(0, r, GT)
            with eng.Fori(1, turns_n) as k:
                for r in range(CR):
                    step(k, r, GT)
            step(turns_n, 0, 1)

        def early(k):
            return isinstance(k, int) and k == 0

        def rows(dram, k, r, nt):
            if nt == 1:
                return dram[NG * GT * P:N, :]
            return dram[0:NG * GT * P, :].rearrange("(g t p) d -> g p t d", t=GT, p=P)[k * CR + r]

        def part(buf, r, nt):
            return buf[0:REST, r, 0, :] if nt == 1 else buf[:, r]

        y2 = y_d[0:2 * N, :].rearrange("(n j) d -> n (j d)", j=2)
        with nc.Block() as block:

            @block.sync
            def _(sp):
                def step(k, r, nt):
                    if not early(k):
                        sp.wait_ge(res_r, (k - 1) * CR + r + 1)
                        sp.sem_inc(turns)
                    sp.dma_start(part(yg, r, nt), rows(y2, k, r, nt)).then_inc(arrived[r], 16)

                run(sp, step)

            @block.vector
            def _(dve):
                def step(k, r, nt):
                    g = k * CR + r
                    n = REST if nt == 1 else P
                    dve.wait_ge(arrived[r], k * 16 + 16)
                    if not early(k):
                        dve.wait_ge(stored[r], k * 16)
                    for j, step_r in enumerate((first, res_r)):
                        for i in range(nt):
                            t = g * GT + i
                            so_far = acc[0:n, bass.ds(t, 1), 0:D].rearrange("p o d -> p (o d)") if j == 0 else res[0:n, r, i]
                            share = R["share"][0:n, bass.ds(t, 1), :].rearrange("p o j -> p (o j)")
                            ins = dve.scalar_tensor_tensor(res[0:n, r, i], yg[0:n, r, i, j * D:(j + 1) * D],
                                                           share[:, j:j + 1], so_far, ALU.mult, ALU.add)
                        ins.then_inc(step_r, 1)
                        if j == 0:
                            dve.wait_ge(first, g + 1)

                run(dve, step)

            @block.gpsimd
            def _(pool):
                def step(k, r, nt):
                    pool.wait_ge(res_r, k * CR + r + 1)
                    pool.sem_inc(turns)
                    pool.dma_start(rows(out, k, r, nt), part(res, r, nt)).then_inc(stored[r], 16)

                run(pool, step)
                for r in range(CR):
                    pool.wait_ge(stored[r], 16 * (turns_n + (r == 0)))
def program(nc, A_in, out):
    ctx, sb, pb, sem = make_tools(nc)

    def scratch(name, shape, dt=F32):
        return nc.dram_tensor(name, shape, dt, kind="Internal").ap()

    h0_d, k_d, v_d, n_d = (scratch(n, [N, D]) for n in ("h0_d", "k_d", "v_d", "n_d"))
    ids_d, tile_d, y_d = scratch("ids_d", [XR, 2], I32), scratch("tile_d", [2, P], I32), scratch("y_d", [2 * N + XR, D])
    sorted_d, win_d = scratch("sorted_d", [P * ST, 2], I32), scratch("win_d", [ST], I32)
    with ctx:
        K = constants(nc, sb)
        big = sb("big", [P, max(NT * (D + H), 2 * CL + 1)])
        q_sb = big[:, 0:NT * D].rearrange("p (t d) -> p t d", t=NT)
        acc = big[:, 0:NT * (D + H)].rearrange("p (t d) -> p t d", t=NT)
        stage_constants(nc, K)

        def projections(sb, sem, banks):
            return Projections(nc, K, sb, sem, banks, A_in["x"], A_in["L0_gnn_w_qkv"], A_in["L0_gnn_b_qkv"],
                               h0_d, k_d, v_d, q_sb)

        stage_sort(nc, K, A_in["src"], A_in["dst"], sorted_d, win_d, projections)
        edges, sb2, _, sem2 = make_tools(nc)
        with edges:
            T = {}
            for x in ("", "_x"):
                T["key" + x], T["lo" + x] = sb2("T_key" + x, [P, ST]), sb2("T_lo" + x, [P, ST])
                T["dst" + x], T["win" + x] = sb2("T_dst" + x, [P, ST], I32), sb2("T_win" + x, [1, ST], I32)
            T["keep"] = sb2("T_keep", [P, ST])
            A = sb2("A", [P, ST, H])
            stage_tables(nc, sorted_d, win_d, T, ids_d)
            stage_scores(nc, K, T, q_sb, k_d, A)
            V = {"rows": sb2("vg", [P, GR, GB, D]), "idx": sb2("idx_v", [P, GR, GB], I32),
                 "idx_ready": sem2("idx_v_ready"), "arrived": [sem2(f"v_in{r}") for r in range(GR)]}
            stage_softmax(nc, K, T, A, big, v_d, V)
            stage_sums(nc, K, T, A, v_d, V, acc)
        R = {"w1": sb("xw1", [P, NX, DC, FX]), "w2": sb("xw2", [P, NX, FX // P, D]), "in": sem("xw_in"),
             "b1": sb("xb1", [P, NX, FX]),
             "share": sb("share", [P, NT, 2]), "taken": sb("taken", [P, NX])}
        stage_front(nc, K, A_in, acc, h0_d, n_d, ids_d, R)
        stage_experts(nc, K, A_in, n_d, ids_d, tile_d, y_d, R)
        stage_combine(nc, acc, y_d, out, R)


_INS = ["x", "src", "dst"] + ["L0_gnn_" + n for n in ("w_qkv", "b_qkv", "ln1_g", "ln1_b", "ln2_g", "ln2_b", "w1",
                                                      "b1", "w2", "b2")] \
    + ["L0_ffn_" + n for n in ("gate_w", "gate_b", "W1", "b1", "W2", "b2")]


def kernel(**inputs):
    import numpy as _np
    import concourse.bacc as _bacc
    from concourse import mybir as _mybir
    from concourse.bass_utils import run_bass_kernel_spmd as _run

    nc = _bacc.Bacc("TRN2", target_bir_lowering=False, num_devices=1)
    arrays, args = {}, {}
    for name in _INS:
        a = _np.ascontiguousarray(inputs[name])
        arrays[f"in_{name}_dram"] = a
        args[name] = nc.dram_tensor(f"in_{name}_dram", a.shape, _mybir.dt.from_np(a.dtype), kind="ExternalInput").ap()
    out = nc.dram_tensor("out_dram", (6250, 256), _mybir.dt.float32, kind="ExternalOutput").ap()
    program(nc, args, out)
    r = _run(nc, [arrays], core_ids=[0])
    return r.results[0]["out_dram"]
```
